# Optimizing a Trainium2 kernel written in Bass

```python
import numpy as np
import jax
import jax.numpy as jnp

def _softmax(x, axis=-1):
    return jax.nn.softmax(x, axis=axis)

def _gelu(x):
    return jax.nn.gelu(x, approximate=True)

def _silu(x):
    return jax.nn.silu(x)

def _sigmoid(x):
    return jax.nn.sigmoid(x)

def _layernorm(x, axis=-1, eps=1e-05):
    m = jnp.mean(x, axis=axis, keepdims=True)
    v = jnp.var(x, axis=axis, keepdims=True)
    return (x - m) / jnp.sqrt(v + eps)

def _scatter_add(tgt, idx, src, axis=0):
    return tgt.at[idx].add(src)

def _segment_sum(src, seg, n):
    return jax.ops.segment_sum(src, seg, n)
kernel_name = 'mk_adaln_d1_jaxref_r8_296332'

def setup_inputs(seed: int=0):
    np.random.seed(seed)
    _w = jnp.asarray

    def _L0_attn_setup():
        import jax, jax.numpy as jnp
        import numpy as np
        import math
        DK = 128
        key = jax.random.key(seed)
        k1, k2 = jax.random.split(key)
        x = jax.random.normal(k1, (4, 256, 128), dtype=jnp.float32)
        W = jax.random.normal(k2, (128, 3 * DK), dtype=jnp.float32) * (1.0 / math.sqrt(128))
        b = jnp.zeros((3 * DK,), dtype=jnp.float32)
        return {'x': x, 'W': W, 'b': b}
    _L0_attn_in = _L0_attn_setup()

    def _L0_ffn_setup():
        import jax, jax.numpy as jnp
        import numpy as np
        B, N, D = (4, 1024, 128)
        HEADS, DH = (8, 64)
        HID = HEADS * DH
        WIN = 128
        NQ, NKV = (128, 256)
        EPS, N_ITERS, FETCH_K = (1.0, 50, 9.0 / 8.0)
        SCALE = DH ** (-0.5)

        def rmsnorm(x, gamma):
            norm = jnp.maximum(jnp.linalg.norm(x, axis=-1, keepdims=True), 1e-12)
            return x / norm * x.shape[-1] ** 0.5 * gamma

        def coor_descent(s, k):
            logk = jnp.log(jnp.asarray(k, s.dtype))

            def body(_, ab):
                a, b = ab
                a = EPS * (logk - jax.nn.logsumexp((s + b) / EPS, axis=-1, keepdims=True))
                b = -jax.nn.relu(s + a)
                return (a, b)
            a, b = jax.lax.fori_loop(0, N_ITERS, body, (jnp.zeros_like(s[..., :1]), -s))
            return jnp.exp((s + a + b) / EPS)

        def route(x, routing_token, num_tokens):
            s = jnp.einsum('bnd,d->bn', x, routing_token)
            k = min(num_tokens * FETCH_K, x.shape[1])
            scores = coor_descent(s, k)
            sel_scores, sel_idx = jax.lax.top_k(scores, num_tokens)
            sel_scores = sel_scores + jax.lax.stop_gradient(1.0 - sel_scores)
            return (sel_scores, sel_idx)

        def light_local_attn(x, gamma, wq, wkv, wo):
            b, n, d = x.shape
            xn = rmsnorm(x, gamma)
            q = xn @ wq
            k, v = jnp.split(xn @ wkv, 2, axis=-1)

            def win(t):
                return t.reshape(b, n // WIN, WIN, HEADS, DH).transpose(0, 1, 3, 2, 4)
            q, k, v = (win(q) * SCALE, win(k), win(v))
            attn = jax.nn.softmax(jnp.einsum('bwhid,bwhjd->bwhij', q, k), axis=-1)
            out = jnp.einsum('bwhij,bwhjd->bwhid', attn, v)
            out = out.transpose(0, 1, 3, 2, 4).reshape(b, n, HID)
            return out @ wo

        def heavy_attn(xq, context, scores_kv, gamma, wq, wkv_t, wo):
            b, nq, d = xq.shape
            nkv = context.shape[1]
            xqn = rmsnorm(xq, gamma)
            ctx = rmsnorm(context, gamma)[:, None]
            q = (xqn @ wq).reshape(b, nq, HEADS, DH).transpose(0, 2, 1, 3) * SCALE
            kvw = wkv_t.reshape(1, HEADS, 2 * DH, d)
            kv = jnp.einsum('rhdi,brni->brhnd', kvw, ctx)
            k, v = jnp.split(kv, 2, axis=-1)
            v = v * scores_kv[:, None, None, :, None]
            k = k.reshape(b, HEADS, nkv, DH)
            v = v.reshape(b, HEADS, nkv, DH)
            attn = jax.nn.softmax(jnp.einsum('bhid,bhjd->bhij', q, k), axis=-1)
            out = jnp.einsum('bhij,bhjd->bhid', attn, v)
            out = out.transpose(0, 2, 1, 3).reshape(b, nq, HID)
            return out @ wo
        key = jax.random.key(seed)
        ks = jax.random.split(key, 10)
        lin = lambda k, shape, fan: jax.random.normal(k, shape, jnp.float32) * fan ** (-0.5)
        return dict(x=jax.random.normal(ks[0], (B, N, D), jnp.float32), gamma_light=jnp.ones((D,), jnp.float32), wq_light=lin(ks[1], (D, HID), D), wkv_light=lin(ks[2], (D, 2 * HID), D), wo_light=lin(ks[3], (HID, D), HID), q_routing_token=jax.random.normal(ks[4], (D,), jnp.float32), kv_routing_token=jax.random.normal(ks[5], (D,), jnp.float32), gamma_heavy=jnp.ones((D,), jnp.float32), wq_heavy=lin(ks[6], (D, HID), D), wkv_heavy=lin(ks[7], (2 * HID, D), D), wo_heavy=lin(ks[8], (HID, D), HID))
    _L0_ffn_in = _L0_ffn_setup()
    _L0_c = _w((lambda *s: np.random.randn(*s).astype(np.float32) * 0.05)(16, 128))
    _L0_wmod = _w((lambda *s: np.random.randn(*s).astype(np.float32) * 0.05)(128, 6 * 128) * 128 ** (-0.5))
    _d = {'L0_attn_x': _L0_attn_in['x'], 'L0_attn_W': _L0_attn_in['W'], 'L0_attn_b': _L0_attn_in['b'], 'L0_ffn_gamma_light': _L0_ffn_in['gamma_light'], 'L0_ffn_wq_light': _L0_ffn_in['wq_light'], 'L0_ffn_wkv_light': _L0_ffn_in['wkv_light'], 'L0_ffn_wo_light': _L0_ffn_in['wo_light'], 'L0_ffn_q_routing_token': _L0_ffn_in['q_routing_token'], 'L0_ffn_kv_routing_token': _L0_ffn_in['kv_routing_token'], 'L0_ffn_gamma_heavy': _L0_ffn_in['gamma_heavy'], 'L0_ffn_wq_heavy': _L0_ffn_in['wq_heavy'], 'L0_ffn_wkv_heavy': _L0_ffn_in['wkv_heavy'], 'L0_ffn_wo_heavy': _L0_ffn_in['wo_heavy'], 'L0_c': _L0_c, 'L0_wmod': _L0_wmod}
    _x0 = _d['L0_attn_x']
    _d['L0_attn_x'] = jax.random.normal(jax.random.fold_in(jax.random.key(seed), 1), (16, 256, 128), dtype=_x0.dtype)
    del _x0
    return _d

def reference(L0_attn_x, L0_attn_W, L0_attn_b, L0_ffn_gamma_light, L0_ffn_wq_light, L0_ffn_wkv_light, L0_ffn_wo_light, L0_ffn_q_routing_token, L0_ffn_kv_routing_token, L0_ffn_gamma_heavy, L0_ffn_wq_heavy, L0_ffn_wkv_heavy, L0_ffn_wo_heavy, L0_c, L0_wmod):

    def _L0_attn_ref(x, W, b):
        import jax, jax.numpy as jnp
        import numpy as np
        import math
        DK = 128
        qkv = jnp.einsum('btc,cd->btd', x, W) + b
        q, k, v = jnp.split(qkv, 3, axis=-1)
        scale = 1.0 / math.sqrt(DK)
        weights = jnp.einsum('btc,bTc->btT', q, k) * scale
        T = weights.shape[-1]
        mask = jnp.tril(jnp.ones((T, T), dtype=jnp.float32))
        logits = jnp.where(mask == 0, jnp.float32(-9000000000000000.0), weights)
        attention = jax.nn.softmax(logits, axis=-1)
        values = jnp.einsum('btT,bTc->btc', attention, v)
        return values

    def _L0_ffn_ref(x, gamma_light, wq_light, wkv_light, wo_light, q_routing_token, kv_routing_token, gamma_heavy, wq_heavy, wkv_heavy, wo_heavy):
        import jax, jax.numpy as jnp
        import numpy as np
        B, N, D = (4, 1024, 128)
        HEADS, DH = (8, 64)
        HID = HEADS * DH
        WIN = 128
        NQ, NKV = (128, 256)
        EPS, N_ITERS, FETCH_K = (1.0, 50, 9.0 / 8.0)
        SCALE = DH ** (-0.5)

        def rmsnorm(x, gamma):
            norm = jnp.maximum(jnp.linalg.norm(x, axis=-1, keepdims=True), 1e-12)
            return x / norm * x.shape[-1] ** 0.5 * gamma

        def coor_descent(s, k):
            logk = jnp.log(jnp.asarray(k, s.dtype))

            def body(_, ab):
                a, b = ab
                a = EPS * (logk - jax.nn.logsumexp((s + b) / EPS, axis=-1, keepdims=True))
                b = -jax.nn.relu(s + a)
                return (a, b)
            a, b = jax.lax.fori_loop(0, N_ITERS, body, (jnp.zeros_like(s[..., :1]), -s))
            return jnp.exp((s + a + b) / EPS)

        def route(x, routing_token, num_tokens):
            s = jnp.einsum('bnd,d->bn', x, routing_token)
            k = min(num_tokens * FETCH_K, x.shape[1])
            scores = coor_descent(s, k)
            sel_scores, sel_idx = jax.lax.top_k(scores, num_tokens)
            sel_scores = sel_scores + jax.lax.stop_gradient(1.0 - sel_scores)
            return (sel_scores, sel_idx)

        def light_local_attn(x, gamma, wq, wkv, wo):
            b, n, d = x.shape
            xn = rmsnorm(x, gamma)
            q = xn @ wq
            k, v = jnp.split(xn @ wkv, 2, axis=-1)

            def win(t):
                return t.reshape(b, n // WIN, WIN, HEADS, DH).transpose(0, 1, 3, 2, 4)
            q, k, v = (win(q) * SCALE, win(k), win(v))
            attn = jax.nn.softmax(jnp.einsum('bwhid,bwhjd->bwhij', q, k), axis=-1)
            out = jnp.einsum('bwhij,bwhjd->bwhid', attn, v)
            out = out.transpose(0, 1, 3, 2, 4).reshape(b, n, HID)
            return out @ wo

        def heavy_attn(xq, context, scores_kv, gamma, wq, wkv_t, wo):
            b, nq, d = xq.shape
            nkv = context.shape[1]
            xqn = rmsnorm(xq, gamma)
            ctx = rmsnorm(context, gamma)[:, None]
            q = (xqn @ wq).reshape(b, nq, HEADS, DH).transpose(0, 2, 1, 3) * SCALE
            kvw = wkv_t.reshape(1, HEADS, 2 * DH, d)
            kv = jnp.einsum('rhdi,brni->brhnd', kvw, ctx)
            k, v = jnp.split(kv, 2, axis=-1)
            v = v * scores_kv[:, None, None, :, None]
            k = k.reshape(b, HEADS, nkv, DH)
            v = v.reshape(b, HEADS, nkv, DH)
            attn = jax.nn.softmax(jnp.einsum('bhid,bhjd->bhij', q, k), axis=-1)
            out = jnp.einsum('bhij,bhjd->bhid', attn, v)
            out = out.transpose(0, 2, 1, 3).reshape(b, nq, HID)
            return out @ wo
        b = x.shape[0]
        light_out = light_local_attn(x, gamma_light, wq_light, wkv_light, wo_light)
        scores_q, idx_q = route(x, q_routing_token, NQ)
        scores_kv, idx_kv = route(x, kv_routing_token, NKV)
        routed_q = jnp.take_along_axis(x, idx_q[..., None], axis=1)
        routed_kv = jnp.take_along_axis(x, idx_kv[..., None], axis=1)
        routed_out = heavy_attn(routed_q, routed_kv, scores_kv, gamma_heavy, wq_heavy, wkv_heavy, wo_heavy)
        routed_out = routed_out * scores_q[..., None]
        heavy_out = jnp.zeros_like(x).at[jnp.arange(b)[:, None], idx_q].set(routed_out)
        return light_out + heavy_out
    x = L0_attn_x
    mod = (_silu(L0_c) @ L0_wmod).reshape(L0_c.shape[0], 6, 1, -1)
    sa, ca, ga, sb, cb, gb = (mod[:, 0], mod[:, 1], mod[:, 2], mod[:, 3], mod[:, 4], mod[:, 5])
    ga = (2 * (ga >= 0) - 1) * jnp.maximum(jnp.abs(ga), 0.25)
    gb = (2 * (gb >= 0) - 1) * jnp.maximum(jnp.abs(gb), 0.25)
    h = _layernorm(x, axis=-1) * (1 + ca) + sa
    x = x + ga * _L0_attn_ref(h, L0_attn_W, L0_attn_b)
    h = _layernorm(x, axis=-1) * (1 + cb) + sb
    x = x + gb * _L0_ffn_ref(h, L0_ffn_gamma_light, L0_ffn_wq_light, L0_ffn_wkv_light, L0_ffn_wo_light, L0_ffn_q_routing_token, L0_ffn_kv_routing_token, L0_ffn_gamma_heavy, L0_ffn_wq_heavy, L0_ffn_wkv_heavy, L0_ffn_wo_heavy)
    return x

_drawn_inputs = setup_inputs


def setup_inputs(seed=0):
    import zlib

    import numpy as np

    out = dict(_drawn_inputs(seed))
    spreads = {'L0_attn_b': (0.0, 0.307),
     'L0_ffn_gamma_light': (1.0, 0.6),
     'L0_ffn_gamma_heavy': (1.0, 0.6)}
    factors = {'L0_ffn_q_routing_token': 2.956, 'L0_ffn_kv_routing_token': 8.0}
    for name, (base, spread) in spreads.items():
        noise = np.random.default_rng([zlib.crc32(name.encode()), seed]).standard_normal(out[name].shape)
        drawn = base * np.exp(spread * noise) if base else spread * noise
        out[name] = jnp.asarray(drawn.astype(out[name].dtype))
    for name, factor in factors.items():
        out[name] = (out[name] * factor).astype(out[name].dtype)
    return out
```

```python
from contextlib import ExitStack

import numpy as np

import concourse.bass as bass
from concourse import mybir
from concourse.alu_op_type import AluOpType as ALU

ACT = mybir.ActivationFunctionType
AX = mybir.AxisListType
F32 = mybir.dt.float32
F32R = mybir.dt.float32r

P = 128
B, N, D = 16, 256, 128
C = N // P
HEADS, DH = 8, 64
HID = HEADS * DH
NQ = 128
K_Q, K_KV = NQ * 9 / 8, float(N)
CD_ITERS = 50
LN_EPS = 1e-5
MASKED = -9.0e15
ATTN_SCALE = float(D) ** -0.5
HEAD_SCALE = float(DH) ** -0.5
PAIRS = B // 2


def at_least(eng, sem, value):
    if isinstance(value, int) and value <= 0:
        return
    eng.wait_ge(sem, value)


def run_stages(eng, stages, units, first, last, extra=None):
    def step(p, k):
        for lag, f in stages:
            q, kk = p + (k - lag) // units, (k - lag) % units
            if isinstance(p, int) and not 0 <= q < PAIRS:
                continue
            f(q, kk)
        if extra is not None:
            extra(p, k)

    deepest = max(lag for lag, _ in stages)
    tail = -(-deepest // units)
    for p in range(first):
        for k in range(units):
            step(p, k)
    with eng.Fori(first, last) as p:
        for k in range(units):
            step(p, k)
    for p in range(last, PAIRS + tail):
        for k in range(units):
            step(p, k)


def adaln_routed_attention(nc, x, w_attn, b_attn, gamma_l, wq_l, wkv_l, wo_l, q_tok, kv_tok,
                           gamma_h, wq_h, wkv_h, wo_h, c, wmod, out):
    with ExitStack() as ctx:
        def sb(name, shape, dt=F32):
            return ctx.enter_context(nc.sbuf_tensor(name, shape, dt))

        def sem(name):
            return ctx.enter_context(nc.semaphore(name))

        ps = [ctx.enter_context(nc.psum_tensor(f"bank{i}", [P, 512], F32)) for i in range(8)]
        xh_dram = nc.dram_tensor("xh_scratch", [B, P, C * D], F32).ap()
        mod_rows_dram = nc.dram_tensor("mod_rows_scratch", [B, 4, D], F32).ap()

        X = sb("X", [P, B, C, D])
        XT_hi = sb("XT_hi", [P, B, N], F32R)
        XT_lo = sb("XT_lo", [P, B, N], F32R)
        ident = sb("ident", [P, P])
        tri = sb("tri", [P, P])
        ones = sb("ones", [P, P])
        iota = sb("iota", [P, P])
        mask = sb("mask", [P, 3 * P])
        neg_half = sb("neg_half", [P, B * C])
        mod_bc = sb("mod_bc", [P, B, 4, D])
        tok_bc = sb("tok_bc", [P, 2, D])
        bv_bc = sb("bv_bc", [P, D])
        gam_bc = sb("gam_bc", [P, 2, D])
        gam_col = sb("gam_col", [P, 2])
        gam_sc = sb("gam_sc", [P, 2])
        b_col = sb("b_col", [P, 2])
        bq_sc = sb("bq_sc", [P, 1])
        modT = sb("modT", [P, 2, B])
        w_at = sb("w_at", [P, 3 * D])
        wmod_sb = sb("wmod_sb", [P, 6 * D])
        wo_l_sb = sb("wo_l_sb", [P, 4, D])
        wo_h_sb = sb("wo_h_sb", [P, 4, D])
        U_w = [sb(f"U_w_{s}", [P, HEADS, D], F32R) for s in ("hi", "lo")]
        V_w = [sb(f"V_w_{s}", [P, HID], F32R) for s in ("hi", "lo")]
        T_w = sb("T_w", [P, HEADS, D])
        VH_w = [sb(f"VH_w_{s}", [P, HID], F32R) for s in ("hi", "lo")]

        S_all = sb("S_all", [P, B, C, 2])
        two = range(2)
        xhs = [sb(f"xhs{i}", [P, C, D]) for i in two]

        R = 2 * B
        S_dense = sb("S_dense", [P, C, R])
        s_rows = sb("s_rows", [R, N])
        smax = sb("smax", [R, 1])
        log_k = sb("log_k", [R, 1])
        cd_t = sb("cd_t", [R, N])
        cd_e = sb("cd_e", [R, N])
        cd_m = sb("cd_m", [R, 1])
        cd_sum = sb("cd_sum", [R, 1])
        cd_ln = sb("cd_ln", [R, 1])
        cd_na = sb("cd_na", [R, 1])
        score = sb("score", [R, N])
        left = [sb(f"left{i}", [R, N]) for i in two]
        top8 = [sb(f"top8{i}", [R, 8]) for i in two]
        w1m = sb("w1m", [R, N])
        wsel = sb("wsel", [R, 2, N])
        selT = sb("selT", [P, 2, C, R])
        pos_p = sb("pos_p", [P, C, B])
        pos = sb("pos", [P, C, B])

        st1 = sb("st1", [P, B, C, 6])
        t1 = sb("t1", [P, 5, B * C])
        mean1 = sb("mean1", [P, B * C])
        ve1 = sb("ve1", [P, B * C])
        rs1 = sb("rs1", [P, B * C])
        early = ExitStack()
        late = sb
        sb = lambda name, shape, dt=F32: early.enter_context(nc.sbuf_tensor(name, shape, dt))
        wq_raw = sb("wq_raw", [P, 2, HID])
        wkv_raw = sb("wkv_raw", [P, 2 * HID])
        wk_hT = sb("wk_hT", [P, 4, D])
        wv_hT = sb("wv_hT", [P, 4, D])
        wqT = sb("wqT", [P, 2, 4, D])
        wkT = sb("wkT", [P, 4, D])
        big = sb("big", [P, HEADS, D])
        c_sb = sb("c_sb", [B, D])
        c_e = sb("c_e", [B, D])
        c_d = sb("c_d", [B, D])
        c_r = sb("c_r", [B, D])
        c_s = sb("c_s", [B, D])
        cT = sb("cT", [P, B])
        mod_raw = sb("mod_raw", [B, 6, D])
        mod_fix = sb("mod_fix", [B, 4, D])
        gate_s = sb("gate_s", [B, 2, D])
        gate_a = sb("gate_a", [B, 2, D])
        gate_m = sb("gate_m", [B, 2, D])

        early.close()
        xl = [sb(f"xl{i}", [P, C, D]) for i in two]
        hT = [sb(f"hT{i}", [P, N]) for i in two]
        qT = [sb(f"qT{i}", [P, N]) for i in two]
        kT = [sb(f"kT{i}", [P, N]) for i in two]
        va = [sb(f"va{i}", [P, C, D]) for i in two]
        sm = [sb(f"sm{i}", [P, 3 * P]) for i in two]
        nmxa = [sb(f"nmxa{i}", [P, C]) for i in two]
        pa = [sb(f"pa{i}", [P, 3 * P]) for i in two]
        suma = [sb(f"suma{i}", [P, C]) for i in two]
        rinva = [sb(f"rinva{i}", [P, C]) for i in two]
        pta = [sb(f"pta{i}", [P, 3 * P]) for i in two]
        ao = [sb(f"ao{i}", [P, C, D]) for i in two]
        st2 = [sb(f"st2{i}", [P, C, 6]) for i in two]
        t2 = [sb(f"t2{i}", [P, 5, C]) for i in two]
        mean2 = [sb(f"mean2{i}", [P, C]) for i in two]
        ve2 = [sb(f"ve2{i}", [P, C]) for i in two]
        rs2 = [sb(f"rs2{i}", [P, C]) for i in two]
        hn = [sb(f"hn{i}", [P, C, D]) for i in two]
        hm = [sb(f"hm{i}", [P, C, D]) for i in two]
        h2 = [sb(f"h2{i}", [P, C, D]) for i in two]
        sq = sb("sq", [P, 2, C, D])
        ss = [sb(f"ss{i}", [P, C]) for i in two]
        ssc = [sb(f"ssc{i}", [P, C]) for i in two]
        rn = [sb(f"rn{i}", [P, C]) for i in two]
        rprod = sb("rprod", [P, 2, 4, D])
        s4 = [sb(f"s4{i}", [P, 4]) for i in two]
        early.close()
        sb = late
        xt = [[sb(f"xt{i}{s}", [P, N], F32R) for s in ("hi", "lo")] for i in two]
        xh = [sb(f"xh{i}", [P, C, D]) for i in two]
        U = [[sb(f"U{i}{s}", [P, HEADS, N], F32R) for s in ("hi", "lo")] for i in two]
        V = [sb(f"V{i}", [P, C, HID]) for i in two]
        nmx = [sb(f"nmx{i}", [P, 4]) for i in range(4)]
        sums = [sb(f"sums{i}", [P, 4]) for i in range(4)]
        rinv = [sb(f"rinv{i}", [P, 4]) for i in range(4)]
        pr = [sb(f"pr{i}", [P, 512]) for i in range(4)]
        pt = [sb(f"pt{i}", [P, 512]) for i in two]
        oT = [sb(f"oT{i}", [P, 4, P]) for i in two]
        tmp = [sb(f"tmp{i}", [P, C, D]) for i in two]
        G = [sb(f"G{i}", [P, C, NQ]) for i in two]
        GT = [sb(f"GT{i}", [P, C, P]) for i in two]
        xq = [sb(f"xq{i}", [P, NQ]) for i in two]
        rt = [sb(f"rt{i}", [P, D]) for i in two]
        ob = [sb(f"ob{i}", [P, C, D]) for i in two]

        x_in = [sem(f"x_in{i}") for i in range(4)]
        w_in, bc_in, mod_out, mod_in = sem("w_in"), sem("bc_in"), sem("mod_out"), sem("mod_in")
        g_const, g_tab = sem("g_const"), sem("g_tab")
        st1_done, mv1_sums, mv1_parts, ve1_done, rs1_done = (sem("st1_done"), sem("mv1_sums"), sem("mv1_parts"),
                                                             sem("ve1_done"), sem("rs1_done"))
        w_tr, w_trs, w_pr, w_prs, w_split = sem("w_tr"), sem("w_trs"), sem("w_pr"), sem("w_prs"), sem("w_split")
        w_small, v_hi, v_lo, c_den, mod_raws = (sem("w_small"), sem("v_hi"), sem("v_lo"), sem("c_den"),
                                                         sem("mod_raws"))
        c_exp, c_act, cT_ps, cT_sb, mod_ps, mod_sb = (sem("c_exp"), sem("c_act"), sem("cT_ps"), sem("cT_sb"),
                                                      sem("mod_ps"), sem("mod_sb"))
        a = {n: sem("a_" + n) for n in (
            "xl", "hp", "hT", "qkp", "vp", "qkT", "v", "Sp", "sm", "nmx", "p", "PTp", "PT", "Op", "ri",
            "ao", "x1", "st", "mv", "mp", "ve", "rs", "hn", "hm", "h2", "ss", "ssc", "rn", "s4", "S", "xh",
            "xhd0", "xhd1", "xp", "xhi", "xlo")}
        r = {n: sem("r_" + n) for n in (
            "Sd", "Sp", "rows", "smax", "m", "t", "e", "ln", "na", "tf", "sc", "top", "left", "w1", "w", "selp",
            "selT", "cum", "pp", "pos")}
        lt = {n: sem("l_" + n) for n in (
            "xt0", "xt1", "pj", "hi", "pe", "Sp", "mx", "p", "ri", "pn", "PTp", "PT", "Op", "oT", "outp", "fin", "x")}
        hv = {n: sem("h_" + n) for n in (
            "xt0", "xt1", "G", "xqp", "xq", "gtp", "gt", "tp", "thi", "tlo", "vp", "v", "Sp", "mx", "p", "ri", "pn",
            "PTp", "PT", "Op", "oT", "outp", "rt", "scp", "fin", "ob", "out0", "out1")}

        block = ctx.enter_context(nc.Block())

        U_PIECE, V_PIECE = (0, 1, 2, 4), (3, 5)

        def b_par(k):
            return k // 4

        W_LOADS = 14
        BC_LOADS = 7

        @block.sync
        def _(sp):
            for i in range(4):
                sp.dma_start(X[:, 4 * i:4 * i + 4, :, :],
                             x[4 * i:4 * i + 4].rearrange("b (c p) d -> p b c d", p=P)).then_inc(x_in[i], 16)
            sp.dma_start(tok_bc[:, 0, :], q_tok.rearrange("(a d) -> a d", a=1).broadcast_to([P, D])).then_inc(bc_in, 16)
            sp.dma_start(tok_bc[:, 1, :], kv_tok.rearrange("(a d) -> a d", a=1).broadcast_to([P, D])).then_inc(bc_in, 16)
            sp.dma_start(bv_bc[:, :], b_attn[2 * D:3 * D].rearrange("(a d) -> a d", a=1).broadcast_to([P, D])).then_inc(bc_in, 16)
            sp.dma_start(gam_bc[:, 0, :], gamma_l.rearrange("(a d) -> a d", a=1).broadcast_to([P, D])).then_inc(bc_in, 16)
            sp.dma_start(gam_bc[:, 1, :], gamma_h.rearrange("(a d) -> a d", a=1).broadcast_to([P, D])).then_inc(bc_in, 16)
            for j in range(2):
                sp.dma_start(b_col[:, j:j + 1], b_attn[j * D:(j + 1) * D].rearrange("(p a) -> p a", a=1)).then_inc(bc_in, 16)
            sp.wait_ge(mod_sb, 5)
            sp.dma_start(mod_rows_dram, mod_fix[:, :, :]).then_inc(mod_out, 16)
            sp.wait_ge(mod_out, 16)
            sp.dma_start(mod_bc[:, :, :, :].rearrange("p b j d -> p (b j d)"),
                         mod_rows_dram.rearrange("b j d -> (b j d)").rearrange("(a n) -> a n", a=1)
                         .broadcast_to([P, B * 4 * D])).then_inc(mod_in, 16)

            with sp.Fori(0, PAIRS) as p:
                for k in range(2):
                    sp.wait_ge(a["xh"], 4 * p + 2 * k + 2)
                    sp.dma_start(xh_dram[2 * p + k], xhs[k][:, :, :].rearrange("p c d -> p (c d)")).then_inc(a[f"xhd{k}"], 16)
            sp.wait_ge(a["xlo"], B)

            def load_light(p, k):
                b = 2 * p + k
                at_least(sp, lt["Sp"], 4 * (b - 1))
                sp.dma_start(xt[k][0][:, :].bitcast(F32), XT_hi[:, b, :].bitcast(F32)).then_inc(lt[f"xt{k}"], 16)
                sp.dma_start(xt[k][1][:, :].bitcast(F32), XT_lo[:, b, :].bitcast(F32)).then_inc(lt[f"xt{k}"], 16)

            for k in range(2):
                load_light(0, k)
            with sp.Fori(1, PAIRS) as p:
                for k in range(2):
                    load_light(p, k)

            sp.wait_ge(lt["Sp"], 4 * B)
            for k in range(2):
                sp.wait_ge(a[f"xhd{k}"], 16 * PAIRS)

            def load_heavy(p, k):
                b = 2 * p + k
                at_least(sp, hv["vp"], 2 * (b - 1))
                at_least(sp, hv["xqp"], b - 1)
                sp.dma_start(xt[k][0][:, :].bitcast(F32), XT_hi[:, b, :].bitcast(F32)).then_inc(hv[f"xt{k}"], 16)
                sp.dma_start(xt[k][1][:, :].bitcast(F32), XT_lo[:, b, :].bitcast(F32)).then_inc(hv[f"xt{k}"], 16)
                sp.dma_start(xh[k][:, :, :].rearrange("p c d -> p (c d)"), xh_dram[b]).then_inc(hv[f"xt{k}"], 16)

            def store(p, k):
                b = 2 * p + k
                sp.wait_ge(hv["ob"], b + 1)
                sp.dma_start(out[b].rearrange("(c p) d -> p c d", p=P), ob[k][:, :, :]).then_inc(hv[f"out{k}"], 16)

            for p in range(2):
                for k in range(2):
                    load_heavy(p, k)
            with sp.Fori(2, PAIRS) as p:
                for k in range(2):
                    store(p - 2, k)
                    load_heavy(p, k)
            for p in range(PAIRS - 2, PAIRS):
                for k in range(2):
                    store(p, k)
            for k in range(2):
                sp.wait_ge(hv[f"out{k}"], 16 * PAIRS)

        @block.gpsimd
        def _(pool):
            pool.memset(ident[:, :], 0.0).then_inc(g_const, 1)
            pool.memset(tri[:, :], 1.0).then_inc(g_const, 1)
            pool.memset(ones[:, :], 1.0).then_inc(g_const, 1)
            pool.memset(mask[:, :], 0.0).then_inc(g_const, 1)
            pool.memset(neg_half[:, :], -0.5).then_inc(g_const, 1)
            pool.iota(iota[:, :], [[1, P]], base=0, channel_multiplier=0,
                      allow_small_or_imprecise_dtypes=True).then_inc(g_const, 1)
            pool.memset(log_k[:, :], float(np.log(np.float32(K_KV)))).then_inc(g_const, 1)
            pool.wait_ge(g_const, 7)
            pool.affine_select(ident[:, :], ident[:, :], pattern=[[-1, P]], compare_op=ALU.not_equal, fill=1.0,
                               base=0, channel_multiplier=1).then_inc(g_tab, 1)
            pool.affine_select(tri[:, :], tri[:, :], pattern=[[1, P]], compare_op=ALU.is_ge, fill=0.0,
                               base=0, channel_multiplier=-1).then_inc(g_tab, 1)
            pool.affine_select(mask[:, 0:P], mask[:, 0:P], pattern=[[-1, P]], compare_op=ALU.is_ge, fill=MASKED,
                               base=0, channel_multiplier=1).then_inc(g_tab, 1)
            pool.affine_select(mask[:, 2 * P:3 * P], mask[:, 2 * P:3 * P], pattern=[[-1, P]], compare_op=ALU.is_ge,
                               fill=MASKED, base=0, channel_multiplier=1).then_inc(g_tab, 1)
            pool.memset(log_k[0:B, :], float(np.log(np.float32(K_Q)))).then_inc(g_tab, 1)

            pool.wait_ge(ve1_done, 1)
            pool.tensor_tensor(rs1[:, :], ve1[:, :], neg_half[:, :], ALU.pow).then_inc(rs1_done, 1)
            pool.wait_ge(mod_in, 16)

            def residual(p, k):
                b = 2 * p + k
                pool.wait_ge(a["ao"], 2 * b + 2)
                pool.tensor_tensor(X[:, b], X[:, b], ao[k][:, :, :], ALU.add).then_inc(a["x1"], 1)

            def ln2_rstd(p, k):
                pool.wait_ge(a["ve"], 2 * p + k + 1)
                pool.tensor_tensor(rs2[k][:, :], ve2[k][:, :], neg_half[:, 0:C], ALU.pow).then_inc(a["rs"], 1)

            def modulate(p, k):
                b = 2 * p + k
                pool.wait_ge(a["hn"], 2 * b + 2)
                pool.tensor_tensor(hm[k][:, :, :], hn[k][:, :, :],
                                   mod_bc[:, b, 1:2, :].broadcast_to([P, C, D]), ALU.mult).then_inc(a["hm"], 1)
                pool.wait_ge(a["hm"], b + 1)
                at_least(pool, a["ss"], 2 * (b - 1))
                at_least(pool, a["xh"], 2 * (b - 1))
                pool.tensor_tensor(h2[k][:, :, :], hm[k][:, :, :],
                                   mod_bc[:, b, 2:3, :].broadcast_to([P, C, D]), ALU.add).then_inc(a["h2"], 1)

            def rms(p, k):
                pool.wait_ge(a["ssc"], 2 * p + k + 1)
                pool.tensor_tensor(rn[k][:, :], ssc[k][:, :], neg_half[:, 0:C], ALU.pow).then_inc(a["rn"], 1)

            run_stages(pool, [(3, residual), (4, ln2_rstd), (6, rms), (5, modulate)], 2, 5, PAIRS)

            pool.wait_ge(a["xlo"], B)
            def normalise(p, k):
                g = 8 * p + k
                pool.wait_ge(lt["ri"], g + 1)
                q = pr[k % 4][:, :].rearrange("p (h t) -> p h t", h=4)
                pool.tensor_tensor(q, q, rinv[k % 4][:, :, None].broadcast_to([P, 4, P]), ALU.mult)\
                    .then_inc(lt["pn"], 1)

            def add_light(p, k):
                if k % 2 == 0:
                    return
                b, w = 2 * p + k // 4, k % 4 // 2
                pool.wait_ge(lt["fin"], 2 * b + w + 1)
                pool.tensor_tensor(X[:, b, w, :], X[:, b, w, :], tmp[w][:, 0, :], ALU.add).then_inc(lt["x"], 1)

            run_stages(pool, [(6, normalise), (10, add_light)], 8, 3, PAIRS)

            def normalise_h(p, k):
                g = 8 * p + k
                pool.wait_ge(hv["ri"], g + 1)
                q = pr[k % 4][:, :].rearrange("p (h t) -> p h t", h=2)
                pool.tensor_tensor(q, q, rinv[k % 4][:, 0:2, None].broadcast_to([P, 2, N]), ALU.mult)\
                    .then_inc(hv["pn"], 1)

            def add_heavy(p, k):
                if k % 4 != 3:
                    return
                b = 2 * p + k // 4
                pool.wait_ge(hv["fin"], 2 * b + 2)
                at_least(pool, hv[f"out{b_par(k)}"], 16 * p)
                pool.tensor_tensor(ob[b_par(k)][:, :, :], X[:, b], tmp[b_par(k)][:, :, :], ALU.add)\
                    .then_inc(hv["ob"], 1)

            run_stages(pool, [(6, normalise_h), (11, add_heavy)], 8, 3, PAIRS)

        @block.scalar
        def _(act):
            act.preload_act_table_set("natural_log_exp_and_others")
            act.dma_start(c_sb[:, :], c).then_inc(w_in, 16)
            act.dma_start(wmod_sb[:, :], wmod).then_inc(w_in, 16)
            act.dma_start(wq_raw[:, 0, :], wq_l).then_inc(w_in, 16)
            act.dma_start(wkv_raw[:, :], wkv_l).then_inc(w_in, 16)
            act.dma_start(wq_raw[:, 1, :], wq_h).then_inc(w_in, 16)
            kv_rows = wkv_h.rearrange("(q i t m) d -> i t m q d", i=2, t=2, m=DH)
            for i in range(2):
                act.dma_start(wk_hT[i * DH:(i + 1) * DH, :, :], kv_rows[i, 0]).then_inc(w_in, 16)
                act.dma_start(wv_hT[i * DH:(i + 1) * DH, :, :], kv_rows[i, 1]).then_inc(w_in, 16)
            act.dma_start(wo_l_sb[:, :, :], wo_l.rearrange("(q p) d -> p q d", p=P)).then_inc(w_in, 16)
            act.dma_start(wo_h_sb[:, :, :], wo_h.rearrange("(q p) d -> p q d", p=P)).then_inc(w_in, 16)
            act.dma_start(w_at[:, :], w_attn).then_inc(w_in, 16)
            act.dma_start(gam_col[:, 0:1], gamma_l.rearrange("(p a) -> p a", a=1)).then_inc(w_in, 16)
            act.dma_start(gam_col[:, 1:2], gamma_h.rearrange("(p a) -> p a", a=1)).then_inc(w_in, 16)

            act.wait_ge(w_in, 16 * W_LOADS)
            act.activation(c_e[:, :], c_sb[:, :], ACT.Exp, scale=-1.0).then_inc(c_exp, 1)

            act.wait_ge(w_small, 2)

            def qk_evac(p, k):
                b = 2 * p + k
                act.wait_ge(a["qkp"], b + 1)
                act.activation(qT[k][:, :], ps[2][:, 0:N], ACT.Identity, bias=bq_sc[:, :], scale=ATTN_SCALE)\
                    .then_inc(a["qkT"], 1)
                act.activation(kT[k][:, :], ps[2][:, N:2 * N], ACT.Identity, bias=b_col[:, 1:2]).then_inc(a["qkT"], 1)

            def exps_a(p, k):
                b = 2 * p + k
                act.wait_ge(a["nmx"], 2 * b + 2)
                at_least(act, a["PTp"], b - 1)
                at_least(act, a["ri"], b - 1)
                act.activation(pa[k][:, 0:P], sm[k][:, 0:P], ACT.Exp, bias=nmxa[k][:, 0:1],
                               accum_out=suma[k][:, 0:1]).then_inc(a["p"], 1)
                act.activation(pa[k][:, P:3 * P], sm[k][:, P:3 * P], ACT.Exp, bias=nmxa[k][:, 1:2],
                               accum_out=suma[k][:, 1:2]).then_inc(a["p"], 1)

            def pt_evac_a(p, k):
                b = 2 * p + k
                act.wait_ge(a["PTp"], b + 1)
                at_least(act, a["Op"], b - 1)
                act.activation(pta[k][:, :], ps[5][:, 0:3 * P], ACT.Copy).then_inc(a["PT"], 1)

            def squares(p, k):
                b = 2 * p + k
                act.wait_ge(a["h2"], b + 1)
                at_least(act, a["ssc"], b - 1)
                at_least(act, a["ss"], 2 * (b - 1))
                for i in range(C):
                    act.activation(sq[:, k, i, :], h2[k][:, i, :], ACT.Square,
                                   accum_out=ss[k][:, i:i + 1]).then_inc(a["ss"], 1)

            def xt_hi(p, k):
                b = 2 * p + k
                act.wait_ge(a["xp"], b + 1)
                act.activation(XT_hi[:, b, :], ps[1][:, 0:N], ACT.Copy).then_inc(a["xhi"], 1)

            run_stages(act, [(2, pt_evac_a), (0, qk_evac), (1, exps_a), (6, squares), (7, xt_hi)], 2, 5, PAIRS)

            act.wait_ge(a["xlo"], B)
            def cd_sums(n):
                act.wait_ge(r["t"], n + 1)
                at_least(act, r["ln"], n)
                act.activation(cd_e[:, :], cd_t[:, :], ACT.Exp, accum_out=cd_sum[:, :]).then_inc(r["e"], 1)
                act.wait_ge(r["e"], n + 1)
                act.activation(cd_ln[:, :], cd_sum[:, :], ACT.Ln).then_inc(r["ln"], 1)

            def u_hi(p, k):
                b, j = 2 * p + k // 4, k % 4
                act.wait_ge(lt["pj"], 6 * b + U_PIECE[j] + 1)
                act.activation(U[b_par(k)][0][:, 2 * j:2 * j + 2, :],
                               ps[U_PIECE[j] % 2][:, :].rearrange("p (h t) -> p h t", h=2),
                               ACT.Copy).then_inc(lt["hi"], 1)

            def exps(p, k):
                g = 8 * p + k
                act.wait_ge(lt["mx"], g + 1)
                at_least(act, lt["PTp"], g - 3)
                for i in range(4):
                    act.activation(pr[k % 4][:, i * P:(i + 1) * P], ps[2 + k % 2][:, i * P:(i + 1) * P], ACT.Exp,
                                   bias=nmx[k % 4][:, i:i + 1],
                                   accum_out=sums[k % 4][:, i:i + 1]).then_inc(lt["p"], 1)

            def cd_act(p, k):
                if isinstance(p, int) and (p == 0 or p >= PAIRS - 1):
                    if p == 0:
                        cd_sums(k)
                    elif p == PAIRS - 1 and k == 1:
                        act.wait_ge(r["tf"], 1)
                        act.activation(score[:, :], cd_t[:, :], ACT.Exp).then_inc(r["sc"], 1)
                elif k < 7:
                    cd_sums(7 * p + 1 + k)

            run_stages(act, [(5, exps), (0, u_hi)], 8, 3, PAIRS - 1, extra=cd_act)

            def xq_evac(p, k):
                if k % 4:
                    return
                b = 2 * p + k // 4
                act.wait_ge(hv["xqp"], b + 1)
                act.activation(xq[b_par(k)][:, :], ps[7][:, 0:NQ], ACT.Copy).then_inc(hv["xq"], 1)

            def gt_evac(p, k):
                if k % 4:
                    return
                b = 2 * p + k // 4
                act.wait_ge(hv["gtp"], b + 1)
                act.activation(GT[b_par(k)][:, :, :], ps[7][:, P:3 * P].rearrange("p (c t) -> p c t", c=C),
                               ACT.Copy).then_inc(hv["gt"], 1)

            def t_hi(p, k):
                g, j = 8 * p + k, k % 4
                act.wait_ge(hv["tp"], g + 1)
                act.activation(U[b_par(k)][0][:, 2 * j:2 * j + 2, 0:NQ],
                               ps[0][:, 0:2 * NQ].rearrange("p (h t) -> p h t", h=2), ACT.Copy).then_inc(hv["thi"], 1)

            def exps_h(p, k):
                g = 8 * p + k
                act.wait_ge(hv["mx"], g + 1)
                at_least(act, hv["PTp"], g - 3)
                for i in range(2):
                    act.activation(pr[k % 4][:, i * N:(i + 1) * N], ps[2 + k % 2][:, i * N:(i + 1) * N], ACT.Exp,
                                   bias=nmx[k % 4][:, i:i + 1],
                                   accum_out=sums[k % 4][:, i:i + 1]).then_inc(hv["p"], 1)

            def rt_evac(p, k):
                if k % 4 != 3:
                    return
                b = 2 * p + k // 4
                act.wait_ge(hv["outp"], b + 1)
                act.activation(rt[b_par(k)][:, :], ps[7][:, 0:D], ACT.Copy).then_inc(hv["rt"], 1)

            def pt_evac_h(p, k):
                g = 8 * p + k
                act.wait_ge(hv["PTp"], g + 1)
                at_least(act, hv["Op"], g - 1)
                act.activation(pt[k % 2][:, :], ps[4 + k % 2][:, :], ACT.Copy).then_inc(hv["PT"], 1)

            act.wait_ge(lt["Op"], 8 * PAIRS)
            act.wait_ge(lt["PT"], 8 * PAIRS)
            run_stages(act, [(8, pt_evac_h), (5, exps_h), (2, t_hi), (10, rt_evac), (7, gt_evac), (0, xq_evac)],
                       8, 3, PAIRS)


        @block.tensor
        def _(pe):
            def triple(out, weights, moving, start=True, stop=True):
                pe.matmul(out, weights[1], moving[0], start=start, stop=False)
                pe.matmul(out, weights[0], moving[1], start=False, stop=False)
                return pe.matmul(out, weights[0], moving[0], start=False, stop=stop)

            pe.wait_ge(g_tab, 1)
            pe.wait_ge(w_in, 16 * W_LOADS)
            for n, src in enumerate((wq_raw[:, 0, :], wkv_raw[:, 0:HID], wq_raw[:, 1, :], None)):
                for q in range(4):
                    s = wv_hT[:, q, :] if src is None else src[:, q * P:(q + 1) * P]
                    mm = pe.transpose(ps[n][:, q * P:(q + 1) * P], s, ident[:, :])
                mm.then_inc(w_tr, 1)
            pe.wait_ge(c_act, 1)
            pe.transpose(ps[4][:, 0:B], c_s[:, :], ident[0:B, 0:B]).then_inc(cT_ps, 1)
            pe.wait_ge(cT_sb, 1)
            pe.matmul(ps[5][0:B, :], cT[:, :], wmod_sb[:, 0:512], start=True, stop=True)
            pe.matmul(ps[6][0:B, 0:256], cT[:, :], wmod_sb[:, 512:768], start=True, stop=True)
            for j in range(2):
                mm = pe.matmul(ps[7][:, j * B:(j + 1) * B], wmod_sb[:, j * D:(j + 1) * D], cT[:, :],
                               start=True, stop=True)
            mm.then_inc(mod_ps, 1)
            pe.wait_ge(w_trs, 4)
            for h in range(HEADS):
                r0 = h % 2 * DH
                mm = pe.matmul(ps[h % 2][:, h // 2 * P:(h // 2 + 1) * P], wkT[r0:r0 + DH, h // 2, :],
                               wqT[r0:r0 + DH, 0, h // 2, :], start=True, stop=True)
            mm.then_inc(w_pr, 1)
            for h in range(HEADS):
                r0 = h % 2 * DH
                mm = pe.matmul(ps[2 + h % 2][:, h // 2 * P:(h // 2 + 1) * P], wqT[r0:r0 + DH, 1, h // 2, :],
                               wk_hT[r0:r0 + DH, h // 2, :], start=True, stop=True)
            mm.then_inc(w_pr, 1)
            pe.wait_ge(w_split, 1)
            pe.wait_ge(mod_sb, 5)

            def h_transpose(p, k):
                b = 2 * p + k
                pe.wait_ge(a["xl"], 2 * b + 2)
                at_least(pe, a["hT"], b)
                for i in range(C):
                    mm = pe.transpose(ps[0][:, i * P:(i + 1) * P], xl[k][:, i, :], ident[:, :])
                mm.then_inc(a["hp"], 1)

            def query_key(p, k):
                b = 2 * p + k
                pe.wait_ge(a["hT"], b + 1)
                at_least(pe, a["qkT"], 2 * b)
                pe.matmul(ps[2][:, 0:N], w_at[:, 0:D], hT[k][:, :], start=True, stop=True)
                pe.matmul(ps[2][:, N:2 * N], w_at[:, D:2 * D], hT[k][:, :], start=True, stop=True).then_inc(a["qkp"], 1)

            def value_a(p, k):
                b = 2 * p + k
                at_least(pe, a["v"], b)
                for i in range(C):
                    mm = pe.matmul(ps[3][:, i * P:(i + 1) * P], hT[k][:, i * P:(i + 1) * P], w_at[:, 2 * D:3 * D],
                                   start=True, stop=True)
                mm.then_inc(a["vp"], 1)

            def scores_a(p, k):
                b = 2 * p + k
                pe.wait_ge(a["qkT"], 2 * b + 2)
                at_least(pe, a["sm"], b)
                pe.matmul(ps[4][:, 0:P], qT[k][:, 0:P], kT[k][:, 0:P], start=True, stop=True)
                pe.matmul(ps[4][:, P:3 * P], qT[k][:, P:2 * P], kT[k][:, :], start=True, stop=True).then_inc(a["Sp"], 1)

            def p_transpose_a(p, k):
                b = 2 * p + k
                pe.wait_ge(a["p"], 2 * b + 2)
                at_least(pe, a["PT"], b)
                for i in range(3):
                    mm = pe.transpose(ps[5][:, i * P:(i + 1) * P], pa[k][:, i * P:(i + 1) * P], ident[:, :])
                mm.then_inc(a["PTp"], 1)

            def values_a(p, k):
                b = 2 * p + k
                pe.wait_ge(a["PT"], b + 1)
                pe.wait_ge(a["v"], b + 1)
                at_least(pe, a["ao"], 2 * b)
                pe.matmul(ps[6][:, 0:P], pta[k][:, 0:P], va[k][:, 0, :], start=True, stop=True)
                pe.matmul(ps[6][:, P:2 * P], pta[k][:, P:2 * P], va[k][:, 0, :], start=True, stop=False)
                pe.matmul(ps[6][:, P:2 * P], pta[k][:, 2 * P:3 * P], va[k][:, 1, :], start=False, stop=True)\
                    .then_inc(a["Op"], 1)

            def x_transpose(p, k):
                b = 2 * p + k
                pe.wait_ge(a["xh"], 2 * b + 2)
                at_least(pe, a["xlo"], b)
                for i in range(C):
                    mm = pe.transpose(ps[1][:, i * P:(i + 1) * P], xhs[k][:, i, :], ident[:, :])
                mm.then_inc(a["xp"], 1)

            run_stages(pe, [(0, h_transpose), (3, values_a), (1, scores_a), (1, value_a), (0, query_key), (2, p_transpose_a),
                            (7, x_transpose)], 2, 5, PAIRS)

            pe.wait_ge(r["Sd"], 2)
            for i in range(C):
                mm = pe.transpose(ps[7][0:R, i * P:(i + 1) * P], S_dense[:, i, :], ident[:, :])
            mm.then_inc(r["Sp"], 1)
            pe.wait_ge(r["rows"], 1)
            pe.wait_ge(a["xlo"], B)
            pe.wait_ge(a["ao"], 2 * B)

            def project(p, k):
                b, j, par = 2 * p + k // 4, k % 4, b_par(k)
                n = 6 * b + U_PIECE[j]
                at_least(pe, lt["pe"], n - 1)
                moving = (XT_hi[:, b, :], XT_lo[:, b, :])
                for i in range(2):
                    mm = triple(ps[U_PIECE[j] % 2][:, i * N:(i + 1) * N],
                                [u[:, 2 * j + i, :] for u in U_w], moving)
                mm.then_inc(lt["pj"], 1)
                if j >= 2:
                    w = j - 2
                    n = 6 * b + V_PIECE[w]
                    at_least(pe, lt["pe"], n - 1)
                    pe.wait_ge(lt[f"xt{par}"], 32 * (p + 1))
                    triple(ps[V_PIECE[w] % 2][:, :], [t[:, w * P:(w + 1) * P] for t in xt[par]],
                           [v[:, :] for v in V_w]).then_inc(lt["pj"], 1)

            def scores(p, k):
                g, b, j, par = 8 * p + k, 2 * p + k // 4, k % 4, b_par(k)
                w, half = j // 2, j % 2
                pe.wait_ge(lt["pe"], 6 * b + (2 if j == 0 else 5))
                at_least(pe, lt["p"], 4 * (g - 1))
                triple(ps[2 + k % 2][:, :].rearrange("p (h t) -> p h t", h=4),
                       [t[:, w * P:(w + 1) * P] for t in xt[par]],
                       [u[:, 4 * half:4 * half + 4, w * P:(w + 1) * P] for u in U[par]]).then_inc(lt["Sp"], 1)

            def p_transpose(p, k):
                g = 8 * p + k
                pe.wait_ge(lt["pn"], g + 1)
                at_least(pe, lt["PT"], g - 1)
                for i in range(4):
                    mm = pe.transpose(ps[4 + k % 2][:, i * P:(i + 1) * P], pr[k % 4][:, i * P:(i + 1) * P], ident[:, :])
                mm.then_inc(lt["PTp"], 1)

            def values(p, k):
                g, b, j, par = 8 * p + k, 2 * p + k // 4, k % 4, b_par(k)
                w, half = j // 2, j % 2
                pe.wait_ge(lt["PT"], g + 1)
                pe.wait_ge(lt["pe"], 6 * b + V_PIECE[w] + 1)
                at_least(pe, lt["oT"], g)
                for q in range(2):
                    for i in range(2):
                        h = 4 * half + 2 * q + i
                        mm = pe.matmul(ps[6][i * DH:(i + 1) * DH, q * P:(q + 1) * P],
                                       V[par][:, w, h * DH:(h + 1) * DH],
                                       pt[k % 2][:, (2 * q + i) * P:(2 * q + i + 1) * P], start=True, stop=True)
                mm.then_inc(lt["Op"], 1)

            def out_light(p, k):
                if k % 2 == 0:
                    return
                g, b, w = 8 * p + k, 2 * p + k // 4, k % 4 // 2
                pe.wait_ge(lt["oT"], g + 1)
                at_least(pe, lt["fin"], 2 * b + w)
                for q in range(4):
                    mm = pe.matmul(ps[7][:, 0:D], oT[w][:, q, :], wo_l_sb[:, q, :], start=(q == 0), stop=(q == 3))
                mm.then_inc(lt["outp"], 1)

            run_stages(pe, [(4, scores), (0, project), (8, values), (7, p_transpose), (9, out_light)],
                       8, 3, PAIRS - 1)

            pe.wait_ge(r["w"], 2)
            pe.wait_ge(lt["fin"], 2 * B)
            for n in range(2):
                for i in range(C):
                    mm = pe.transpose(ps[7][:, (n * C + i) * R:(n * C + i + 1) * R], wsel[:, n, i * P:(i + 1) * P],
                                      ident[0:R, 0:R])
            mm.then_inc(r["selp"], 1)
            pe.wait_ge(r["selT"], 1)
            pe.matmul(ps[7][:, 0:B], tri[:, :], selT[:, 1, 0, 0:B], start=True, stop=True)
            pe.matmul(ps[7][:, B:2 * B], tri[:, :], selT[:, 1, 1, 0:B], start=True, stop=False)
            pe.matmul(ps[7][:, B:2 * B], ones[:, :], selT[:, 1, 0, 0:B], start=False, stop=True).then_inc(r["cum"], 1)
            pe.wait_ge(r["pp"], 1)
            pe.wait_ge(lt["pe"], 6 * B)
            pe.wait_ge(lt["p"], 32 * PAIRS)
            pe.wait_ge(lt["PT"], 8 * PAIRS)
            pe.wait_ge(lt["oT"], 8 * PAIRS)

            def gather(p, k):
                if k % 4:
                    return
                b, par = 2 * p + k // 4, b_par(k)
                pe.wait_ge(hv["G"], 2 * b + 2)
                pe.wait_ge(hv[f"xt{par}"], 48 * (p + 1))
                at_least(pe, hv["gt"], b - 1)
                for i in range(C):
                    mm = pe.matmul(ps[7][:, 0:NQ], xh[par][:, i, :], G[par][:, i, :], start=(i == 0), stop=(i == C - 1))
                mm.then_inc(hv["xqp"], 1)

            def g_transpose(p, k):
                if k % 4:
                    return
                b, par = 2 * p + k // 4, b_par(k)
                at_least(pe, hv["fin"], 2 * (b - 1))
                for i in range(C):
                    mm = pe.transpose(ps[7][:, P + i * P:P + (i + 1) * P], G[par][:, i, :], ident[:, :])
                mm.then_inc(hv["gtp"], 1)

            def project_h(p, k):
                g, b, j, par = 8 * p + k, 2 * p + k // 4, k % 4, b_par(k)
                pe.wait_ge(hv["xq"], b + 1)
                at_least(pe, hv["tlo"], g)
                for i in range(2):
                    mm = pe.matmul(ps[0][:, i * NQ:(i + 1) * NQ], T_w[:, 2 * j + i, :], xq[par][:, :],
                                   start=True, stop=True)
                mm.then_inc(hv["tp"], 1)
                if j % 2:
                    w = j // 2
                    at_least(pe, hv["v"], 2 * b + w)
                    triple(ps[1][:, :], [t[:, w * P:(w + 1) * P] for t in xt[par]],
                           [v[:, :] for v in VH_w]).then_inc(hv["vp"], 1)

            def scores_h(p, k):
                g, b, j, par = 8 * p + k, 2 * p + k // 4, k % 4, b_par(k)
                pe.wait_ge(hv["tlo"], g + 1)
                at_least(pe, hv["p"], 2 * (g - 1))
                for i in range(2):
                    mm = triple(ps[2 + k % 2][:, i * N:(i + 1) * N], [u[:, 2 * j + i, 0:NQ] for u in U[par]],
                                (XT_hi[:, b, :], XT_lo[:, b, :]))
                mm.then_inc(hv["Sp"], 1)

            def p_transpose_h(p, k):
                g = 8 * p + k
                pe.wait_ge(hv["pn"], g + 1)
                at_least(pe, hv["PT"], g - 1)
                for i in range(4):
                    mm = pe.transpose(ps[4 + k % 2][:, i * P:(i + 1) * P], pr[k % 4][:, i * P:(i + 1) * P], ident[:, :])
                mm.then_inc(hv["PTp"], 1)

            def values_h(p, k):
                g, b, j, par = 8 * p + k, 2 * p + k // 4, k % 4, b_par(k)
                pe.wait_ge(hv["PT"], g + 1)
                pe.wait_ge(hv["v"], 2 * b + 2)
                at_least(pe, hv["oT"], g)
                for w in range(C):
                    for i in range(2):
                        h = 2 * j + i
                        mm = pe.matmul(ps[6][i * DH:(i + 1) * DH, 0:NQ], V[par][:, w, h * DH:(h + 1) * DH],
                                       pt[k % 2][:, (2 * i + w) * P:(2 * i + w + 1) * P],
                                       start=(w == 0), stop=(w == C - 1))
                mm.then_inc(hv["Op"], 1)

            def out_heavy(p, k):
                if k % 4 != 3:
                    return
                g, b, par = 8 * p + k, 2 * p + k // 4, b_par(k)
                pe.wait_ge(hv["oT"], g + 1)
                pe.wait_ge(hv["xq"], min(b + 4, B) if isinstance(b, int) else b + 4)
                if isinstance(b, int) and b + 4 > B:
                    pe.wait_ge(hv["gt"], min(b + 2, B))
                for q in range(4):
                    mm = pe.matmul(ps[7][:, 0:D], oT[par][:, q, :], wo_h_sb[:, q, :], start=(q == 0), stop=(q == 3))
                mm.then_inc(hv["outp"], 1)

            def scatter(p, k):
                if k % 4 != 3:
                    return
                b, par = 2 * p + k // 4, b_par(k)
                pe.wait_ge(hv["rt"], b + 1)
                for i in range(C):
                    mm = pe.matmul(ps[7][:, P + i * P:P + (i + 1) * P], GT[par][:, i, :], rt[par][:, :],
                                   start=True, stop=True)
                mm.then_inc(hv["scp"], 1)

            run_stages(pe, [(4, scores_h), (2, project_h), (8, values_h), (10, out_heavy), (11, scatter),
                            (7, g_transpose), (7, p_transpose_h), (0, gather)], 8, 3, PAIRS)

        @block.vector
        def _(dve):
            def mean_var(st, t, mean, ve, three, six, seven, base=0):
                (me, ce), (mo, co) = (st[..., 1], st[..., 2]), (st[..., 4], st[..., 5])
                dve.tensor_tensor(t[0], me, mo, ALU.add).then_inc(three, 1)
                dve.tensor_tensor(t[1], me, mo, ALU.subtract).then_inc(three, 1)
                dve.tensor_tensor(t[2], ce, co, ALU.add).then_inc(three, 1)
                dve.wait_ge(three, 3 * base + 3)
                dve.tensor_scalar(mean, t[0], 0.5, None, ALU.mult).then_inc(six, 1)
                dve.scalar_tensor_tensor(t[3], t[1], 0.25, t[1], ALU.mult, ALU.mult).then_inc(six, 1)
                dve.tensor_scalar(t[4], t[2], 1.0 / D, LN_EPS, ALU.mult, ALU.add).then_inc(six, 1)
                dve.wait_ge(six, 3 * base + 3)
                dve.tensor_tensor(ve, t[3], t[4], ALU.add).then_inc(seven, 1)

            for i in range(4):
                dve.wait_ge(x_in[i], 16)
                with dve.Fori(4 * i, 4 * i + 4) as b:
                    for q in range(C):
                        dve.bn_stats(st1[:, b, q, :], X[:, b, q, :]).then_inc(st1_done, 1)
            dve.wait_ge(st1_done, 2 * B)
            mean_var(st1[:, :, :, :].rearrange("p b c s -> p (b c) s"), [t1[:, i, :] for i in range(5)], mean1[:, :],
                     ve1[:, :], mv1_sums, mv1_parts, ve1_done)

            dve.wait_ge(c_exp, 1)
            dve.tensor_scalar(c_d[:, :], c_e[:, :], 1.0, None, ALU.add).then_inc(c_den, 1)
            dve.wait_ge(c_den, 1)
            dve.reciprocal(c_r[:, :], c_d[:, :]).then_inc(c_den, 1)
            dve.wait_ge(c_den, 2)
            dve.tensor_tensor(c_s[:, :], c_sb[:, :], c_r[:, :], ALU.mult).then_inc(c_act, 1)
            dve.wait_ge(w_tr, 4)
            dve.tensor_copy(wqT[:, 0], ps[0][:, :].rearrange("p (q d) -> p q d", q=4)).then_inc(w_trs, 1)
            dve.tensor_copy(wkT[:, :, :], ps[1][:, :].rearrange("p (q d) -> p q d", q=4)).then_inc(w_trs, 1)
            dve.tensor_copy(wqT[:, 1], ps[2][:, :].rearrange("p (q d) -> p q d", q=4)).then_inc(w_trs, 1)
            dve.tensor_scalar(big[:, 0:4, :], ps[3][:, :].rearrange("p (q d) -> p q d", q=4), gam_col[:, 1:2], None,
                              ALU.mult).then_inc(w_trs, 1)
            dve.tensor_scalar(big[:, 4:8, :], wkv_raw[:, HID:2 * HID].rearrange("p (q d) -> p q d", q=4),
                              gam_col[:, 0:1], None, ALU.mult).then_inc(w_trs, 1)
            dve.wait_ge(cT_ps, 1)
            dve.tensor_copy(cT[:, :], ps[4][:, 0:B]).then_inc(cT_sb, 1)
            dve.wait_ge(w_trs, 5)
            for w, lo in ((VH_w, 0), (V_w, 4)):
                v = big[:, lo:lo + 4, :].rearrange("p q d -> p (q d)")
                dve.tensor_copy(w[0][:, :], v).then_inc(v_hi, 1)
            dve.wait_ge(v_hi, 2)
            for w, lo in ((VH_w, 0), (V_w, 4)):
                v = big[:, lo:lo + 4, :].rearrange("p q d -> p (q d)")
                dve.tensor_tensor(w[1][:, :], v, w[0][:, :].bitcast(F32), ALU.subtract).then_inc(v_lo, 1)
            dve.tensor_scalar(gam_sc[:, :], gam_col[:, :], HEAD_SCALE, None, ALU.mult).then_inc(w_small, 1)
            dve.wait_ge(bc_in, 16 * BC_LOADS)
            dve.wait_ge(w_in, 16 * W_LOADS)
            dve.tensor_scalar(bq_sc[:, :], b_col[:, 0:1], ATTN_SCALE, None, ALU.mult).then_inc(w_small, 1)
            dve.wait_ge(mod_ps, 1)
            dve.tensor_copy(modT[:, 0, :], ps[7][:, 0:B]).then_inc(mod_sb, 1)
            dve.tensor_scalar(modT[:, 1, :], ps[7][:, B:2 * B], 1.0, None, ALU.add).then_inc(mod_sb, 1)
            dve.tensor_copy(mod_raw[:, 0:4, :], ps[5][0:B, :].rearrange("b (j d) -> b j d", j=4)).then_inc(mod_raws, 1)
            dve.tensor_copy(mod_raw[:, 4:6, :], ps[6][0:B, 0:256].rearrange("b (j d) -> b j d", j=2)).then_inc(mod_raws, 1)
            dve.wait_ge(mod_raws, 2)
            gates = mod_raw[:, 2:6:3, :]
            dve.tensor_scalar(gate_s[:, :, :], gates, 0.0, 2.0, ALU.is_ge, ALU.mult).then_inc(mod_raws, 1)
            dve.scalar_tensor_tensor(gate_a[:, :, :], gates, -1.0, gates, ALU.mult, ALU.max).then_inc(mod_raws, 1)
            dve.wait_ge(mod_raws, 4)
            dve.tensor_scalar(gate_m[:, :, :], gate_a[:, :, :], 0.25, None, ALU.max).then_inc(mod_raws, 1)
            dve.wait_ge(mod_raws, 5)
            dve.scalar_tensor_tensor(mod_fix[:, 0:4:3, :], gate_s[:, :, :], -1.0, gate_m[:, :, :], ALU.add, ALU.mult)\
                .then_inc(mod_sb, 1)
            dve.tensor_copy(mod_fix[:, 2, :], mod_raw[:, 3, :]).then_inc(mod_sb, 1)
            dve.tensor_scalar(mod_fix[:, 1, :], mod_raw[:, 4, :], 1.0, None, ALU.add).then_inc(mod_sb, 1)
            dve.wait_ge(w_small, 1)
            dve.wait_ge(w_pr, 1)
            dve.wait_ge(v_lo, 2)
            for i in range(2):
                dve.scalar_tensor_tensor(big[:, i:HEADS:2, :], ps[i][:, :].rearrange("p (h d) -> p h d", h=4),
                                         gam_sc[:, 0:1], gam_bc[:, 0:1, :].broadcast_to([P, 4, D]), ALU.mult, ALU.mult)\
                    .then_inc(w_prs, 1)
            dve.wait_ge(w_pr, 2)
            for i in range(2):
                dve.scalar_tensor_tensor(T_w[:, i:HEADS:2, :], ps[2 + i][:, :].rearrange("p (h d) -> p h d", h=4),
                                         gam_sc[:, 1:2], gam_bc[:, 1:2, :].broadcast_to([P, 4, D]), ALU.mult, ALU.mult)\
                    .then_inc(w_prs, 1)
            dve.wait_ge(w_prs, 4)
            dve.tensor_copy(U_w[0][:, :, :], big[:, :, :]).then_inc(w_prs, 1)
            dve.wait_ge(w_prs, 5)
            dve.tensor_tensor(U_w[1][:, :, :], big[:, :, :], U_w[0][:, :, :].bitcast(F32), ALU.subtract)\
                .then_inc(w_split, 1)
            dve.memset(cd_t[:, :], 0.0).then_inc(r["t"], 1)
            dve.memset(cd_m[:, :], 0.0).then_inc(r["m"], 1)
            dve.wait_ge(rs1_done, 1)
            dve.wait_ge(w_split, 1)
            dve.wait_ge(g_tab, 5)
            dve.wait_ge(mod_sb, 5)
            dve.wait_ge(mod_in, 16)

            def ln1(p, k):
                b = 2 * p + k
                at_least(dve, a["hp"], b - 1)
                for i in range(C):
                    dve.tensor_scalar(xl[k][:, i, :], X[:, b, i, :], mean1_bc[:, b, i:i + 1],
                                      rs1_bc[:, b, i:i + 1], ALU.subtract, ALU.mult).then_inc(a["xl"], 1)

            def h_evac(p, k):
                b = 2 * p + k
                dve.wait_ge(a["hp"], b + 1)
                at_least(dve, a["vp"], b - 1)
                dve.tensor_scalar(hT[k][:, :], ps[0][:, 0:N], modT[:, 1, bass.ds(b, 1)], modT[:, 0, bass.ds(b, 1)],
                                  ALU.mult, ALU.add).then_inc(a["hT"], 1)

            def v_evac(p, k):
                b = 2 * p + k
                dve.wait_ge(a["vp"], b + 1)
                at_least(dve, a["Op"], b - 1)
                dve.tensor_tensor(va[k][:, :, :], ps[3][:, 0:N].rearrange("p (c d) -> p c d", c=C),
                                  bv_bc[:, None, :].broadcast_to([P, C, D]), ALU.add).then_inc(a["v"], 1)

            def mask_max(p, k):
                b = 2 * p + k
                dve.wait_ge(a["Sp"], b + 1)
                at_least(dve, a["p"], 2 * (b - 1))
                dve.tensor_tensor(sm[k][:, :], ps[4][:, 0:3 * P], mask[:, :], ALU.add).then_inc(a["sm"], 1)
                dve.wait_ge(a["sm"], b + 1)
                for i, (s, e) in enumerate(((0, P), (P, 3 * P))):
                    dve.tensor_reduce(nmxa[k][:, i:i + 1], sm[k][:, s:e], AX.X, ALU.max, negate=True)\
                        .then_inc(a["nmx"], 1)

            def attn_out(p, k):
                b = 2 * p + k
                dve.wait_ge(a["p"], 2 * b + 2)
                dve.reciprocal(rinva[k][:, :], suma[k][:, :]).then_inc(a["ri"], 1)
                dve.wait_ge(a["ri"], b + 1)
                dve.wait_ge(a["Op"], b + 1)
                at_least(dve, a["x1"], b - 1)
                for i in range(C):
                    dve.scalar_tensor_tensor(ao[k][:, i, :], ps[6][:, i * P:(i + 1) * P], rinva[k][:, i:i + 1],
                                             mod_bc[:, b, 0, :], ALU.mult, ALU.mult).then_inc(a["ao"], 1)

            def ln2_stats(p, k):
                b = 2 * p + k
                dve.wait_ge(a["x1"], b + 1)
                for i in range(C):
                    dve.bn_stats(st2[k][:, i, :], X[:, b, i, :]).then_inc(a["st"], 1)
                dve.wait_ge(a["st"], 2 * b + 2)
                mean_var(st2[k][:, :, :], [t2[k][:, i, :] for i in range(5)], mean2[k][:, :], ve2[k][:, :],
                         a["mv"], a["mp"], a["ve"], b)

            def ln2(p, k):
                b = 2 * p + k
                dve.wait_ge(a["rs"], b + 1)
                at_least(dve, a["hm"], b - 1)
                for i in range(C):
                    dve.tensor_scalar(hn[k][:, i, :], X[:, b, i, :], mean2[k][:, i:i + 1], rs2[k][:, i:i + 1],
                                      ALU.subtract, ALU.mult).then_inc(a["hn"], 1)

            def route(p, k):
                b = 2 * p + k
                dve.wait_ge(a["h2"], b + 1)
                at_least(dve, a["S"], b - 1)
                for i in range(C):
                    for t in range(2):
                        dve.tensor_tensor_reduce(rprod[:, k, 2 * i + t, :], h2[k][:, i, :], tok_bc[:, t, :], 1.0, 0.0,
                                                 ALU.mult, ALU.add, s4[k][:, 2 * i + t:2 * i + t + 1])\
                            .then_inc(a["s4"], 1)
                dve.wait_ge(a["ss"], 2 * b + 2)
                dve.tensor_scalar(ssc[k][:, :], ss[k][:, :], 1e-24, None, ALU.max).then_inc(a["ssc"], 1)
                dve.wait_ge(a["s4"], 4 * b + 4)
                dve.tensor_copy(S_all[:, b, :, :], s4[k][:, :].rearrange("p (c t) -> p c t", c=C)).then_inc(a["S"], 1)

            def xhat(p, k):
                b = 2 * p + k
                dve.wait_ge(a["rn"], b + 1)
                at_least(dve, a["xp"], b - 1)
                at_least(dve, a[f"xhd{k}"], 16 * p)
                for i in range(C):
                    dve.tensor_scalar(xhs[k][:, i, :], h2[k][:, i, :], rn[k][:, i:i + 1], float(D) ** 0.5,
                                      ALU.mult, ALU.mult).then_inc(a["xh"], 1)

            def xt_lo(p, k):
                b = 2 * p + k
                dve.wait_ge(a["xhi"], b + 1)
                dve.tensor_tensor(XT_lo[:, b, :], ps[1][:, 0:N], XT_hi[:, b, :].bitcast(F32), ALU.subtract)\
                    .then_inc(a["xlo"], 1)

            mean1_bc = mean1[:, :].rearrange("p (b c) -> p b c", c=C)
            rs1_bc = rs1[:, :].rearrange("p (b c) -> p b c", c=C)
            ln1(0, 0)
            run_stages(dve, [(0, h_evac), (1, mask_max), (1, v_evac), (3, attn_out), (7, xhat), (4, ln2_stats),
                             (5, ln2), (7, xt_lo), (6, route), (-1, ln1)], 2, 5, PAIRS - 1)

            dve.wait_ge(a["S"], B)
            dve.wait_ge(a["xlo"], B)
            for t in range(2):
                dve.tensor_copy(S_dense[:, :, t * B:(t + 1) * B], S_all[:, :, :, t].rearrange("p b c -> p c b"))\
                    .then_inc(r["Sd"], 1)
            dve.wait_ge(r["Sp"], 1)
            dve.tensor_copy(s_rows[:, :], ps[7][0:R, 0:N]).then_inc(r["rows"], 1)
            dve.wait_ge(r["rows"], 1)
            dve.tensor_reduce(smax[:, :], s_rows[:, :], AX.X, ALU.max).then_inc(r["smax"], 1)
            dve.wait_ge(r["smax"], 1)

            def cd_next(n):
                dve.wait_ge(r["ln"], n)
                dve.tensor_scalar(cd_na[:, :], cd_ln[:, :], cd_m[:, :], log_k[:, :], ALU.add, ALU.subtract)\
                    .then_inc(r["na"], 1)
                dve.wait_ge(r["na"], n)
                dve.tensor_tensor(cd_m[:, :], smax[:, :], cd_na[:, :], ALU.min).then_inc(r["m"], 1)
                dve.wait_ge(r["m"], n + 1)
                dve.tensor_scalar(cd_t[:, :], s_rows[:, :], cd_na[:, :], cd_m[:, :], ALU.min, ALU.subtract)\
                    .then_inc(r["t"], 1)

            def u_lo(p, k):
                b, j, par = 2 * p + k // 4, k % 4, b_par(k)
                dve.wait_ge(lt["hi"], 4 * b + j + 1)
                dve.tensor_tensor(U[par][1][:, 2 * j:2 * j + 2, :],
                                  ps[U_PIECE[j] % 2][:, :].rearrange("p (h t) -> p h t", h=2),
                                  U[par][0][:, 2 * j:2 * j + 2, :].bitcast(F32), ALU.subtract).then_inc(lt["pe"], 1)
                if j >= 2:
                    w = j - 2
                    dve.wait_ge(lt["pj"], 6 * b + V_PIECE[w] + 1)
                    at_least(dve, lt["Op"], 4 * (b - 2) + 2 * (w + 1))
                    dve.tensor_copy(V[par][:, w, :], ps[V_PIECE[w] % 2][:, :]).then_inc(lt["pe"], 1)

            def neg_max(p, k):
                g = 8 * p + k
                dve.wait_ge(lt["Sp"], g + 1)
                dve.tensor_reduce(nmx[k % 4][:, :], ps[2 + k % 2][:, :].rearrange("p (h t) -> p h t", h=4), AX.X,
                                  ALU.max, negate=True).then_inc(lt["mx"], 1)

            def recip(p, k):
                g = 8 * p + k
                dve.wait_ge(lt["p"], 4 * g + 4)
                dve.reciprocal(rinv[k % 4][:, :], sums[k % 4][:, :]).then_inc(lt["ri"], 1)

            def pt_evac(p, k):
                g = 8 * p + k
                dve.wait_ge(lt["PTp"], g + 1)
                at_least(dve, lt["Op"], g - 1)
                dve.tensor_copy(pt[k % 2][:, :], ps[4 + k % 2][:, :]).then_inc(lt["PT"], 1)

            def o_evac(p, k):
                g, b, j = 8 * p + k, 2 * p + k // 4, k % 4
                w, half = j // 2, j % 2
                dve.wait_ge(lt["Op"], g + 1)
                at_least(dve, lt["outp"], 2 * b + w - 1)
                dve.tensor_copy(oT[w][:, 2 * half:2 * half + 2, :],
                                ps[6][:, 0:2 * P].rearrange("p (q t) -> p q t", q=2)).then_inc(lt["oT"], 1)

            def finish_light(p, k):
                if k % 2 == 0:
                    return
                b, w = 2 * p + k // 4, k % 4 // 2
                dve.wait_ge(lt["outp"], 2 * b + w + 1)
                at_least(dve, lt["x"], 2 * b + w - 1)
                dve.tensor_tensor(tmp[w][:, 0, :], ps[7][:, 0:D], mod_bc[:, b, 3, :], ALU.mult).then_inc(lt["fin"], 1)

            def top_round(n):
                src = score if n == 0 else left[(n + 1) % 2]
                if n:
                    dve.wait_ge(r["left"], n)
                dve.max(top8[n % 2][:, :], src[:, :]).then_inc(r["top"], 1)
                dve.wait_ge(r["top"], n + 1)
                dve.match_replace(left[n % 2][:, :], top8[n % 2][:, :], src[:, :], -1.0).then_inc(r["left"], 1)

            def cd_dve(p, k):
                if isinstance(p, int) and (p == 0 or p >= PAIRS - 1):
                    if p == 0 and k >= 1:
                        cd_next(k)
                    elif p == PAIRS - 1 and k == 0:
                        dve.wait_ge(r["ln"], CD_ITERS)
                        dve.tensor_scalar(cd_na[:, :], cd_ln[:, :], cd_m[:, :], log_k[:, :], ALU.add, ALU.subtract)\
                            .then_inc(r["na"], 1)
                        dve.wait_ge(r["na"], CD_ITERS)
                        dve.tensor_scalar(cd_t[:, :], s_rows[:, :], cd_na[:, :], 0.0, ALU.subtract, ALU.min)\
                            .then_inc(r["tf"], 1)
                    elif p == PAIRS - 1 and k >= 2:
                        if k == 2:
                            dve.wait_ge(r["sc"], 1)
                        for n in range(3 * (k - 2), min(3 * (k - 1), NQ // 8)):
                            top_round(n)
                    elif p == PAIRS and k == 0:
                        dve.tensor_scalar(w1m[:, :], score[:, :], -1.0, 1.0, ALU.mult, ALU.add).then_inc(r["w1"], 1)
                        dve.wait_ge(r["w1"], 1)
                        dve.tensor_tensor(wsel[:, 0, :], score[:, :], w1m[:, :], ALU.add).then_inc(r["w"], 1)
                        dve.wait_ge(r["left"], NQ // 8)
                        dve.tensor_scalar(wsel[:, 1, :], left[(NQ // 8 - 1) % 2][:, :], -1.0, None, ALU.is_equal)\
                            .then_inc(r["w"], 1)
                elif k < 7:
                    cd_next(7 * p + 1 + k)

            run_stages(dve, [(1, u_lo), (8, pt_evac), (6, recip), (4, neg_max), (8, o_evac), (10, finish_light)],
                       8, 3, PAIRS - 1, extra=cd_dve)

            dve.wait_ge(r["selp"], 1)
            dve.tensor_copy(selT[:, :, :, :].rearrange("p n c r -> p (n c r)"), ps[7][:, 0:2 * C * R]).then_inc(r["selT"], 1)
            dve.wait_ge(r["cum"], 1)
            dve.wait_ge(r["selT"], 1)
            dve.tensor_tensor(pos_p[:, :, :], ps[7][:, 0:C * B].rearrange("p (c b) -> p c b", c=C),
                              selT[:, 1, :, 0:B], ALU.mult).then_inc(r["pp"], 1)
            dve.wait_ge(r["pp"], 1)
            dve.tensor_scalar(pos[:, :, :], pos_p[:, :, :], -1.0, None, ALU.add).then_inc(r["pos"], 1)
            dve.wait_ge(r["pos"], 1)

            def one_hot(p, k):
                if k % 4:
                    return
                b, par = 2 * p + k // 4, b_par(k)
                at_least(dve, hv["gtp"], b - 1)
                for i in range(C):
                    dve.tensor_scalar(G[par][:, i, :], iota[:, :], pos[:, i, bass.ds(b, 1)], None, ALU.is_equal)\
                        .then_inc(hv["G"], 1)

            def t_lo(p, k):
                g, b, j, par = 8 * p + k, 2 * p + k // 4, k % 4, b_par(k)
                dve.wait_ge(hv["thi"], g + 1)
                dve.tensor_tensor(U[par][1][:, 2 * j:2 * j + 2, 0:NQ],
                                  ps[0][:, 0:2 * NQ].rearrange("p (h t) -> p h t", h=2),
                                  U[par][0][:, 2 * j:2 * j + 2, 0:NQ].bitcast(F32), ALU.subtract).then_inc(hv["tlo"], 1)
                if j % 2:
                    w = j // 2
                    dve.wait_ge(hv["vp"], 2 * b + w + 1)
                    at_least(dve, hv["Op"], 4 * (b - 1))
                    dve.tensor_scalar(V[par][:, w, :], ps[1][:, :], selT[:, 0, w, bass.ds(B + b, 1)], None, ALU.mult)\
                        .then_inc(hv["v"], 1)

            def neg_max_h(p, k):
                g = 8 * p + k
                dve.wait_ge(hv["Sp"], g + 1)
                dve.tensor_reduce(nmx[k % 4][:, 0:2], ps[2 + k % 2][:, :].rearrange("p (h t) -> p h t", h=2), AX.X,
                                  ALU.max, negate=True).then_inc(hv["mx"], 1)

            def recip_h(p, k):
                g = 8 * p + k
                dve.wait_ge(hv["p"], 2 * g + 2)
                dve.reciprocal(rinv[k % 4][:, 0:2], sums[k % 4][:, 0:2]).then_inc(hv["ri"], 1)

            def o_evac_h(p, k):
                g, b, j, par = 8 * p + k, 2 * p + k // 4, k % 4, b_par(k)
                dve.wait_ge(hv["Op"], g + 1)
                at_least(dve, hv["outp"], b - 1)
                dve.tensor_copy(oT[par][:, j, :], ps[6][:, 0:NQ]).then_inc(hv["oT"], 1)

            def finish_heavy(p, k):
                if k % 4 != 3:
                    return
                b, par = 2 * p + k // 4, b_par(k)
                dve.wait_ge(hv["scp"], b + 1)
                at_least(dve, hv["ob"], b - 1)
                for i in range(C):
                    dve.scalar_tensor_tensor(tmp[par][:, i, :], ps[7][:, P + i * P:P + (i + 1) * P],
                                             selT[:, 0, i, bass.ds(b, 1)], mod_bc[:, b, 3, :], ALU.mult, ALU.mult)\
                        .then_inc(hv["fin"], 1)

            dve.wait_ge(lt["x"], 2 * B)
            run_stages(dve, [(0, one_hot), (3, t_lo), (6, recip_h), (4, neg_max_h), (8, o_evac_h), (11, finish_heavy)],
                       8, 3, PAIRS)


_INS = ["L0_attn_x", "L0_attn_W", "L0_attn_b", "L0_ffn_gamma_light", "L0_ffn_wq_light", "L0_ffn_wkv_light",
        "L0_ffn_wo_light", "L0_ffn_q_routing_token", "L0_ffn_kv_routing_token", "L0_ffn_gamma_heavy",
        "L0_ffn_wq_heavy", "L0_ffn_wkv_heavy", "L0_ffn_wo_heavy", "L0_c", "L0_wmod"]


def kernel(**inputs):
    import numpy as _np
    import concourse.bacc as _bacc
    from concourse import mybir as _mybir
    from concourse.bass_utils import run_bass_kernel_spmd as _run

    nc = _bacc.Bacc("TRN2", target_bir_lowering=False, num_devices=1)
    arrays, args = {}, []
    for name in _INS:
        arr = _np.ascontiguousarray(inputs[name])
        arrays[f"in_{name}"] = arr
        args.append(nc.dram_tensor(f"in_{name}", arr.shape, _mybir.dt.from_np(arr.dtype), kind="ExternalInput").ap())
    out = nc.dram_tensor("out", (B, N, D), F32, kind="ExternalOutput").ap()
    adaln_routed_attention(nc, *args, out)
    r = _run(nc, [arrays], core_ids=[0])
    return r.results[0]["out"]
```

```python
from contextlib import ExitStack

import numpy as np

import concourse.bass as bass
from concourse import mybir
from concourse.alu_op_type import AluOpType as ALU

ACT = mybir.ActivationFunctionType
AX = mybir.AxisListType
F32 = mybir.dt.float32
F32R = mybir.dt.float32r

P = 128
B, N, D = 16, 256, 128
C = N // P
HEADS, DH = 8, 64
HID = HEADS * DH
NQ = 128
K_Q, K_KV = NQ * 9 / 8, float(N)
CD_ITERS = 50
LN_EPS = 1e-5
MASKED = -9.0e15
ATTN_SCALE = float(D) ** -0.5
HEAD_SCALE = float(DH) ** -0.5
PAIRS = B // 2


def at_least(eng, sem, value):
    if isinstance(value, int) and value <= 0:
        return
    eng.wait_ge(sem, value)


def run_stages(eng, stages, units, first, last, extra=None):
    def step(p, k):
        for lag, f in stages:
            q, kk = p + (k - lag) // units, (k - lag) % units
            if isinstance(p, int) and not 0 <= q < PAIRS:
                continue
            f(q, kk)
        if extra is not None:
            extra(p, k)

    deepest = max(lag for lag, _ in stages)
    tail = -(-deepest // units)
    for p in range(first):
        for k in range(units):
            step(p, k)
    with eng.Fori(first, last) as p:
        for k in range(units):
            step(p, k)
    for p in range(last, PAIRS + tail):
        for k in range(units):
            step(p, k)


def adaln_routed_attention(nc, x, w_attn, b_attn, gamma_l, wq_l, wkv_l, wo_l, q_tok, kv_tok,
                           gamma_h, wq_h, wkv_h, wo_h, c, wmod, out):
    with ExitStack() as ctx:
        def sb(name, shape, dt=F32):
            return ctx.enter_context(nc.sbuf_tensor(name, shape, dt))

        def sem(name):
            return ctx.enter_context(nc.semaphore(name))

        ps = [ctx.enter_context(nc.psum_tensor(f"bank{i}", [P, 512], F32)) for i in range(8)]
        xh_dram = nc.dram_tensor("xh_scratch", [B, P, C * D], F32).ap()
        mod_rows_dram = nc.dram_tensor("mod_rows_scratch", [B, 4, D], F32).ap()

        X = sb("X", [P, B, C, D])
        XT_hi = sb("XT_hi", [P, B, N], F32R)
        XT_lo = sb("XT_lo", [P, B, N], F32R)
        ident = sb("ident", [P, P])
        tri = sb("tri", [P, P])
        ones = sb("ones", [P, P])
        iota = sb("iota", [P, P])
        mask = sb("mask", [P, 3 * P])
        neg_half = sb("neg_half", [P, B * C])
        mod_bc = sb("mod_bc", [P, B, 4, D])
        tok_bc = sb("tok_bc", [P, 2, D])
        bv_bc = sb("bv_bc", [P, D])
        gam_bc = sb("gam_bc", [P, 2, D])
        gam_col = sb("gam_col", [P, 2])
        gam_sc = sb("gam_sc", [P, 2])
        b_col = sb("b_col", [P, 2])
        bq_sc = sb("bq_sc", [P, 1])
        modT = sb("modT", [P, 2, B])
        w_at = sb("w_at", [P, 3 * D])
        wmod_sb = sb("wmod_sb", [P, 6 * D])
        wo_l_sb = sb("wo_l_sb", [P, 4, D])
        wo_h_sb = sb("wo_h_sb", [P, 4, D])
        U_w = [sb(f"U_w_{s}", [P, HEADS, D], F32R) for s in ("hi", "lo")]
        V_w = [sb(f"V_w_{s}", [P, HID], F32R) for s in ("hi", "lo")]
        T_w = sb("T_w", [P, HEADS, D])
        VH_w = [sb(f"VH_w_{s}", [P, HID], F32R) for s in ("hi", "lo")]

        S_all = sb("S_all", [P, B, C, 2])
        two = range(2)
        xhs = [sb(f"xhs{i}", [P, C, D]) for i in two]

        R = 2 * B
        S_dense = sb("S_dense", [P, C, R])
        s_rows = sb("s_rows", [R, N])
        smax = sb("smax", [R, 1])
        log_k = sb("log_k", [R, 1])
        cd_t = sb("cd_t", [R, N])
        cd_e = sb("cd_e", [R, N])
        cd_m = sb("cd_m", [R, 1])
        cd_sum = sb("cd_sum", [R, 1])
        cd_ln = sb("cd_ln", [R, 1])
        cd_na = sb("cd_na", [R, 1])
        score = sb("score", [R, N])
        left = [sb(f"left{i}", [R, N]) for i in two]
        top8 = [sb(f"top8{i}", [R, 8]) for i in two]
        w1m = sb("w1m", [R, N])
        wsel = sb("wsel", [R, 2, N])
        selT = sb("selT", [P, 2, C, R])
        pos_p = sb("pos_p", [P, C, B])
        pos = sb("pos", [P, C, B])

        st1 = sb("st1", [P, B, C, 6])
        t1 = sb("t1", [P, 5, B * C])
        mean1 = sb("mean1", [P, B * C])
        ve1 = sb("ve1", [P, B * C])
        rs1 = sb("rs1", [P, B * C])
        nm1 = sb("nm1", [P, B * C])
        early = ExitStack()
        late = sb
        sb = lambda name, shape, dt=F32: early.enter_context(nc.sbuf_tensor(name, shape, dt))
        wq_raw = sb("wq_raw", [P, 2, HID])
        wkv_raw = sb("wkv_raw", [P, 2 * HID])
        wk_hT = sb("wk_hT", [P, 4, D])
        wv_hT = sb("wv_hT", [P, 4, D])
        wqT = sb("wqT", [P, 2, 4, D])
        wkT = sb("wkT", [P, 4, D])
        big = sb("big", [P, HEADS, D])
        v_big = sb("v_big", [P, 2, HID])
        c_sb = sb("c_sb", [B, D])
        c_e = sb("c_e", [B, D])
        c_d = sb("c_d", [B, D])
        c_r = sb("c_r", [B, D])
        c_s = sb("c_s", [B, D])
        cT = sb("cT", [P, B])
        mod_raw = sb("mod_raw", [B, 4, D])
        mod_fix = sb("mod_fix", [B, 4, D])
        gate_s = sb("gate_s", [B, 2, D])
        gate_a = sb("gate_a", [B, 2, D])
        gate_m = sb("gate_m", [B, 2, D])

        xl = [sb(f"xl{i}", [P, C, D]) for i in two]
        hT = [sb(f"hT{i}", [P, N]) for i in two]
        qT = [sb(f"qT{i}", [P, N]) for i in two]
        kT = [sb(f"kT{i}", [P, N]) for i in two]
        va = [sb(f"va{i}", [P, C, D]) for i in two]
        sm = [sb(f"sm{i}", [P, 3 * P]) for i in two]
        mxa = [sb(f"mxa{i}", [P, C]) for i in two]
        nmxa = [sb(f"nmxa{i}", [P, C]) for i in two]
        pa = [sb(f"pa{i}", [P, 3 * P]) for i in two]
        suma = [sb(f"suma{i}", [P, C]) for i in two]
        rinva = [sb(f"rinva{i}", [P, C]) for i in two]
        pta = [sb(f"pta{i}", [P, 3 * P]) for i in two]
        ao = [sb(f"ao{i}", [P, C, D]) for i in two]
        st2 = [sb(f"st2{i}", [P, C, 6]) for i in two]
        mv2 = [sb(f"mv2{i}", [P, C, 2]) for i in two]
        nm2 = [sb(f"nm2{i}", [P, C]) for i in two]
        ve2 = [sb(f"ve2{i}", [P, C]) for i in two]
        rs2 = [sb(f"rs2{i}", [P, C]) for i in two]
        hn = [sb(f"hn{i}", [P, C, D]) for i in two]
        hm = [sb(f"hm{i}", [P, C, D]) for i in two]
        h2 = [sb(f"h2{i}", [P, C, D]) for i in two]
        sq = sb("sq", [P, 2, C, D])
        ss = [sb(f"ss{i}", [P, C]) for i in two]
        ssc = [sb(f"ssc{i}", [P, C]) for i in two]
        rn = [sb(f"rn{i}", [P, C]) for i in two]
        rprod = sb("rprod", [P, 2, 4, D])
        s4 = [sb(f"s4{i}", [P, 4]) for i in two]
        early.close()
        sb = late
        xt = [[sb(f"xt{i}{s}", [P, N], F32R) for s in ("hi", "lo")] for i in two]
        xh = [sb(f"xh{i}", [P, C, D]) for i in two]
        U = [[sb(f"U{i}{s}", [P, HEADS, N], F32R) for s in ("hi", "lo")] for i in two]
        V = [sb(f"V{i}", [P, C, HID]) for i in two]
        nmx = [sb(f"nmx{i}", [P, 4]) for i in range(4)]
        sums = [sb(f"sums{i}", [P, 4]) for i in range(4)]
        rinv = [sb(f"rinv{i}", [P, 4]) for i in range(4)]
        pr = [sb(f"pr{i}", [P, 512]) for i in range(4)]
        pt = [sb(f"pt{i}", [P, 512]) for i in two]
        oT = [sb(f"oT{i}", [P, 4, P]) for i in two]
        tmp = [sb(f"tmp{i}", [P, C, D]) for i in two]
        G = [sb(f"G{i}", [P, C, NQ]) for i in two]
        GT = [sb(f"GT{i}", [P, C, P]) for i in two]
        xq = [sb(f"xq{i}", [P, NQ]) for i in two]
        rt = [sb(f"rt{i}", [P, D]) for i in two]
        ob = [sb(f"ob{i}", [P, C, D]) for i in two]

        x_in = [sem(f"x_in{i}") for i in range(4)]
        c_in, wmod_in, w_at_in, wl_in, wh_in, wo_in = (sem("c_in"), sem("wmod_in"), sem("w_at_in"), sem("wl_in"),
                                                       sem("wh_in"), sem("wo_in"))
        col_in, bc_in, mod_out, mod_in = sem("col_in"), sem("bc_in"), sem("mod_out"), sem("mod_in")
        g_const, g_tab = sem("g_const"), sem("g_tab")
        st1_done, mv1_sums, mv1_parts, ve1_done, rs1_done, nm1_done = (
            sem("st1_done"), sem("mv1_sums"), sem("mv1_parts"), sem("ve1_done"), sem("rs1_done"), sem("nm1_done"))
        c_exp, c_den, c_act, cT_ps, cT_sb = sem("c_exp"), sem("c_den"), sem("c_act"), sem("cT_ps"), sem("cT_sb")
        col_ps, row_ps, col_sb, row_sb, gate_done, fix_done = (
            sem("col_ps"), sem("row_ps"), sem("col_sb"), sem("row_sb"), sem("gate_done"), sem("fix_done"))
        w_small, w_ps, w_tr, w_prod, v_scaled, w_hi, w_split = (
            sem("w_small"), sem("w_ps"), sem("w_tr"), sem("w_prod"), sem("v_scaled"), sem("w_hi"), sem("w_split"))
        a = {n: sem("a_" + n) for n in (
            "xl", "hp", "hT", "qkp", "vp", "qkT", "v", "Sp", "sm", "nmx", "p", "PTp", "PT", "Op", "ri",
            "ao", "x1", "st", "mv", "ve", "rs", "nm", "hn", "hm", "h2", "ss", "ssc", "rn", "s4", "S", "xh",
            "xhd0", "xhd1", "xp", "xhi", "xlo")}
        r = {n: sem("r_" + n) for n in (
            "Sd", "Sp", "rows", "smax", "m", "t", "e", "ln", "na", "tf", "sc", "top", "left", "w1", "w", "selp",
            "selT", "cum", "pp", "pos")}
        lt = {n: sem("l_" + n) for n in (
            "xt0", "xt1", "up", "vp", "hi", "lo", "v", "Sp", "mx", "p", "ri", "pn", "PTp", "PT", "Op", "oT", "outp", "fin", "x")}
        hv = {n: sem("h_" + n) for n in (
            "xt0", "xt1", "G", "xqp", "xq", "gtp", "gt", "tp", "thi", "tlo", "vp", "v", "Sp", "mx", "p", "ri", "pn",
            "PTp", "PT", "Op", "oT", "outp", "rt", "scp", "fin", "ob", "out0", "out1")}

        block = ctx.enter_context(nc.Block())

        CD_FIRST = 8 * (PAIRS - 1) - CD_ITERS
        TOP_FIRST = CD_FIRST + CD_ITERS + 2

        def b_par(k):
            return k // 4

        W_PIECES = ("wq light", "wk light", "even light", "odd light", "wq heavy", "even heavy", "odd heavy", "wv heavy")
        TRANSPOSED = (0, 1, 4)

        def evacuated(n):
            if n in TRANSPOSED:
                return w_tr, TRANSPOSED.index(n) + 1
            return w_prod, sum(i not in TRANSPOSED for i in range(n + 1))

        @block.sync
        def _(sp):
            for j in range(2):
                sp.dma_start(b_col[:, j:j + 1], b_attn[j * D:(j + 1) * D].rearrange("(p a) -> p a", a=1)).then_inc(col_in, 16)
            for i in range(4):
                sp.dma_start(X[:, 4 * i:4 * i + 4, :, :],
                             x[4 * i:4 * i + 4].rearrange("b (c p) d -> p b c d", p=P)).then_inc(x_in[i], 16)
            for dst, src in ((bv_bc[:, :], b_attn[2 * D:3 * D]), (gam_bc[:, 0, :], gamma_l), (gam_bc[:, 1, :], gamma_h),
                             (tok_bc[:, 0, :], q_tok), (tok_bc[:, 1, :], kv_tok)):
                sp.dma_start(dst, src.rearrange("(a d) -> a d", a=1).broadcast_to([P, D])).then_inc(bc_in, 16)
            sp.wait_ge(fix_done, 3)
            sp.dma_start(mod_rows_dram, mod_fix[:, :, :]).then_inc(mod_out, 16)
            sp.wait_ge(mod_out, 16)
            sp.dma_start(mod_bc[:, :, :, :].rearrange("p b j d -> p (b j d)"),
                         mod_rows_dram.rearrange("b j d -> (b j d)").rearrange("(a n) -> a n", a=1)
                         .broadcast_to([P, B * 4 * D])).then_inc(mod_in, 16)

            with sp.Fori(0, PAIRS) as p:
                for k in range(2):
                    sp.wait_ge(a["xh"], 4 * p + 2 * k + 2)
                    sp.dma_start(xh_dram[2 * p + k], xhs[k][:, :, :].rearrange("p c d -> p (c d)")).then_inc(a[f"xhd{k}"], 16)
            sp.wait_ge(a["xlo"], B)
            sp.wait_ge(w_split, 3)

            def load_light(p, k):
                b = 2 * p + k
                at_least(sp, lt["Sp"], 4 * (b - 1))
                sp.dma_start(xt[k][0][:, :].bitcast(F32), XT_hi[:, b, :].bitcast(F32)).then_inc(lt[f"xt{k}"], 16)
                sp.dma_start(xt[k][1][:, :].bitcast(F32), XT_lo[:, b, :].bitcast(F32)).then_inc(lt[f"xt{k}"], 16)

            for k in range(2):
                load_light(0, k)
            with sp.Fori(1, PAIRS) as p:
                for k in range(2):
                    load_light(p, k)

            sp.wait_ge(lt["Sp"], 4 * B)
            for k in range(2):
                sp.wait_ge(a[f"xhd{k}"], 16 * PAIRS)

            def load_heavy(p, k):
                b = 2 * p + k
                at_least(sp, hv["vp"], 2 * (b - 1))
                at_least(sp, hv["xqp"], b - 1)
                sp.dma_start(xt[k][0][:, :].bitcast(F32), XT_hi[:, b, :].bitcast(F32)).then_inc(hv[f"xt{k}"], 16)
                sp.dma_start(xt[k][1][:, :].bitcast(F32), XT_lo[:, b, :].bitcast(F32)).then_inc(hv[f"xt{k}"], 16)
                sp.dma_start(xh[k][:, :, :].rearrange("p c d -> p (c d)"), xh_dram[b]).then_inc(hv[f"xt{k}"], 16)

            def store(p, k):
                b = 2 * p + k
                sp.wait_ge(hv["ob"], b + 1)
                sp.dma_start(out[b].rearrange("(c p) d -> p c d", p=P), ob[k][:, :, :]).then_inc(hv[f"out{k}"], 16)

            for p in range(2):
                for k in range(2):
                    load_heavy(p, k)
            with sp.Fori(2, PAIRS) as p:
                for k in range(2):
                    load_heavy(p, k)
                    store(p - 2, k)
            for p in range(PAIRS - 2, PAIRS):
                for k in range(2):
                    store(p, k)
            for k in range(2):
                sp.wait_ge(hv[f"out{k}"], 16 * PAIRS)

        @block.gpsimd
        def _(pool):
            pool.memset(ident[:, :], 0.0).then_inc(g_const, 1)
            pool.memset(tri[:, :], 1.0).then_inc(g_const, 1)
            pool.memset(ones[:, :], 1.0).then_inc(g_const, 1)
            pool.memset(mask[:, :], 0.0).then_inc(g_const, 1)
            pool.memset(neg_half[:, :], -0.5).then_inc(g_const, 1)
            pool.iota(iota[:, :], [[1, P]], base=0, channel_multiplier=0,
                      allow_small_or_imprecise_dtypes=True).then_inc(g_const, 1)
            pool.memset(log_k[:, :], float(np.log(np.float32(K_KV)))).then_inc(g_const, 1)
            pool.wait_ge(g_const, 7)
            pool.affine_select(ident[:, :], ident[:, :], pattern=[[-1, P]], compare_op=ALU.not_equal, fill=1.0,
                               base=0, channel_multiplier=1).then_inc(g_tab, 1)
            pool.affine_select(tri[:, :], tri[:, :], pattern=[[1, P]], compare_op=ALU.is_ge, fill=0.0,
                               base=0, channel_multiplier=-1).then_inc(g_tab, 1)
            pool.affine_select(mask[:, 0:P], mask[:, 0:P], pattern=[[-1, P]], compare_op=ALU.is_ge, fill=MASKED,
                               base=0, channel_multiplier=1).then_inc(g_tab, 1)
            pool.affine_select(mask[:, 2 * P:3 * P], mask[:, 2 * P:3 * P], pattern=[[-1, P]], compare_op=ALU.is_ge,
                               fill=MASKED, base=0, channel_multiplier=1).then_inc(g_tab, 1)
            pool.memset(log_k[0:B, :], float(np.log(np.float32(K_Q)))).then_inc(g_tab, 1)

            for n, (lo, hi) in enumerate(((0, 4 * C), (4 * C, B * C))):
                pool.wait_ge(ve1_done, n + 1)
                pool.tensor_tensor(rs1[:, lo:hi], ve1[:, lo:hi], neg_half[:, lo:hi], ALU.pow).then_inc(rs1_done, 1)

            def residual(p, k):
                b = 2 * p + k
                pool.wait_ge(a["ao"], 2 * b + 2)
                pool.tensor_tensor(X[:, b], X[:, b], ao[k][:, :, :], ALU.add).then_inc(a["x1"], 1)

            def ln2_rstd(p, k):
                pool.wait_ge(a["ve"], 2 * p + k + 1)
                at_least(pool, a["hn"], 2 * (2 * p + k - 1))
                pool.tensor_tensor(rs2[k][:, :], ve2[k][:, :], neg_half[:, 0:C], ALU.pow).then_inc(a["rs"], 1)

            def modulate(p, k):
                b = 2 * p + k
                pool.wait_ge(a["hn"], 2 * b + 2)
                if isinstance(b, int) and b == 0:
                    pool.wait_ge(mod_in, 16)
                pool.tensor_tensor(hm[k][:, :, :], hn[k][:, :, :],
                                   mod_bc[:, b, 1:2, :].broadcast_to([P, C, D]), ALU.mult).then_inc(a["hm"], 1)
                pool.wait_ge(a["hm"], b + 1)
                at_least(pool, a["ss"], 2 * (b - 1))
                at_least(pool, a["xh"], 2 * (b - 1))
                pool.tensor_tensor(h2[k][:, :, :], hm[k][:, :, :],
                                   mod_bc[:, b, 2:3, :].broadcast_to([P, C, D]), ALU.add).then_inc(a["h2"], 1)

            def rms(p, k):
                pool.wait_ge(a["ssc"], 2 * p + k + 1)
                at_least(pool, a["xh"], 2 * (2 * p + k - 1))
                pool.tensor_tensor(rn[k][:, :], ssc[k][:, :], neg_half[:, 0:C], ALU.pow).then_inc(a["rn"], 1)

            run_stages(pool, [(4, residual), (5, modulate), (4, ln2_rstd), (6, rms)], 2, 5, PAIRS)

            pool.wait_ge(a["xlo"], B)
            def normalise(p, k):
                g = 8 * p + k
                pool.wait_ge(lt["ri"], g + 1)
                q = pr[k % 4][:, :].rearrange("p (h t) -> p h t", h=4)
                pool.tensor_tensor(q, q, rinv[k % 4][:, :, None].broadcast_to([P, 4, P]), ALU.mult)\
                    .then_inc(lt["pn"], 1)

            def add_light(p, k):
                if k % 2 == 0:
                    return
                b, w = 2 * p + k // 4, k % 4 // 2
                pool.wait_ge(lt["fin"], 2 * b + w + 1)
                pool.tensor_tensor(X[:, b, w, :], X[:, b, w, :], tmp[w][:, 0, :], ALU.add).then_inc(lt["x"], 1)

            run_stages(pool, [(5, normalise), (9, add_light)], 8, 3, PAIRS)

            def normalise_h(p, k):
                g = 8 * p + k
                pool.wait_ge(hv["ri"], g + 1)
                q = pr[k % 4][:, :].rearrange("p (h t) -> p h t", h=2)
                pool.tensor_tensor(q, q, rinv[k % 4][:, 0:2, None].broadcast_to([P, 2, N]), ALU.mult)\
                    .then_inc(hv["pn"], 1)

            def add_heavy(p, k):
                if k % 4 != 3:
                    return
                b = 2 * p + k // 4
                pool.wait_ge(hv["fin"], 2 * b + 2)
                at_least(pool, hv[f"out{b_par(k)}"], 16 * p)
                pool.tensor_tensor(ob[b_par(k)][:, :, :], X[:, b], tmp[b_par(k)][:, :, :], ALU.add)\
                    .then_inc(hv["ob"], 1)

            run_stages(pool, [(3, normalise_h), (11, add_heavy)], 8, 3, PAIRS)

        @block.scalar
        def _(act):
            act.preload_act_table_set("natural_log_exp_and_others")
            act.dma_start(c_sb[:, :], c).then_inc(c_in, 16)
            act.dma_start(wmod_sb[:, :], wmod).then_inc(wmod_in, 16)
            act.dma_start(w_at[:, :], w_attn).then_inc(w_at_in, 16)
            act.dma_start(gam_col[:, 0:1], gamma_l.rearrange("(p a) -> p a", a=1)).then_inc(col_in, 16)
            act.dma_start(gam_col[:, 1:2], gamma_h.rearrange("(p a) -> p a", a=1)).then_inc(col_in, 16)
            act.dma_start(wq_raw[:, 0, :], wq_l).then_inc(wl_in, 16)
            act.dma_start(wkv_raw[:, :], wkv_l).then_inc(wl_in, 16)
            act.dma_start(wq_raw[:, 1, :], wq_h).then_inc(wh_in, 16)
            kv_rows = wkv_h.rearrange("(q i t m) d -> i t m q d", i=2, t=2, m=DH)
            for i in range(2):
                act.dma_start(wk_hT[i * DH:(i + 1) * DH, :, :], kv_rows[i, 0]).then_inc(wh_in, 16)
                act.dma_start(wv_hT[i * DH:(i + 1) * DH, :, :], kv_rows[i, 1]).then_inc(wh_in, 16)
            act.dma_start(wo_l_sb[:, :, :], wo_l.rearrange("(q p) d -> p q d", p=P)).then_inc(wo_in, 16)
            act.dma_start(wo_h_sb[:, :, :], wo_h.rearrange("(q p) d -> p q d", p=P)).then_inc(wo_in, 16)

            act.wait_ge(c_in, 16)
            act.activation(c_e[:, :], c_sb[:, :], ACT.Exp, scale=-1.0).then_inc(c_exp, 1)

            act.wait_ge(w_small, 2)
            act.wait_ge(col_sb, 2)

            rs1_bc = rs1[:, :].rearrange("p (b c) -> p b c", c=C)
            nm1_bc = nm1[:, :].rearrange("p (b c) -> p b c", c=C)

            def ln1(p, k):
                b = 2 * p + k
                if isinstance(b, int):
                    act.wait_ge(nm1_done, 1 if b < 4 else 2)
                at_least(act, a["hp"], b - 1)
                for i in range(C):
                    act.activation(xl[k][:, i, :], X[:, b, i, :], ACT.Identity, bias=nm1_bc[:, b, i:i + 1],
                                   scale=rs1_bc[:, b, i:i + 1]).then_inc(a["xl"], 1)

            def h_evac(p, k):
                b = 2 * p + k
                act.wait_ge(a["hp"], b + 1)
                at_least(act, a["vp"], b - 1)
                act.activation(hT[k][:, :], ps[0][:, 0:N], ACT.Identity, bias=modT[:, 0, bass.ds(b, 1)],
                               scale=modT[:, 1, bass.ds(b, 1)]).then_inc(a["hT"], 1)

            def ln2(p, k):
                b = 2 * p + k
                act.wait_ge(a["nm"], b + 1)
                at_least(act, a["hm"], b - 1)
                for i in range(C):
                    act.activation(hn[k][:, i, :], X[:, b, i, :], ACT.Identity, bias=nm2[k][:, i:i + 1],
                                   scale=rs2[k][:, i:i + 1]).then_inc(a["hn"], 1)

            def w_evac(p, k):
                n = 2 * p + k - 1
                if isinstance(n, int) and n in TRANSPOSED:
                    act.wait_ge(w_ps, n + 1)
                    dst = (wqT[:, 0], wkT[:, :, :], wqT[:, 1])[TRANSPOSED.index(n)]
                    act.activation(dst, ps[7][:, :].rearrange("p (q d) -> p q d", q=4), ACT.Copy).then_inc(w_tr, 1)

            def qk_evac(p, k):
                b = 2 * p + k
                act.wait_ge(a["qkp"], b + 1)
                at_least(act, a["Sp"], b - 1)
                act.activation(qT[k][:, :], ps[2][:, 0:N], ACT.Identity, bias=bq_sc[:, :], scale=ATTN_SCALE)\
                    .then_inc(a["qkT"], 1)
                act.activation(kT[k][:, :], ps[2][:, N:2 * N], ACT.Identity, bias=b_col[:, 1:2]).then_inc(a["qkT"], 1)

            def exps_a(p, k):
                b = 2 * p + k
                act.wait_ge(a["nmx"], b + 1)
                at_least(act, a["PTp"], b - 1)
                at_least(act, a["ri"], b - 1)
                act.activation(pa[k][:, 0:P], sm[k][:, 0:P], ACT.Exp, bias=nmxa[k][:, 0:1],
                               accum_out=suma[k][:, 0:1]).then_inc(a["p"], 1)
                act.activation(pa[k][:, P:3 * P], sm[k][:, P:3 * P], ACT.Exp, bias=nmxa[k][:, 1:2],
                               accum_out=suma[k][:, 1:2]).then_inc(a["p"], 1)

            def pt_evac_a(p, k):
                b = 2 * p + k
                act.wait_ge(a["PTp"], b + 1)
                at_least(act, a["Op"], b - 1)
                act.activation(pta[k][:, :], ps[5][:, 0:3 * P], ACT.Copy).then_inc(a["PT"], 1)

            def squares(p, k):
                b = 2 * p + k
                act.wait_ge(a["h2"], b + 1)
                at_least(act, a["ssc"], b - 1)
                at_least(act, a["ss"], 2 * (b - 1))
                for i in range(C):
                    act.activation(sq[:, k, i, :], h2[k][:, i, :], ACT.Square,
                                   accum_out=ss[k][:, i:i + 1]).then_inc(a["ss"], 1)

            def xt_hi(p, k):
                b = 2 * p + k
                act.wait_ge(a["xp"], b + 1)
                act.activation(XT_hi[:, b, :], ps[1][:, 0:N], ACT.Copy).then_inc(a["xhi"], 1)

            run_stages(act, [(2, qk_evac), (1, h_evac), (6, squares), (3, exps_a), (5, ln2), (0, ln1), (3, pt_evac_a),
                             (7, xt_hi)], 2, 5, PAIRS, extra=w_evac)

            act.wait_ge(a["xlo"], B)
            def cd_sums(n):
                act.wait_ge(r["t"], n + 1)
                at_least(act, r["ln"], n)
                act.activation(cd_e[:, :], cd_t[:, :], ACT.Exp, accum_out=cd_sum[:, :]).then_inc(r["e"], 1)
                act.wait_ge(r["e"], n + 1)
                act.activation(cd_ln[:, :], cd_sum[:, :], ACT.Ln).then_inc(r["ln"], 1)

            def u_hi(p, k):
                b, j = 2 * p + k // 4, k % 4
                act.wait_ge(lt["up"], 4 * b + j + 1)
                act.activation(U[b_par(k)][0][:, 2 * j:2 * j + 2, :], ps[j == 1][:, :].rearrange("p (h t) -> p h t", h=2),
                               ACT.Copy).then_inc(lt["hi"], 1)

            def v_evac_l(p, k):
                b, w = 2 * p + k // 4, k % 4 - 2
                if w < 0:
                    return
                act.wait_ge(lt["vp"], 2 * b + w + 1)
                at_least(act, lt["Op"], 4 * (b - 2) + 2 * (w + 1))
                act.activation(V[b_par(k)][:, w, :], ps[1][:, :], ACT.Copy).then_inc(lt["v"], 1)

            def o_evac(p, k):
                g, b, j = 8 * p + k, 2 * p + k // 4, k % 4
                w, half = j // 2, j % 2
                act.wait_ge(lt["Op"], g + 1)
                at_least(act, lt["outp"], 2 * b + w - 1)
                act.activation(oT[w][:, 2 * half:2 * half + 2, :],
                               ps[6][:, 0:2 * P].rearrange("p (q t) -> p q t", q=2), ACT.Copy).then_inc(lt["oT"], 1)

            def exps(p, k):
                g = 8 * p + k
                act.wait_ge(lt["mx"], g + 1)
                at_least(act, lt["PTp"], g - 3)
                for i in range(4):
                    act.activation(pr[k % 4][:, i * P:(i + 1) * P], ps[2 + k % 2][:, i * P:(i + 1) * P], ACT.Exp,
                                   bias=nmx[k % 4][:, i:i + 1],
                                   accum_out=sums[k % 4][:, i:i + 1]).then_inc(lt["p"], 1)

            def cd_act(p, k):
                u = 8 * p + k
                if not isinstance(p, int) or CD_FIRST <= u < CD_FIRST + CD_ITERS:
                    cd_sums(u - CD_FIRST)
                elif u == CD_FIRST + CD_ITERS + 1:
                    act.wait_ge(r["tf"], 1)
                    act.activation(score[:, :], cd_t[:, :], ACT.Exp).then_inc(r["sc"], 1)

            run_stages(act, [(7, o_evac), (1, v_evac_l), (0, u_hi), (0, cd_act), (3, exps)], 8, 3, PAIRS - 1)

            def xq_evac(p, k):
                if k % 4:
                    return
                b = 2 * p + k // 4
                act.wait_ge(hv["xqp"], b + 1)
                act.activation(xq[b_par(k)][:, :], ps[7][:, 0:NQ], ACT.Copy).then_inc(hv["xq"], 1)

            def gt_evac(p, k):
                if k % 4:
                    return
                b = 2 * p + k // 4
                act.wait_ge(hv["gtp"], b + 1)
                act.activation(GT[b_par(k)][:, :, :], ps[7][:, P:3 * P].rearrange("p (c t) -> p c t", c=C),
                               ACT.Copy).then_inc(hv["gt"], 1)

            def t_hi(p, k):
                g, j = 8 * p + k, k % 4
                act.wait_ge(hv["tp"], g + 1)
                act.activation(U[b_par(k)][0][:, 2 * j:2 * j + 2, 0:NQ],
                               ps[0][:, 0:2 * NQ].rearrange("p (h t) -> p h t", h=2), ACT.Copy).then_inc(hv["thi"], 1)

            def exps_h(p, k):
                g = 8 * p + k
                act.wait_ge(hv["mx"], g + 1)
                at_least(act, hv["PTp"], g - 3)
                for i in range(2):
                    act.activation(pr[k % 4][:, i * N:(i + 1) * N], ps[2 + k % 2][:, i * N:(i + 1) * N], ACT.Exp,
                                   bias=nmx[k % 4][:, i:i + 1],
                                   accum_out=sums[k % 4][:, i:i + 1]).then_inc(hv["p"], 1)

            def rt_evac(p, k):
                if k % 4 != 3:
                    return
                b = 2 * p + k // 4
                act.wait_ge(hv["outp"], b + 1)
                act.activation(rt[b_par(k)][:, :], ps[7][:, 0:D], ACT.Copy).then_inc(hv["rt"], 1)

            def pt_evac_h(p, k):
                g = 8 * p + k
                act.wait_ge(hv["PTp"], g + 1)
                at_least(act, hv["Op"], g - 1)
                act.activation(pt[k % 2][:, :], ps[4 + k % 2][:, :], ACT.Copy).then_inc(hv["PT"], 1)

            act.wait_ge(lt["Op"], 8 * PAIRS)
            act.wait_ge(lt["PT"], 8 * PAIRS)
            run_stages(act, [(0, xq_evac), (10, rt_evac), (5, pt_evac_h), (0, t_hi), (7, gt_evac), (2, exps_h)],
                       8, 3, PAIRS)


        @block.tensor
        def _(pe):
            def triple(out, weights, moving, start=True, stop=True):
                pe.matmul(out, weights[1], moving[0], start=start, stop=False)
                pe.matmul(out, weights[0], moving[1], start=False, stop=False)
                return pe.matmul(out, weights[0], moving[0], start=False, stop=stop)

            pe.wait_ge(g_tab, 1)
            pe.wait_ge(c_act, 1)
            pe.transpose(ps[4][:, 0:B], c_s[:, :], ident[0:B, 0:B]).then_inc(cT_ps, 1)
            pe.wait_ge(cT_sb, 1)
            pe.wait_ge(wmod_in, 16)
            for j in range(2):
                mm = pe.matmul(ps[7][:, j * B:(j + 1) * B], wmod_sb[:, j * D:(j + 1) * D], cT[:, :],
                               start=True, stop=True)
            mm.then_inc(col_ps, 1)
            pe.matmul(ps[5][0:B, :], cT[:, :], wmod_sb[:, 2 * D:6 * D], start=True, stop=True).then_inc(row_ps, 1)
            pe.wait_ge(w_at_in, 16)

            def w_piece(p, k):
                n = 2 * p + k
                if not isinstance(n, int) or n >= len(W_PIECES):
                    return
                if n == 0:
                    pe.wait_ge(col_sb, 2)
                    pe.wait_ge(wl_in, 32)
                else:
                    pe.wait_ge(*evacuated(n - 1))
                if n == 4:
                    pe.wait_ge(wh_in, 80)
                what, light = W_PIECES[n].split()[0], "light" in W_PIECES[n]
                for q in range(4):
                    o = ps[7][:, q * P:(q + 1) * P]
                    if what == "wv":
                        mm = pe.transpose(o, wv_hT[:, q, :], ident[:, :])
                    elif what in ("wq", "wk"):
                        src = wkv_raw[:, 0:HID] if what == "wk" else wq_raw[:, 0 if light else 1, :]
                        mm = pe.transpose(o, src[:, q * P:(q + 1) * P], ident[:, :])
                    else:
                        r0 = DH * (what == "odd")
                        if light:
                            mm = pe.matmul(o, wkT[r0:r0 + DH, q, :], wqT[r0:r0 + DH, 0, q, :], start=True, stop=True)
                        else:
                            mm = pe.matmul(o, wqT[r0:r0 + DH, 1, q, :], wk_hT[r0:r0 + DH, q, :], start=True, stop=True)
                mm.then_inc(w_ps, 1)

            def h_transpose(p, k):
                b = 2 * p + k
                pe.wait_ge(a["xl"], 2 * b + 2)
                at_least(pe, a["hT"], b)
                for i in range(C):
                    mm = pe.transpose(ps[0][:, i * P:(i + 1) * P], xl[k][:, i, :], ident[:, :])
                mm.then_inc(a["hp"], 1)

            def query_key(p, k):
                b = 2 * p + k
                pe.wait_ge(a["hT"], b + 1)
                at_least(pe, a["qkT"], 2 * b)
                pe.matmul(ps[2][:, 0:N], w_at[:, 0:D], hT[k][:, :], start=True, stop=True)
                pe.matmul(ps[2][:, N:2 * N], w_at[:, D:2 * D], hT[k][:, :], start=True, stop=True).then_inc(a["qkp"], 1)

            def value_a(p, k):
                b = 2 * p + k
                at_least(pe, a["v"], b)
                for i in range(C):
                    mm = pe.matmul(ps[3][:, i * P:(i + 1) * P], hT[k][:, i * P:(i + 1) * P], w_at[:, 2 * D:3 * D],
                                   start=True, stop=True)
                mm.then_inc(a["vp"], 1)

            def scores_a(p, k):
                b = 2 * p + k
                pe.wait_ge(a["qkT"], 2 * b + 2)
                at_least(pe, a["sm"], 2 * b)
                pe.matmul(ps[4][:, 0:P], qT[k][:, 0:P], kT[k][:, 0:P], start=True, stop=True)
                pe.matmul(ps[4][:, P:3 * P], qT[k][:, P:2 * P], kT[k][:, :], start=True, stop=True).then_inc(a["Sp"], 1)

            def p_transpose_a(p, k):
                b = 2 * p + k
                pe.wait_ge(a["p"], 2 * b + 2)
                at_least(pe, a["PT"], b)
                for i in range(3):
                    mm = pe.transpose(ps[5][:, i * P:(i + 1) * P], pa[k][:, i * P:(i + 1) * P], ident[:, :])
                mm.then_inc(a["PTp"], 1)

            def values_a(p, k):
                b = 2 * p + k
                pe.wait_ge(a["PT"], b + 1)
                pe.wait_ge(a["v"], b + 1)
                at_least(pe, a["ao"], 2 * b)
                pe.matmul(ps[6][:, 0:P], pta[k][:, 0:P], va[k][:, 0, :], start=True, stop=True)
                pe.matmul(ps[6][:, P:2 * P], pta[k][:, P:2 * P], va[k][:, 0, :], start=True, stop=False)
                pe.matmul(ps[6][:, P:2 * P], pta[k][:, 2 * P:3 * P], va[k][:, 1, :], start=False, stop=True)\
                    .then_inc(a["Op"], 1)

            def x_transpose(p, k):
                b = 2 * p + k
                pe.wait_ge(a["xh"], 2 * b + 2)
                at_least(pe, a["xlo"], b)
                for i in range(C):
                    mm = pe.transpose(ps[1][:, i * P:(i + 1) * P], xhs[k][:, i, :], ident[:, :])
                mm.then_inc(a["xp"], 1)

            run_stages(pe, [(0, h_transpose), (2, value_a), (3, values_a), (1, scores_a), (0, query_key), (6, x_transpose),
                            (2, p_transpose_a)], 2, 5, PAIRS, extra=w_piece)

            pe.wait_ge(r["Sd"], 2)
            for i in range(C):
                mm = pe.transpose(ps[7][0:R, i * P:(i + 1) * P], S_dense[:, i, :], ident[:, :])
            mm.then_inc(r["Sp"], 1)
            pe.wait_ge(r["rows"], 1)
            pe.wait_ge(a["xlo"], B)
            pe.wait_ge(a["ao"], 2 * B)
            pe.wait_ge(w_split, 3)
            pe.wait_ge(wo_in, 32)

            def project(p, k):
                b, j = 2 * p + k // 4, k % 4
                if j == 1:
                    at_least(pe, lt["v"], 2 * b)
                else:
                    at_least(pe, lt["lo"], 4 * b + (0, None, 1, 3)[j])
                for i in range(2):
                    mm = triple(ps[j == 1][:, i * N:(i + 1) * N], [u[:, 2 * j + i, :] for u in U_w],
                                (XT_hi[:, b, :], XT_lo[:, b, :]))
                mm.then_inc(lt["up"], 1)

            def project_v(p, k):
                b, w, par = 2 * p + k // 4, k % 4 - 2, b_par(k)
                if w < 0:
                    return
                if w == 0:
                    pe.wait_ge(lt["lo"], 4 * b + 2)
                else:
                    pe.wait_ge(lt["v"], 2 * b + 1)
                pe.wait_ge(lt[f"xt{par}"], 32 * (p + 1))
                triple(ps[1][:, :], [t[:, w * P:(w + 1) * P] for t in xt[par]],
                       [v[:, :] for v in V_w]).then_inc(lt["vp"], 1)

            def scores(p, k):
                g, b, j, par = 8 * p + k, 2 * p + k // 4, k % 4, b_par(k)
                w, half = j // 2, j % 2
                pe.wait_ge(lt["lo"], 4 * b + (2 if j == 0 else 4))
                at_least(pe, lt["p"], 4 * (g - 1))
                triple(ps[2 + k % 2][:, :].rearrange("p (h t) -> p h t", h=4),
                       [t[:, w * P:(w + 1) * P] for t in xt[par]],
                       [u[:, 4 * half:4 * half + 4, w * P:(w + 1) * P] for u in U[par]]).then_inc(lt["Sp"], 1)

            def p_transpose(p, k):
                g = 8 * p + k
                pe.wait_ge(lt["pn"], g + 1)
                at_least(pe, lt["PT"], g - 1)
                for i in range(4):
                    mm = pe.transpose(ps[4 + k % 2][:, i * P:(i + 1) * P], pr[k % 4][:, i * P:(i + 1) * P], ident[:, :])
                mm.then_inc(lt["PTp"], 1)

            def values(p, k):
                g, b, j, par = 8 * p + k, 2 * p + k // 4, k % 4, b_par(k)
                w, half = j // 2, j % 2
                pe.wait_ge(lt["PT"], g + 1)
                pe.wait_ge(lt["v"], 2 * b + w + 1)
                at_least(pe, lt["oT"], g)
                for q in range(2):
                    for i in range(2):
                        h = 4 * half + 2 * q + i
                        mm = pe.matmul(ps[6][i * DH:(i + 1) * DH, q * P:(q + 1) * P],
                                       V[par][:, w, h * DH:(h + 1) * DH],
                                       pt[k % 2][:, (2 * q + i) * P:(2 * q + i + 1) * P], start=True, stop=True)
                mm.then_inc(lt["Op"], 1)

            def out_light(p, k):
                if k % 2 == 0:
                    return
                g, b, w = 8 * p + k, 2 * p + k // 4, k % 4 // 2
                pe.wait_ge(lt["oT"], g + 1)
                at_least(pe, lt["fin"], 2 * b + w)
                for q in range(4):
                    mm = pe.matmul(ps[7][:, 0:D], oT[w][:, q, :], wo_l_sb[:, q, :], start=(q == 0), stop=(q == 3))
                mm.then_inc(lt["outp"], 1)

            run_stages(pe, [(3, scores), (0, project), (8, out_light), (5, p_transpose), (6, values), (0, project_v)],
                       8, 3, PAIRS - 1)

            pe.wait_ge(r["w"], 2)
            pe.wait_ge(lt["fin"], 2 * B)
            for n in range(2):
                for i in range(C):
                    mm = pe.transpose(ps[7][:, (n * C + i) * R:(n * C + i + 1) * R], wsel[:, n, i * P:(i + 1) * P],
                                      ident[0:R, 0:R])
            mm.then_inc(r["selp"], 1)
            pe.wait_ge(r["selT"], 1)
            pe.matmul(ps[7][:, 0:B], tri[:, :], selT[:, 1, 0, 0:B], start=True, stop=True)
            pe.matmul(ps[7][:, B:2 * B], tri[:, :], selT[:, 1, 1, 0:B], start=True, stop=False)
            pe.matmul(ps[7][:, B:2 * B], ones[:, :], selT[:, 1, 0, 0:B], start=False, stop=True).then_inc(r["cum"], 1)
            pe.wait_ge(r["pp"], 1)
            pe.wait_ge(lt["lo"], 4 * B)
            pe.wait_ge(lt["v"], 2 * B)
            pe.wait_ge(lt["p"], 32 * PAIRS)
            pe.wait_ge(lt["PT"], 8 * PAIRS)
            pe.wait_ge(lt["oT"], 8 * PAIRS)

            def gather(p, k):
                if k % 4:
                    return
                b, par = 2 * p + k // 4, b_par(k)
                pe.wait_ge(hv["G"], 2 * b + 2)
                pe.wait_ge(hv[f"xt{par}"], 48 * (p + 1))
                at_least(pe, hv["gt"], b - 1)
                for i in range(C):
                    mm = pe.matmul(ps[7][:, 0:NQ], xh[par][:, i, :], G[par][:, i, :], start=(i == 0), stop=(i == C - 1))
                mm.then_inc(hv["xqp"], 1)

            def g_transpose(p, k):
                if k % 4:
                    return
                b, par = 2 * p + k // 4, b_par(k)
                at_least(pe, hv["fin"], 2 * (b - 1))
                for i in range(C):
                    mm = pe.transpose(ps[7][:, P + i * P:P + (i + 1) * P], G[par][:, i, :], ident[:, :])
                mm.then_inc(hv["gtp"], 1)

            def project_h(p, k):
                g, b, j, par = 8 * p + k, 2 * p + k // 4, k % 4, b_par(k)
                pe.wait_ge(hv["xq"], b + 1)
                at_least(pe, hv["tlo"], g)
                for i in range(2):
                    mm = pe.matmul(ps[0][:, i * NQ:(i + 1) * NQ], T_w[:, 2 * j + i, :], xq[par][:, :],
                                   start=True, stop=True)
                mm.then_inc(hv["tp"], 1)

            def project_vh(p, k):
                b, w, par = 2 * p + k // 4, k % 4 // 2, b_par(k)
                if k % 2 == 0:
                    return
                at_least(pe, hv["v"], 2 * b + w)
                triple(ps[1][:, :], [t[:, w * P:(w + 1) * P] for t in xt[par]],
                       [v[:, :] for v in VH_w]).then_inc(hv["vp"], 1)

            def scores_h(p, k):
                g, b, j, par = 8 * p + k, 2 * p + k // 4, k % 4, b_par(k)
                pe.wait_ge(hv["tlo"], g + 1)
                at_least(pe, hv["p"], 2 * (g - 1))
                for i in range(2):
                    mm = triple(ps[2 + k % 2][:, i * N:(i + 1) * N], [u[:, 2 * j + i, 0:NQ] for u in U[par]],
                                (XT_hi[:, b, :], XT_lo[:, b, :]))
                mm.then_inc(hv["Sp"], 1)

            def p_transpose_h(p, k):
                g = 8 * p + k
                pe.wait_ge(hv["pn"], g + 1)
                at_least(pe, hv["PT"], g - 1)
                for i in range(4):
                    mm = pe.transpose(ps[4 + k % 2][:, i * P:(i + 1) * P], pr[k % 4][:, i * P:(i + 1) * P], ident[:, :])
                mm.then_inc(hv["PTp"], 1)

            def values_h(p, k):
                g, b, j, par = 8 * p + k, 2 * p + k // 4, k % 4, b_par(k)
                pe.wait_ge(hv["PT"], g + 1)
                pe.wait_ge(hv["v"], 2 * b + 2)
                at_least(pe, hv["oT"], g)
                for w in range(C):
                    for i in range(2):
                        h = 2 * j + i
                        mm = pe.matmul(ps[6][i * DH:(i + 1) * DH, 0:NQ], V[par][:, w, h * DH:(h + 1) * DH],
                                       pt[k % 2][:, (2 * i + w) * P:(2 * i + w + 1) * P],
                                       start=(w == 0), stop=(w == C - 1))
                mm.then_inc(hv["Op"], 1)

            def out_heavy(p, k):
                if k % 4 != 3:
                    return
                g, b, par = 8 * p + k, 2 * p + k // 4, b_par(k)
                pe.wait_ge(hv["oT"], g + 1)
                pe.wait_ge(hv["xq"], min(b + 4, B) if isinstance(b, int) else b + 4)
                if isinstance(b, int) and b + 4 > B:
                    pe.wait_ge(hv["gt"], min(b + 2, B))
                    pe.wait_ge(hv["fin"], 2 * b)
                for q in range(4):
                    mm = pe.matmul(ps[7][:, 0:D], oT[par][:, q, :], wo_h_sb[:, q, :], start=(q == 0), stop=(q == 3))
                mm.then_inc(hv["outp"], 1)

            def scatter(p, k):
                if k % 4 != 3:
                    return
                b, par = 2 * p + k // 4, b_par(k)
                pe.wait_ge(hv["rt"], b + 1)
                for i in range(C):
                    mm = pe.matmul(ps[7][:, P + i * P:P + (i + 1) * P], GT[par][:, i, :], rt[par][:, :],
                                   start=True, stop=True)
                mm.then_inc(hv["scp"], 1)

            run_stages(pe, [(6, values_h), (0, gather), (0, project_vh), (7, g_transpose), (4, p_transpose_h),
                            (0, project_h), (9, out_heavy), (10, scatter), (1, scores_h)], 8, 3, PAIRS)

        @block.vector
        def _(dve):
            def mean_var(st, t, mean, ve, three, six, seven, base=0):
                (me, ce), (mo, co) = (st[..., 1], st[..., 2]), (st[..., 4], st[..., 5])
                dve.tensor_tensor(t[0], me, mo, ALU.add).then_inc(three, 1)
                dve.tensor_tensor(t[1], me, mo, ALU.subtract).then_inc(three, 1)
                dve.tensor_tensor(t[2], ce, co, ALU.add).then_inc(three, 1)
                dve.wait_ge(three, 3 * base + 3)
                dve.tensor_scalar(mean, t[0], 0.5, None, ALU.mult).then_inc(six, 1)
                dve.scalar_tensor_tensor(t[3], t[1], 0.25, t[1], ALU.mult, ALU.mult).then_inc(six, 1)
                dve.tensor_scalar(t[4], t[2], 1.0 / D, LN_EPS, ALU.mult, ALU.add).then_inc(six, 1)
                dve.wait_ge(six, 3 * base + 3)
                dve.tensor_tensor(ve, t[3], t[4], ALU.add).then_inc(seven, 1)

            def stats1(i):
                dve.wait_ge(x_in[i], 16)
                for b in range(4 * i, 4 * i + 4):
                    for q in range(C):
                        dve.bn_stats(st1[:, b, q, :], X[:, b, q, :]).then_inc(st1_done, 1)

            def mean_var1(n, lo, hi):
                dve.wait_ge(st1_done, C * hi)
                mean_var(st1[:, lo:hi, :, :].rearrange("p b c s -> p (b c) s"), [t1[:, i, C * lo:C * hi] for i in range(5)],
                         mean1[:, C * lo:C * hi], ve1[:, C * lo:C * hi], mv1_sums, mv1_parts, ve1_done, n)

            def neg_mean_rstd(n, lo, hi):
                dve.wait_ge(rs1_done, n + 1)
                dve.scalar_tensor_tensor(nm1[:, C * lo:C * hi], mean1[:, C * lo:C * hi], -1.0, rs1[:, C * lo:C * hi],
                                         ALU.mult, ALU.mult).then_inc(nm1_done, 1)

            dve.wait_ge(c_exp, 1)
            dve.tensor_scalar(c_d[:, :], c_e[:, :], 1.0, None, ALU.add).then_inc(c_den, 1)
            dve.wait_ge(c_den, 1)
            dve.reciprocal(c_r[:, :], c_d[:, :]).then_inc(c_den, 1)
            dve.wait_ge(c_den, 2)
            dve.wait_ge(c_in, 16)
            dve.tensor_tensor(c_s[:, :], c_sb[:, :], c_r[:, :], ALU.mult).then_inc(c_act, 1)
            stats1(0)
            mean_var1(0, 0, 4)
            dve.wait_ge(cT_ps, 1)
            dve.tensor_copy(cT[:, :], ps[4][:, 0:B]).then_inc(cT_sb, 1)
            dve.wait_ge(col_in, 64)
            dve.tensor_scalar(gam_sc[:, :], gam_col[:, :], HEAD_SCALE, None, ALU.mult).then_inc(w_small, 1)
            dve.tensor_scalar(bq_sc[:, :], b_col[:, 0:1], ATTN_SCALE, None, ALU.mult).then_inc(w_small, 1)
            stats1(1)
            neg_mean_rstd(0, 0, 4)
            dve.wait_ge(col_ps, 1)
            dve.tensor_copy(modT[:, 0, :], ps[7][:, 0:B]).then_inc(col_sb, 1)
            dve.tensor_scalar(modT[:, 1, :], ps[7][:, B:2 * B], 1.0, None, ALU.add).then_inc(col_sb, 1)
            dve.wait_ge(row_ps, 1)
            dve.tensor_copy(mod_raw[:, :, :], ps[5][0:B, :].rearrange("b (j d) -> b j d", j=4)).then_inc(row_sb, 1)
            stats1(2)
            dve.wait_ge(row_sb, 1)
            gates = mod_raw[:, 0:4:3, :]
            dve.tensor_scalar(gate_s[:, :, :], gates, 0.0, 2.0, ALU.is_ge, ALU.mult).then_inc(gate_done, 1)
            dve.scalar_tensor_tensor(gate_a[:, :, :], gates, -1.0, gates, ALU.mult, ALU.max).then_inc(gate_done, 1)
            dve.tensor_copy(mod_fix[:, 2, :], mod_raw[:, 1, :]).then_inc(fix_done, 1)
            dve.tensor_scalar(mod_fix[:, 1, :], mod_raw[:, 2, :], 1.0, None, ALU.add).then_inc(fix_done, 1)
            dve.wait_ge(gate_done, 2)
            dve.tensor_scalar(gate_m[:, :, :], gate_a[:, :, :], 0.25, None, ALU.max).then_inc(gate_done, 1)
            dve.wait_ge(gate_done, 3)
            dve.scalar_tensor_tensor(mod_fix[:, 0:4:3, :], gate_s[:, :, :], -1.0, gate_m[:, :, :], ALU.add, ALU.mult)\
                .then_inc(fix_done, 1)
            stats1(3)
            mean_var1(1, 4, B)
            dve.wait_ge(wl_in, 32)
            dve.tensor_scalar(v_big[:, 0, :], wkv_raw[:, HID:2 * HID], gam_col[:, 0:1], None, ALU.mult).then_inc(v_scaled, 1)
            dve.wait_ge(v_scaled, 1)
            dve.tensor_copy(V_w[0][:, :], v_big[:, 0, :]).then_inc(w_hi, 1)
            dve.wait_ge(w_hi, 1)
            dve.tensor_tensor(V_w[1][:, :], v_big[:, 0, :], V_w[0][:, :].bitcast(F32), ALU.subtract).then_inc(w_split, 1)
            neg_mean_rstd(1, 4, B)
            dve.memset(cd_t[:, :], 0.0).then_inc(r["t"], 1)
            dve.memset(cd_m[:, :], 0.0).then_inc(r["m"], 1)
            dve.wait_ge(bc_in, 16 * 5)
            dve.wait_ge(g_tab, 5)

            def w_prods(p, k):
                n = 2 * p + k - 1
                if not isinstance(n, int) or not 0 <= n <= len(W_PIECES):
                    return
                if n == 4:
                    dve.wait_ge(w_prod, 2)
                    dve.tensor_copy(U_w[0][:, :, :], big[:, :, :]).then_inc(w_hi, 1)
                    dve.wait_ge(w_hi, 2)
                    dve.tensor_tensor(U_w[1][:, :, :], big[:, :, :], U_w[0][:, :, :].bitcast(F32), ALU.subtract)\
                        .then_inc(w_split, 1)
                elif n == 8:
                    dve.wait_ge(w_prod, 5)
                    dve.tensor_copy(VH_w[0][:, :], v_big[:, 1, :]).then_inc(w_hi, 1)
                    dve.wait_ge(w_hi, 3)
                    dve.tensor_tensor(VH_w[1][:, :], v_big[:, 1, :], VH_w[0][:, :].bitcast(F32), ALU.subtract)\
                        .then_inc(w_split, 1)
                elif n not in TRANSPOSED:
                    dve.wait_ge(w_ps, n + 1)
                    if n == 7:
                        dve.tensor_scalar(v_big[:, 1, :], ps[7][:, :], gam_col[:, 1:2], None, ALU.mult).then_inc(w_prod, 1)
                    else:
                        dst, j = (big, 0) if n < 4 else (T_w, 1)
                        i = int("odd" in W_PIECES[n])
                        dve.scalar_tensor_tensor(dst[:, i:HEADS:2, :], ps[7][:, :].rearrange("p (h d) -> p h d", h=4),
                                                 gam_sc[:, j:j + 1], gam_bc[:, j:j + 1, :].broadcast_to([P, 4, D]),
                                                 ALU.mult, ALU.mult).then_inc(w_prod, 1)

            def v_evac(p, k):
                b = 2 * p + k
                dve.wait_ge(a["vp"], b + 1)
                at_least(dve, a["Op"], b - 1)
                dve.tensor_tensor(va[k][:, :, :], ps[3][:, 0:N].rearrange("p (c d) -> p c d", c=C),
                                  bv_bc[:, None, :].broadcast_to([P, C, D]), ALU.add).then_inc(a["v"], 1)

            def scores_ready(p, k):
                dve.wait_ge(a["Sp"], 2 * p + k + 1)

            def stats_ready(p, k):
                dve.wait_ge(a["st"], 2 * (2 * p + k) + 2)

            def recip(p, k):
                b = 2 * p + k
                dve.wait_ge(a["p"], 2 * b + 2)
                dve.reciprocal(rinva[k][:, :], suma[k][:, :]).then_inc(a["ri"], 1)

            def mask_max(p, k):
                for i, (s, e) in enumerate(((0, P), (P, 3 * P))):
                    dve.tensor_tensor_reduce(sm[k][:, s:e], ps[4][:, s:e], mask[:, s:e], 1.0, -3.0e38, ALU.add, ALU.max,
                                             mxa[k][:, i:i + 1]).then_inc(a["sm"], 1)

            def neg_max_a(p, k):
                b = 2 * p + k
                dve.wait_ge(a["sm"], 2 * b + 2)
                at_least(dve, a["p"], 2 * (b - 1))
                dve.tensor_scalar(nmxa[k][:, :], mxa[k][:, :], -1.0, None, ALU.mult).then_inc(a["nmx"], 1)

            def attn_out(p, k):
                b = 2 * p + k
                dve.wait_ge(a["ri"], b + 1)
                dve.wait_ge(a["Op"], b + 1)
                if isinstance(b, int) and b == 0:
                    dve.wait_ge(mod_in, 16)
                at_least(dve, a["x1"], b - 1)
                for i in range(C):
                    dve.scalar_tensor_tensor(ao[k][:, i, :], ps[6][:, i * P:(i + 1) * P], rinva[k][:, i:i + 1],
                                             mod_bc[:, b, 0, :], ALU.mult, ALU.mult).then_inc(a["ao"], 1)

            def ln2_stats(p, k):
                b = 2 * p + k
                dve.wait_ge(a["x1"], b + 1)
                for i in range(C):
                    dve.bn_stats(st2[k][:, i, :], X[:, b, i, :]).then_inc(a["st"], 1)

            def aggregate(p, k):
                for i in range(C):
                    dve.bn_aggr(mv2[k][:, i, :], st2[k][:, i, :]).then_inc(a["mv"], 1)

            def var_eps(p, k):
                b = 2 * p + k
                dve.wait_ge(a["mv"], 2 * b + 2)
                at_least(dve, a["rs"], b - 1)
                dve.tensor_scalar(ve2[k][:, :], mv2[k][:, :, 1], LN_EPS, None, ALU.add).then_inc(a["ve"], 1)

            def neg_mean_rstd2(p, k):
                b = 2 * p + k
                dve.wait_ge(a["rs"], b + 1)
                at_least(dve, a["hn"], 2 * (b - 1))
                dve.scalar_tensor_tensor(nm2[k][:, :], mv2[k][:, :, 0], -1.0, rs2[k][:, :], ALU.mult, ALU.mult)\
                    .then_inc(a["nm"], 1)

            def route(p, k):
                b = 2 * p + k
                dve.wait_ge(a["h2"], b + 1)
                for i in range(C):
                    for t in range(2):
                        dve.tensor_tensor_reduce(rprod[:, k, 2 * i + t, :], h2[k][:, i, :], tok_bc[:, t, :], 1.0, 0.0,
                                                 ALU.mult, ALU.add, s4[k][:, 2 * i + t:2 * i + t + 1])\
                            .then_inc(a["s4"], 1)

            def keep_scores(p, k):
                b = 2 * p + k
                dve.wait_ge(a["ss"], 2 * b + 2)
                at_least(dve, a["rn"], b - 1)
                dve.tensor_scalar(ssc[k][:, :], ss[k][:, :], 1e-24, None, ALU.max).then_inc(a["ssc"], 1)
                dve.wait_ge(a["s4"], 4 * b + 4)
                dve.tensor_copy(S_all[:, b, :, :], s4[k][:, :].rearrange("p (c t) -> p c t", c=C)).then_inc(a["S"], 1)

            def xhat(p, k):
                b = 2 * p + k
                dve.wait_ge(a["rn"], b + 1)
                at_least(dve, a["xp"], b - 1)
                at_least(dve, a[f"xhd{k}"], 16 * p)
                for i in range(C):
                    dve.tensor_scalar(xhs[k][:, i, :], h2[k][:, i, :], rn[k][:, i:i + 1], float(D) ** 0.5,
                                      ALU.mult, ALU.mult).then_inc(a["xh"], 1)

            def xt_lo(p, k):
                b = 2 * p + k
                dve.wait_ge(a["xhi"], b + 1)
                dve.tensor_tensor(XT_lo[:, b, :], ps[1][:, 0:N], XT_hi[:, b, :].bitcast(F32), ALU.subtract)\
                    .then_inc(a["xlo"], 1)

            run_stages(dve, [(2, scores_ready), (4, stats_ready), (3, recip), (2, mask_max), (4, aggregate), (4, var_eps),
                             (2, neg_max_a), (5, route), (3, attn_out), (4, neg_mean_rstd2), (5, keep_scores), (6, xhat),
                             (7, xt_lo), (2, v_evac), (3, ln2_stats)], 2, 5, PAIRS, extra=w_prods)

            dve.wait_ge(a["S"], B)
            dve.wait_ge(a["xlo"], B)
            for t in range(2):
                dve.tensor_copy(S_dense[:, :, t * B:(t + 1) * B], S_all[:, :, :, t].rearrange("p b c -> p c b"))\
                    .then_inc(r["Sd"], 1)
            dve.wait_ge(r["Sp"], 1)
            dve.tensor_copy(s_rows[:, :], ps[7][0:R, 0:N]).then_inc(r["rows"], 1)
            dve.wait_ge(r["rows"], 1)
            dve.tensor_reduce(smax[:, :], s_rows[:, :], AX.X, ALU.max).then_inc(r["smax"], 1)
            dve.wait_ge(r["smax"], 1)

            def cd_next(n):
                dve.wait_ge(r["ln"], n)
                dve.tensor_scalar(cd_na[:, :], cd_ln[:, :], cd_m[:, :], log_k[:, :], ALU.add, ALU.subtract)\
                    .then_inc(r["na"], 1)
                dve.wait_ge(r["na"], n)
                dve.tensor_tensor(cd_m[:, :], smax[:, :], cd_na[:, :], ALU.min).then_inc(r["m"], 1)
                dve.wait_ge(r["m"], n + 1)
                dve.tensor_scalar(cd_t[:, :], s_rows[:, :], cd_na[:, :], cd_m[:, :], ALU.min, ALU.subtract)\
                    .then_inc(r["t"], 1)

            def u_lo(p, k):
                b, j, par = 2 * p + k // 4, k % 4, b_par(k)
                dve.wait_ge(lt["hi"], 4 * b + j + 1)
                dve.tensor_tensor(U[par][1][:, 2 * j:2 * j + 2, :], ps[j == 1][:, :].rearrange("p (h t) -> p h t", h=2),
                                  U[par][0][:, 2 * j:2 * j + 2, :].bitcast(F32), ALU.subtract).then_inc(lt["lo"], 1)

            def neg_max(p, k):
                g = 8 * p + k
                dve.wait_ge(lt["Sp"], g + 1)
                dve.tensor_reduce(nmx[k % 4][:, :], ps[2 + k % 2][:, :].rearrange("p (h t) -> p h t", h=4), AX.X,
                                  ALU.max, negate=True).then_inc(lt["mx"], 1)

            def recip(p, k):
                g = 8 * p + k
                dve.wait_ge(lt["p"], 4 * g + 4)
                dve.reciprocal(rinv[k % 4][:, :], sums[k % 4][:, :]).then_inc(lt["ri"], 1)

            def pt_evac(p, k):
                g = 8 * p + k
                dve.wait_ge(lt["PTp"], g + 1)
                at_least(dve, lt["Op"], g - 1)
                dve.tensor_copy(pt[k % 2][:, :], ps[4 + k % 2][:, :]).then_inc(lt["PT"], 1)

            def finish_light(p, k):
                if k % 2 == 0:
                    return
                b, w = 2 * p + k // 4, k % 4 // 2
                dve.wait_ge(lt["outp"], 2 * b + w + 1)
                at_least(dve, lt["x"], 2 * b + w - 1)
                dve.tensor_tensor(tmp[w][:, 0, :], ps[7][:, 0:D], mod_bc[:, b, 3, :], ALU.mult).then_inc(lt["fin"], 1)

            def top_round(n):
                src = score if n == 0 else left[(n + 1) % 2]
                if n:
                    dve.wait_ge(r["left"], n)
                dve.max(top8[n % 2][:, :], src[:, :]).then_inc(r["top"], 1)
                dve.wait_ge(r["top"], n + 1)
                dve.match_replace(left[n % 2][:, :], top8[n % 2][:, :], src[:, :], -1.0).then_inc(r["left"], 1)

            def cd_dve(p, k):
                u = 8 * p + k
                if not isinstance(p, int) or CD_FIRST < u < CD_FIRST + CD_ITERS:
                    cd_next(u - CD_FIRST)
                elif u == CD_FIRST + CD_ITERS:
                    dve.wait_ge(r["ln"], CD_ITERS)
                    dve.tensor_scalar(cd_na[:, :], cd_ln[:, :], cd_m[:, :], log_k[:, :], ALU.add, ALU.subtract)\
                        .then_inc(r["na"], 1)
                    dve.wait_ge(r["na"], CD_ITERS)
                    dve.tensor_scalar(cd_t[:, :], s_rows[:, :], cd_na[:, :], 0.0, ALU.subtract, ALU.min).then_inc(r["tf"], 1)
                elif TOP_FIRST <= u < 8 * PAIRS:
                    if u == TOP_FIRST:
                        dve.wait_ge(r["sc"], 1)
                    for n in range(3 * (u - TOP_FIRST), min(3 * (u - TOP_FIRST + 1), NQ // 8)):
                        top_round(n)
                elif u == 8 * PAIRS:
                    dve.tensor_scalar(w1m[:, :], score[:, :], -1.0, 1.0, ALU.mult, ALU.add).then_inc(r["w1"], 1)
                    dve.wait_ge(r["w1"], 1)
                    dve.tensor_tensor(wsel[:, 0, :], score[:, :], w1m[:, :], ALU.add).then_inc(r["w"], 1)
                    dve.wait_ge(r["left"], NQ // 8)
                    dve.tensor_scalar(wsel[:, 1, :], left[(NQ // 8 - 1) % 2][:, :], -1.0, None, ALU.is_equal)\
                        .then_inc(r["w"], 1)

            run_stages(dve, [(5, recip), (9, finish_light), (1, u_lo), (6, pt_evac), (3, neg_max)], 8, 3, PAIRS - 1,
                       extra=cd_dve)

            dve.wait_ge(r["selp"], 1)
            dve.tensor_copy(selT[:, :, :, :].rearrange("p n c r -> p (n c r)"), ps[7][:, 0:2 * C * R]).then_inc(r["selT"], 1)
            dve.wait_ge(r["cum"], 1)
            dve.wait_ge(r["selT"], 1)
            dve.tensor_tensor(pos_p[:, :, :], ps[7][:, 0:C * B].rearrange("p (c b) -> p c b", c=C),
                              selT[:, 1, :, 0:B], ALU.mult).then_inc(r["pp"], 1)
            dve.wait_ge(r["pp"], 1)
            dve.tensor_scalar(pos[:, :, :], pos_p[:, :, :], -1.0, None, ALU.add).then_inc(r["pos"], 1)
            dve.wait_ge(r["pos"], 1)

            def one_hot(p, k):
                if k % 4:
                    return
                b, par = 2 * p + k // 4, b_par(k)
                at_least(dve, hv["gtp"], b - 1)
                for i in range(C):
                    dve.tensor_scalar(G[par][:, i, :], iota[:, :], pos[:, i, bass.ds(b, 1)], None, ALU.is_equal)\
                        .then_inc(hv["G"], 1)

            def t_lo(p, k):
                g, b, j, par = 8 * p + k, 2 * p + k // 4, k % 4, b_par(k)
                dve.wait_ge(hv["thi"], g + 1)
                dve.tensor_tensor(U[par][1][:, 2 * j:2 * j + 2, 0:NQ],
                                  ps[0][:, 0:2 * NQ].rearrange("p (h t) -> p h t", h=2),
                                  U[par][0][:, 2 * j:2 * j + 2, 0:NQ].bitcast(F32), ALU.subtract).then_inc(hv["tlo"], 1)

            def v_evac_h(p, k):
                b, w, par = 2 * p + k // 4, k % 4 // 2, b_par(k)
                if k % 2 == 0:
                    return
                dve.wait_ge(hv["vp"], 2 * b + w + 1)
                at_least(dve, hv["Op"], 4 * (b - 1))
                dve.tensor_scalar(V[par][:, w, :], ps[1][:, :], selT[:, 0, w, bass.ds(B + b, 1)], None, ALU.mult)\
                    .then_inc(hv["v"], 1)

            def neg_max_h(p, k):
                g = 8 * p + k
                dve.wait_ge(hv["Sp"], g + 1)
                dve.tensor_reduce(nmx[k % 4][:, 0:2], ps[2 + k % 2][:, :].rearrange("p (h t) -> p h t", h=2), AX.X,
                                  ALU.max, negate=True).then_inc(hv["mx"], 1)

            def recip_h(p, k):
                g = 8 * p + k
                dve.wait_ge(hv["p"], 2 * g + 2)
                dve.reciprocal(rinv[k % 4][:, 0:2], sums[k % 4][:, 0:2]).then_inc(hv["ri"], 1)

            def o_evac_h(p, k):
                g, b, j, par = 8 * p + k, 2 * p + k // 4, k % 4, b_par(k)
                dve.wait_ge(hv["Op"], g + 1)
                at_least(dve, hv["outp"], b - 1)
                dve.tensor_copy(oT[par][:, j, :], ps[6][:, 0:NQ]).then_inc(hv["oT"], 1)

            def finish_heavy(p, k):
                if k % 4 != 3:
                    return
                b, par = 2 * p + k // 4, b_par(k)
                dve.wait_ge(hv["scp"], b + 1)
                at_least(dve, hv["ob"], b - 1)
                for i in range(C):
                    dve.scalar_tensor_tensor(tmp[par][:, i, :], ps[7][:, P + i * P:P + (i + 1) * P],
                                             selT[:, 0, i, bass.ds(b, 1)], mod_bc[:, b, 3, :], ALU.mult, ALU.mult)\
                        .then_inc(hv["fin"], 1)

            dve.wait_ge(lt["x"], 2 * B)
            run_stages(dve, [(7, o_evac_h), (12, finish_heavy), (1, v_evac_h), (0, one_hot), (1, t_lo), (2, neg_max_h),
                             (3, recip_h)], 8, 3, PAIRS)


_INS = ["L0_attn_x", "L0_attn_W", "L0_attn_b", "L0_ffn_gamma_light", "L0_ffn_wq_light", "L0_ffn_wkv_light",
        "L0_ffn_wo_light", "L0_ffn_q_routing_token", "L0_ffn_kv_routing_token", "L0_ffn_gamma_heavy",
        "L0_ffn_wq_heavy", "L0_ffn_wkv_heavy", "L0_ffn_wo_heavy", "L0_c", "L0_wmod"]


def kernel(**inputs):
    import numpy as _np
    import concourse.bacc as _bacc
    from concourse import mybir as _mybir
    from concourse.bass_utils import run_bass_kernel_spmd as _run

    nc = _bacc.Bacc("TRN2", target_bir_lowering=False, num_devices=1)
    arrays, args = {}, []
    for name in _INS:
        arr = _np.ascontiguousarray(inputs[name])
        arrays[f"in_{name}"] = arr
        args.append(nc.dram_tensor(f"in_{name}", arr.shape, _mybir.dt.from_np(arr.dtype), kind="ExternalInput").ap())
    out = nc.dram_tensor("out", (B, N, D), F32, kind="ExternalOutput").ap()
    adaln_routed_attention(nc, *args, out)
    r = _run(nc, [arrays], core_ids=[0])
    return r.results[0]["out"]
```

```python
from contextlib import ExitStack

import numpy as np

import concourse.bass as bass
from concourse import mybir
from concourse.alu_op_type import AluOpType as ALU

ACT = mybir.ActivationFunctionType
AX = mybir.AxisListType
F32 = mybir.dt.float32
F32R = mybir.dt.float32r

P = 128
B, N, D = 16, 256, 128
C = N // P
HEADS, DH = 8, 64
HID = HEADS * DH
NQ = 128
K_Q, K_KV = NQ * 9 / 8, float(N)
CD_ITERS = 50
LN_EPS = 1e-5
MASKED = -9.0e15
ATTN_SCALE = float(D) ** -0.5
HEAD_SCALE = float(DH) ** -0.5
PAIRS = B // 2


def at_least(eng, sem, value):
    if isinstance(value, int) and value <= 0:
        return
    eng.wait_ge(sem, value)


UNITS_A, UNITS_LH = 2, 8
LOOP_A, LOOP_L, LOOP_H = (5, PAIRS), (3, PAIRS - 2), (3, PAIRS)
A_END, L_END, H_END = UNITS_A * PAIRS + 7, UNITS_LH * PAIRS + 9, UNITS_LH * PAIRS + 13
SELECTION = UNITS_LH * PAIRS
H_AT = SELECTION + 2


def steps(phase, units, first, end):
    stages, extra = phase
    for t in range(first, end):
        for lag, f in stages:
            if 0 <= t - lag < units * PAIRS:
                f(*divmod(t - lag, units))
        if extra is not None:
            extra(*divmod(t, units))


def loop(eng, phase, units, pairs):
    stages, extra = phase
    with eng.Fori(*pairs) as p:
        for k in range(units):
            for lag, f in stages:
                f(p + (k - lag) // units, (k - lag) % units)
            if extra is not None:
                extra(p, k)


def run_phases(eng, phase_a, phase_l, phase_h, a_to_l, l_to_h):
    a_to_l, l_to_h = a_to_l.replace(" ", ""), l_to_h.replace(" ", "")
    steps(phase_a, UNITS_A, 0, UNITS_A * LOOP_A[0])
    loop(eng, phase_a, UNITS_A, LOOP_A)
    ta, tl = UNITS_A * LOOP_A[1], 0
    for letter in a_to_l:
        if letter == "a":
            steps(phase_a, UNITS_A, ta, ta + 1)
            ta += 1
        else:
            steps(phase_l, UNITS_LH, tl, tl + 1)
            tl += 1
    assert ta == A_END
    steps(phase_l, UNITS_LH, tl, UNITS_LH * LOOP_L[0])
    loop(eng, phase_l, UNITS_LH, LOOP_L)
    steps(phase_l, UNITS_LH, UNITS_LH * LOOP_L[1], H_AT)
    tl, th = H_AT, 0
    for letter in l_to_h:
        if letter == "l":
            steps(phase_l, UNITS_LH, tl, tl + 1)
            tl += 1
        else:
            steps(phase_h, UNITS_LH, th, th + 1)
            th += 1
    assert tl == L_END
    steps(phase_h, UNITS_LH, th, UNITS_LH * LOOP_H[0])
    loop(eng, phase_h, UNITS_LH, LOOP_H)
    steps(phase_h, UNITS_LH, UNITS_LH * LOOP_H[1], H_END)


def is_unit(g, *units):
    return isinstance(g, int) and g in units


def adaln_routed_attention(nc, x, w_attn, b_attn, gamma_l, wq_l, wkv_l, wo_l, q_tok, kv_tok,
                           gamma_h, wq_h, wkv_h, wo_h, c, wmod, out):
    with ExitStack() as ctx:
        def sb(name, shape, dt=F32):
            return ctx.enter_context(nc.sbuf_tensor(name, shape, dt))

        def sem(name):
            return ctx.enter_context(nc.semaphore(name))

        ps = [ctx.enter_context(nc.psum_tensor(f"bank{i}", [P, 512], F32)) for i in range(8)]
        xh_dram = nc.dram_tensor("xh_scratch", [B, P, C * D], F32).ap()
        mod_rows_dram = nc.dram_tensor("mod_rows_scratch", [B, 4, D], F32).ap()

        X = sb("X", [P, B, C, D])
        XT_hi = sb("XT_hi", [P, B, N], F32R)
        XT_lo = sb("XT_lo", [P, B, N], F32R)
        ident = sb("ident", [P, P])
        tri = sb("tri", [P, P])
        ones = sb("ones", [P, P])
        iota = sb("iota", [P, P])
        mask = sb("mask", [P, 3 * P])
        neg_half = sb("neg_half", [P, B * C])
        mod_bc = sb("mod_bc", [P, B, 4, D])
        tok_bc = sb("tok_bc", [P, 2, D])
        bv_bc = sb("bv_bc", [P, D])
        gam_bc = sb("gam_bc", [P, 2, D])
        gam_col = sb("gam_col", [P, 2])
        gam_sc = sb("gam_sc", [P, 2])
        b_col = sb("b_col", [P, 2])
        bq_sc = sb("bq_sc", [P, 1])
        modT = sb("modT", [P, 2, B])
        w_at = sb("w_at", [P, 3 * D])
        wmod_sb = sb("wmod_sb", [P, 6 * D])
        wo_l_sb = sb("wo_l_sb", [P, 4, D])
        wo_h_sb = sb("wo_h_sb", [P, 4, D])
        U_w = [sb(f"U_w_{s}", [P, HEADS, D], F32R) for s in ("hi", "lo")]
        V_w = [sb(f"V_w_{s}", [P, HID], F32R) for s in ("hi", "lo")]
        T_w = sb("T_w", [P, HEADS, D])
        VH_w = [sb(f"VH_w_{s}", [P, HID], F32R) for s in ("hi", "lo")]

        S_all = sb("S_all", [P, B, C, 2])
        two = range(2)
        xhs = [sb(f"xhs{i}", [P, C, D]) for i in two]

        R = 2 * B
        S_dense = sb("S_dense", [P, C, R])
        s_rows = sb("s_rows", [R, N])
        smax = sb("smax", [R, 1])
        log_k = sb("log_k", [R, 1])
        cd_t = sb("cd_t", [R, N])
        cd_e = sb("cd_e", [R, N])
        cd_m = sb("cd_m", [R, 1])
        cd_sum = sb("cd_sum", [R, 1])
        cd_ln = sb("cd_ln", [R, 1])
        cd_na = sb("cd_na", [R, 1])
        score = sb("score", [R, N])
        left = [sb(f"left{i}", [R, N]) for i in two]
        top8 = [sb(f"top8{i}", [R, 8]) for i in two]
        w1m = sb("w1m", [R, N])
        wsel = sb("wsel", [R, 2, N])
        selT = sb("selT", [P, 2, C, R])
        pos_p = sb("pos_p", [P, C, B])
        pos = sb("pos", [P, C, B])

        st1 = sb("st1", [P, B, C, 6])
        t1 = sb("t1", [P, 5, B * C])
        mean1 = sb("mean1", [P, B * C])
        ve1 = sb("ve1", [P, B * C])
        rs1 = sb("rs1", [P, B * C])
        nm1 = sb("nm1", [P, B * C])
        early = ExitStack()
        late = sb
        sb = lambda name, shape, dt=F32: early.enter_context(nc.sbuf_tensor(name, shape, dt))
        wq_raw = sb("wq_raw", [P, 2, HID])
        wkv_raw = sb("wkv_raw", [P, 2 * HID])
        wk_hT = sb("wk_hT", [P, 4, D])
        wv_hT = sb("wv_hT", [P, 4, D])
        wqT = sb("wqT", [P, 2, 4, D])
        wkT = sb("wkT", [P, 4, D])
        big = sb("big", [P, HEADS, D])
        v_big = sb("v_big", [P, 2, HID])
        c_sb = sb("c_sb", [B, D])
        c_e = sb("c_e", [B, D])
        c_d = sb("c_d", [B, D])
        c_r = sb("c_r", [B, D])
        c_s = sb("c_s", [B, D])
        cT = sb("cT", [P, B])
        mod_raw = sb("mod_raw", [B, 4, D])
        mod_fix = sb("mod_fix", [B, 4, D])
        gate_s = sb("gate_s", [B, 2, D])
        gate_a = sb("gate_a", [B, 2, D])
        gate_m = sb("gate_m", [B, 2, D])

        xl = [sb(f"xl{i}", [P, C, D]) for i in two]
        hT = [sb(f"hT{i}", [P, N]) for i in two]
        qT = [sb(f"qT{i}", [P, N]) for i in two]
        kT = [sb(f"kT{i}", [P, N]) for i in two]
        va = [sb(f"va{i}", [P, C, D]) for i in two]
        sm = [sb(f"sm{i}", [P, 3 * P]) for i in two]
        mxa = [sb(f"mxa{i}", [P, C]) for i in two]
        nmxa = [sb(f"nmxa{i}", [P, C]) for i in two]
        pa = [sb(f"pa{i}", [P, 3 * P]) for i in two]
        suma = [sb(f"suma{i}", [P, C]) for i in two]
        rinva = [sb(f"rinva{i}", [P, C]) for i in two]
        pta = [sb(f"pta{i}", [P, 3 * P]) for i in two]
        ao = [sb(f"ao{i}", [P, C, D]) for i in two]
        st2 = [sb(f"st2{i}", [P, C, 6]) for i in two]
        mv2 = [sb(f"mv2{i}", [P, C, 2]) for i in two]
        nm2 = [sb(f"nm2{i}", [P, C]) for i in two]
        ve2 = [sb(f"ve2{i}", [P, C]) for i in two]
        rs2 = [sb(f"rs2{i}", [P, C]) for i in two]
        hn = [sb(f"hn{i}", [P, C, D]) for i in two]
        hm = [sb(f"hm{i}", [P, C, D]) for i in two]
        h2 = [sb(f"h2{i}", [P, C, D]) for i in two]
        sq = sb("sq", [P, 2, C, D])
        ss = [sb(f"ss{i}", [P, C]) for i in two]
        ssc = [sb(f"ssc{i}", [P, C]) for i in two]
        rn = [sb(f"rn{i}", [P, C]) for i in two]
        rprod = sb("rprod", [P, 2, 4, D])
        s4 = [sb(f"s4{i}", [P, 4]) for i in two]
        early.close()
        sb = late
        xt = [[sb(f"xt{i}{s}", [P, N], F32R) for s in ("hi", "lo")] for i in two]
        U = [[sb(f"U{i}{s}", [P, HEADS, N], F32R) for s in ("hi", "lo")] for i in two]
        V = [sb(f"V{i}", [P, C, HID]) for i in two]
        pr = [sb(f"pr{i}", [P, 512]) for i in range(4)]
        nmx = [sb(f"nmx{i}", [P, 4]) for i in range(4)]
        sums = [sb(f"sums{i}", [P, 4]) for i in range(4)]
        rinv = [sb(f"rinv{i}", [P, 4]) for i in range(4)]
        pt = [sb(f"pt{i}", [P, 512]) for i in two]
        oT = [sb(f"oT{i}", [P, 4, P]) for i in two]
        tmp = [sb(f"tmp{i}", [P, C, D]) for i in two]
        xh = [sb(f"xh{i}", [P, C, D]) for i in two]
        G = [sb(f"G{i}", [P, C, NQ]) for i in two]
        GT = [sb(f"GT{i}", [P, C, P]) for i in two]
        xq = [sb(f"xq{i}", [P, NQ]) for i in two]
        rt = [sb(f"rt{i}", [P, D]) for i in two]
        ob = [sb(f"ob{i}", [P, C, D]) for i in two]

        x_in = [sem(f"x_in{i}") for i in range(4)]
        c_in, wmod_in, w_at_in, wl_in, wh_in, wo_in = (sem("c_in"), sem("wmod_in"), sem("w_at_in"), sem("wl_in"),
                                                       sem("wh_in"), sem("wo_in"))
        col_in, bc_in, gam_in, mod_out = sem("col_in"), sem("bc_in"), sem("gam_in"), sem("mod_out")
        mod_in = [sem(f"mod_in{i}") for i in range(2)]
        g_const, g_tab = sem("g_const"), sem("g_tab")
        st1_done, mv1_sums, mv1_parts, ve1_done, rs1_done, nm1_done = (
            sem("st1_done"), sem("mv1_sums"), sem("mv1_parts"), sem("ve1_done"), sem("rs1_done"), sem("nm1_done"))
        c_exp, c_den, c_act, cT_ps, cT_sb = sem("c_exp"), sem("c_den"), sem("c_act"), sem("cT_ps"), sem("cT_sb")
        col_ps, row_ps, col_sb, row_sb, gate_done, fix_done = (
            sem("col_ps"), sem("row_ps"), sem("col_sb"), sem("row_sb"), sem("gate_done"), sem("fix_done"))
        w_small, w_ps, w_tr, w_prod, v_scaled, w_hi, w_split = (
            sem("w_small"), sem("w_ps"), sem("w_tr"), sem("w_prod"), sem("v_scaled"), sem("w_hi"), sem("w_split"))
        a = {n: sem("a_" + n) for n in (
            "xl", "hp", "hT", "qkp", "vp", "qkT", "v", "Sp", "sm", "nmx", "p", "PTp", "PT", "Op", "ri",
            "ao", "x1", "st", "mv", "ve", "rs", "nm", "hn", "hm", "h2", "ss", "ssc", "rn", "s4", "S", "xh",
            "xhd0", "xhd1", "xp", "xhi", "xlo")}
        r = {n: sem("r_" + n) for n in (
            "Sd", "Sp", "rows", "smax", "m", "t", "e", "ln", "na", "tf", "sc", "top", "left", "w1", "w", "selp",
            "selT", "cum", "pp", "pos")}
        lt = {n: sem("l_" + n) for n in (
            "xt0", "xt1", "up", "vp", "hi", "lo", "v", "Sp", "mx", "p", "ri", "pn", "PTp", "PT", "Op", "oT", "outp", "fin", "x")}
        hv = {n: sem("h_" + n) for n in (
            "xt0", "xt1", "G", "xqp", "xq", "gtp", "gt", "tp", "thi", "tlo", "vp", "v", "Sp", "mx", "p", "ri", "pn",
            "PTp", "PT", "Op", "oT", "outp", "rt", "scp", "fin", "ob", "out0", "out1")}

        block = ctx.enter_context(nc.Block())

        CD_FIRST = 8 * (PAIRS - 1) - CD_ITERS
        TOP_FIRST = CD_FIRST + CD_ITERS + 1
        ACT_PT = CD_FIRST + CD_ITERS - 4
        MOD_FIRST = 4
        ROUNDS = NQ // 8
        ROWS_AT = B + 4
        OUT_LAG = 8

        def b_par(k):
            return k // 4

        W_PIECES = ("wq light", "wk light", "even light", "odd light", "wq heavy", "even heavy", "odd heavy", "wv heavy")
        TRANSPOSED = (0, 1, 4)

        def evacuated(n):
            if n in TRANSPOSED:
                return w_tr, TRANSPOSED.index(n) + 1
            return w_prod, sum(i not in TRANSPOSED for i in range(n + 1))

        @block.sync
        def _(sp):
            for i in range(4):
                sp.dma_start(X[:, 4 * i:4 * i + 4, :, :],
                             x[4 * i:4 * i + 4].rearrange("b (c p) d -> p b c d", p=P)).then_inc(x_in[i], 16)
                if i == 0:
                    sp.dma_start(w_at[:, :], w_attn).then_inc(w_at_in, 16)
            sp.dma_start(wq_raw[:, 0, :], wq_l).then_inc(wl_in, 16)
            sp.dma_start(wkv_raw[:, :], wkv_l).then_inc(wl_in, 16)
            for dst, src in ((bv_bc[:, :], b_attn[2 * D:3 * D]), (gam_bc[:, 0, :], gamma_l), (gam_bc[:, 1, :], gamma_h),
                             (tok_bc[:, 0, :], q_tok), (tok_bc[:, 1, :], kv_tok)):
                sp.dma_start(dst, src.rearrange("(a d) -> a d", a=1).broadcast_to([P, D])).then_inc(bc_in, 16)
            sp.wait_ge(fix_done, 3)
            sp.dma_start(mod_rows_dram, mod_fix[:, :, :]).then_inc(mod_out, 16)
            sp.wait_ge(mod_out, 16)
            for i, (lo, hi) in enumerate(((0, MOD_FIRST), (MOD_FIRST, B))):
                sp.dma_start(mod_bc[:, lo:hi].rearrange("p b j d -> p (b j d)"),
                             mod_rows_dram[lo:hi].rearrange("b j d -> (b j d)").rearrange("(a n) -> a n", a=1)
                             .broadcast_to([P, (hi - lo) * 4 * D])).then_inc(mod_in[i], 16)

            def keep_rows(p, k):
                sp.wait_ge(a["xh"], 4 * p + 2 * k + 2)
                sp.dma_start(xh_dram[2 * p + k], xhs[k][:, :, :].rearrange("p c d -> p (c d)")).then_inc(a[f"xhd{k}"], 16)

            def load_light(p, k):
                b = 2 * p + k
                at_least(sp, lt["Sp"], 4 * (b - 1))
                sp.dma_start(xt[k][0][:, :].bitcast(F32), XT_hi[:, b, :].bitcast(F32)).then_inc(lt[f"xt{k}"], 16)
                sp.dma_start(xt[k][1][:, :].bitcast(F32), XT_lo[:, b, :].bitcast(F32)).then_inc(lt[f"xt{k}"], 16)

            with sp.Fori(0, PAIRS - 2) as p:
                for k in range(2):
                    keep_rows(p, k)
            sp.wait_ge(w_split, 3)
            sp.wait_ge(a["xlo"], 2)
            for k in range(2):
                load_light(0, k)
            for p in range(PAIRS - 2, PAIRS):
                for k in range(2):
                    keep_rows(p, k)
            sp.wait_ge(a["xlo"], B)
            with sp.Fori(1, PAIRS) as p:
                for k in range(2):
                    load_light(p, k)

            for k in range(2):
                sp.wait_ge(a[f"xhd{k}"], 16 * PAIRS)

            def load_heavy(p, k):
                b = 2 * p + k
                at_least(sp, hv["vp"], 2 * (b - 1))
                at_least(sp, hv["xqp"], b - 1)
                if is_unit(b, 0, 1):
                    sp.wait_ge(lt["Sp"], 4 * (B - 1 + b))
                sp.dma_start(xt[k][0][:, :].bitcast(F32), XT_hi[:, b, :].bitcast(F32)).then_inc(hv[f"xt{k}"], 16)
                sp.dma_start(xt[k][1][:, :].bitcast(F32), XT_lo[:, b, :].bitcast(F32)).then_inc(hv[f"xt{k}"], 16)
                sp.dma_start(xh[k][:, :, :].rearrange("p c d -> p (c d)"), xh_dram[b]).then_inc(hv[f"xt{k}"], 16)

            def store(p, k):
                b = 2 * p + k
                sp.wait_ge(hv["ob"], b + 1)
                sp.dma_start(out[b].rearrange("(c p) d -> p c d", p=P), ob[k][:, :, :]).then_inc(hv[f"out{k}"], 16)

            for p in range(2):
                for k in range(2):
                    load_heavy(p, k)
            with sp.Fori(2, PAIRS) as p:
                for k in range(2):
                    load_heavy(p, k)
                    store(p - 2, k)
            for p in range(PAIRS - 2, PAIRS):
                for k in range(2):
                    store(p, k)
            for k in range(2):
                sp.wait_ge(hv[f"out{k}"], 16 * PAIRS)

        @block.gpsimd
        def _(pool):
            pool.memset(ident[:, :], 0.0).then_inc(g_const, 1)
            pool.memset(tri[:, :], 1.0).then_inc(g_const, 1)
            pool.memset(ones[:, :], 1.0).then_inc(g_const, 1)
            pool.memset(mask[:, :], 0.0).then_inc(g_const, 1)
            pool.memset(neg_half[:, :], -0.5).then_inc(g_const, 1)
            pool.iota(iota[:, :], [[1, P]], base=0, channel_multiplier=0,
                      allow_small_or_imprecise_dtypes=True).then_inc(g_const, 1)
            pool.memset(log_k[:, :], float(np.log(np.float32(K_KV)))).then_inc(g_const, 1)
            pool.wait_ge(g_const, 7)
            pool.affine_select(ident[:, :], ident[:, :], pattern=[[-1, P]], compare_op=ALU.not_equal, fill=1.0,
                               base=0, channel_multiplier=1).then_inc(g_tab, 1)
            pool.affine_select(tri[:, :], tri[:, :], pattern=[[1, P]], compare_op=ALU.is_ge, fill=0.0,
                               base=0, channel_multiplier=-1).then_inc(g_tab, 1)
            pool.affine_select(mask[:, 0:P], mask[:, 0:P], pattern=[[-1, P]], compare_op=ALU.is_ge, fill=MASKED,
                               base=0, channel_multiplier=1).then_inc(g_tab, 1)
            pool.affine_select(mask[:, 2 * P:3 * P], mask[:, 2 * P:3 * P], pattern=[[-1, P]], compare_op=ALU.is_ge,
                               fill=MASKED, base=0, channel_multiplier=1).then_inc(g_tab, 1)
            pool.memset(log_k[0:B, :], float(np.log(np.float32(K_Q)))).then_inc(g_tab, 1)

            def rstd1(n, lo, hi):
                pool.wait_ge(ve1_done, n + 1)
                pool.tensor_tensor(rs1[:, lo:hi], ve1[:, lo:hi], neg_half[:, lo:hi], ALU.pow).then_inc(rs1_done, 1)

            pool.dma_start(wq_raw[:, 1, :], wq_h).then_inc(wh_in, 16)
            kv_rows = wkv_h.rearrange("(q i t m) d -> i t m q d", i=2, t=2, m=DH)
            for i in range(2):
                pool.dma_start(wk_hT[i * DH:(i + 1) * DH, :, :], kv_rows[i, 0]).then_inc(wh_in, 16)
                if i == 1:
                    rstd1(0, 0, 4 * C)
                pool.dma_start(wv_hT[i * DH:(i + 1) * DH, :, :], kv_rows[i, 1]).then_inc(wh_in, 16)
            pool.dma_start(wo_l_sb[:, :, :], wo_l.rearrange("(q p) d -> p q d", p=P)).then_inc(wo_in, 16)
            pool.dma_start(wo_h_sb[:, :, :], wo_h.rearrange("(q p) d -> p q d", p=P)).then_inc(wo_in, 16)

            rstd1(1, 4 * C, B * C)

            def residual(p, k):
                b = 2 * p + k
                pool.wait_ge(a["ao"], 2 * b + 2)
                pool.tensor_tensor(X[:, b], X[:, b], ao[k][:, :, :], ALU.add).then_inc(a["x1"], 1)

            def ln2_rstd(p, k):
                pool.wait_ge(a["ve"], 2 * p + k + 1)
                at_least(pool, a["hn"], 2 * (2 * p + k - 1))
                pool.tensor_tensor(rs2[k][:, :], ve2[k][:, :], neg_half[:, 0:C], ALU.pow).then_inc(a["rs"], 1)

            def modulate(p, k):
                b = 2 * p + k
                pool.wait_ge(a["hn"], 2 * b + 2)
                if is_unit(b, 0, MOD_FIRST):
                    pool.wait_ge(mod_in[b // MOD_FIRST], 16)
                pool.tensor_tensor(hm[k][:, :, :], hn[k][:, :, :],
                                   mod_bc[:, b, 1:2, :].broadcast_to([P, C, D]), ALU.mult).then_inc(a["hm"], 1)
                pool.wait_ge(a["hm"], b + 1)
                at_least(pool, a["ss"], 2 * (b - 1))
                at_least(pool, a["xh"], 2 * (b - 1))
                pool.tensor_tensor(h2[k][:, :, :], hm[k][:, :, :],
                                   mod_bc[:, b, 2:3, :].broadcast_to([P, C, D]), ALU.add).then_inc(a["h2"], 1)

            def rms(p, k):
                pool.wait_ge(a["ssc"], 2 * p + k + 1)
                at_least(pool, a["xh"], 2 * (2 * p + k - 1))
                pool.tensor_tensor(rn[k][:, :], ssc[k][:, :], neg_half[:, 0:C], ALU.pow).then_inc(a["rn"], 1)

            def normalise(p, k):
                g = 8 * p + k
                pool.wait_ge(lt["ri"], g + 1)
                q = pr[k % 4][:, :].rearrange("p (h t) -> p h t", h=4)
                pool.tensor_tensor(q, q, rinv[k % 4][:, :, None].broadcast_to([P, 4, P]), ALU.mult)\
                    .then_inc(lt["pn"], 1)

            def add_light(p, k):
                if k % 2 == 0:
                    return
                b, w = 2 * p + k // 4, k % 4 // 2
                pool.wait_ge(lt["fin"], 2 * b + w + 1)
                pool.tensor_tensor(X[:, b, w, :], X[:, b, w, :], tmp[w][:, 0, :], ALU.add).then_inc(lt["x"], 1)

            def normalise_h(p, k):
                g = 8 * p + k
                pool.wait_ge(hv["ri"], g + 1)
                q = pr[k % 4][:, :].rearrange("p (h t) -> p h t", h=2)
                pool.tensor_tensor(q, q, rinv[k % 4][:, 0:2, None].broadcast_to([P, 2, N]), ALU.mult)\
                    .then_inc(hv["pn"], 1)

            def add_heavy(p, k):
                if k % 4 != 3:
                    return
                b = 2 * p + k // 4
                pool.wait_ge(hv["fin"], 2 * b + 2)
                at_least(pool, hv[f"out{b_par(k)}"], 16 * p)
                pool.tensor_tensor(ob[b_par(k)][:, :, :], X[:, b], tmp[b_par(k)][:, :, :], ALU.add)\
                    .then_inc(hv["ob"], 1)

            run_phases(pool, ([(4, residual), (5, modulate), (4, ln2_rstd), (6, rms)], None),
                       ([(5, normalise), (9, add_light)], None),
                       ([(3, normalise_h), (11, add_heavy)], None),
                       "al al al al al al al", "lh lh lh lh lh lh lh")

        @block.scalar
        def _(act):
            act.preload_act_table_set("natural_log_exp_and_others")
            act.dma_start(c_sb[:, :], c).then_inc(c_in, 16)
            act.dma_start(wmod_sb[:, :], wmod).then_inc(wmod_in, 16)
            for j in range(2):
                act.dma_start(b_col[:, j:j + 1], b_attn[j * D:(j + 1) * D].rearrange("(p a) -> p a", a=1)).then_inc(col_in, 16)

            act.wait_ge(c_in, 16)
            act.activation(c_e[:, :], c_sb[:, :], ACT.Exp, scale=-1.0).then_inc(c_exp, 1)
            act.dma_start(gam_col[:, 0:1], gamma_l.rearrange("(p a) -> p a", a=1)).then_inc(gam_in, 16)
            act.dma_start(gam_col[:, 1:2], gamma_h.rearrange("(p a) -> p a", a=1)).then_inc(gam_in, 16)

            act.wait_ge(col_sb, 2)

            rs1_bc = rs1[:, :].rearrange("p (b c) -> p b c", c=C)
            nm1_bc = nm1[:, :].rearrange("p (b c) -> p b c", c=C)

            def ln1(p, k):
                b = 2 * p + k
                if isinstance(b, int):
                    act.wait_ge(nm1_done, 1 if b < 4 else 2)
                at_least(act, a["hp"], b - 1)
                for i in range(C):
                    act.activation(xl[k][:, i, :], X[:, b, i, :], ACT.Identity, bias=nm1_bc[:, b, i:i + 1],
                                   scale=rs1_bc[:, b, i:i + 1]).then_inc(a["xl"], 1)

            def h_evac(p, k):
                b = 2 * p + k
                act.wait_ge(a["hp"], b + 1)
                at_least(act, a["vp"], b - 1)
                act.activation(hT[k][:, :], ps[0][:, 0:N], ACT.Identity, bias=modT[:, 0, bass.ds(b, 1)],
                               scale=modT[:, 1, bass.ds(b, 1)]).then_inc(a["hT"], 1)

            def ln2(p, k):
                b = 2 * p + k
                act.wait_ge(a["nm"], b + 1)
                at_least(act, a["hm"], b - 1)
                for i in range(C):
                    act.activation(hn[k][:, i, :], X[:, b, i, :], ACT.Identity, bias=nm2[k][:, i:i + 1],
                                   scale=rs2[k][:, i:i + 1]).then_inc(a["hn"], 1)

            def w_evac(p, k):
                n = 2 * p + k - 1
                if isinstance(n, int) and n in TRANSPOSED:
                    act.wait_ge(w_ps, n + 1)
                    dst = (wqT[:, 0], wkT[:, :, :], wqT[:, 1])[TRANSPOSED.index(n)]
                    act.activation(dst, ps[7][:, :].rearrange("p (q d) -> p q d", q=4), ACT.Copy).then_inc(w_tr, 1)

            def qk_evac(p, k):
                b = 2 * p + k
                act.wait_ge(a["qkp"], b + 1)
                if is_unit(b, 0):
                    act.wait_ge(w_small, 1)
                    act.wait_ge(col_in, 32)
                at_least(act, a["Sp"], b - 1)
                act.activation(qT[k][:, :], ps[2][:, 0:N], ACT.Identity, bias=bq_sc[:, :], scale=ATTN_SCALE)\
                    .then_inc(a["qkT"], 1)
                act.activation(kT[k][:, :], ps[2][:, N:2 * N], ACT.Identity, bias=b_col[:, 1:2]).then_inc(a["qkT"], 1)

            def exps_a(p, k):
                b = 2 * p + k
                act.wait_ge(a["nmx"], b + 1)
                at_least(act, a["PTp"], b - 1)
                at_least(act, a["ri"], b - 1)
                act.activation(pa[k][:, 0:P], sm[k][:, 0:P], ACT.Exp, bias=nmxa[k][:, 0:1],
                               accum_out=suma[k][:, 0:1]).then_inc(a["p"], 1)
                act.activation(pa[k][:, P:3 * P], sm[k][:, P:3 * P], ACT.Exp, bias=nmxa[k][:, 1:2],
                               accum_out=suma[k][:, 1:2]).then_inc(a["p"], 1)

            def pt_evac_a(p, k):
                b = 2 * p + k
                act.wait_ge(a["PTp"], b + 1)
                at_least(act, a["Op"], b - 1)
                act.activation(pta[k][:, :], ps[5][:, 0:3 * P], ACT.Copy).then_inc(a["PT"], 1)

            def squares(p, k):
                b = 2 * p + k
                act.wait_ge(a["h2"], b + 1)
                at_least(act, a["ssc"], b - 1)
                at_least(act, a["ss"], 2 * (b - 1))
                for i in range(C):
                    act.activation(sq[:, k, i, :], h2[k][:, i, :], ACT.Square,
                                   accum_out=ss[k][:, i:i + 1]).then_inc(a["ss"], 1)

            def xt_hi(p, k):
                b = 2 * p + k
                act.wait_ge(a["xp"], b + 1)
                act.activation(XT_hi[:, b, :], ps[1][:, 0:N], ACT.Copy).then_inc(a["xhi"], 1)

            def cd_sums(n):
                act.wait_ge(r["t"], n + 1)
                at_least(act, r["ln"], n)
                act.activation(cd_e[:, :], cd_t[:, :], ACT.Exp, accum_out=cd_sum[:, :]).then_inc(r["e"], 1)
                act.wait_ge(r["e"], n + 1)
                act.activation(cd_ln[:, :], cd_sum[:, :], ACT.Ln).then_inc(r["ln"], 1)

            def u_hi(p, k):
                b, j = 2 * p + k // 4, k % 4
                act.wait_ge(lt["up"], 4 * b + j + 1)
                act.activation(U[b_par(k)][0][:, 2 * j:2 * j + 2, :], ps[7 * (j == 1)][:, :].rearrange("p (h t) -> p h t", h=2),
                               ACT.Copy).then_inc(lt["hi"], 1)

            def v_evac_l(p, k):
                b, w = 2 * p + k // 4, k % 4 - 2
                if w < 0:
                    return
                act.wait_ge(lt["vp"], 2 * b + w + 1)
                at_least(act, lt["Op"], 4 * (b - 2) + 2 * (w + 1))
                act.activation(V[b_par(k)][:, w, :], ps[7][:, :], ACT.Copy).then_inc(lt["v"], 1)

            def o_evac(p, k):
                g, b, j = 8 * p + k, 2 * p + k // 4, k % 4
                w, half = j // 2, j % 2
                act.wait_ge(lt["Op"], g + 1)
                at_least(act, lt["outp"], 2 * b + w - 1)
                act.activation(oT[w][:, 2 * half:2 * half + 2, :],
                               ps[6][:, 0:2 * P].rearrange("p (q t) -> p q t", q=2), ACT.Copy).then_inc(lt["oT"], 1)

            def exps(p, k):
                g = 8 * p + k
                act.wait_ge(lt["mx"], g + 1)
                at_least(act, lt["PTp"], g - 3)
                for i in range(4):
                    act.activation(pr[k % 4][:, i * P:(i + 1) * P], ps[2 + k % 2][:, i * P:(i + 1) * P], ACT.Exp,
                                   bias=nmx[k % 4][:, i:i + 1],
                                   accum_out=sums[k % 4][:, i:i + 1]).then_inc(lt["p"], 1)

            def cd_act(p, k):
                u = 8 * p + k
                if not isinstance(p, int) or CD_FIRST <= u < CD_FIRST + CD_ITERS:
                    cd_sums(u - CD_FIRST)
                elif u == CD_FIRST + CD_ITERS + 1:
                    act.wait_ge(r["tf"], 1)
                    act.activation(score[:, :], cd_t[:, :], ACT.Exp).then_inc(r["sc"], 1)

            def pt_evac_act(p, k):
                g = 8 * p + k
                if not (isinstance(g, int) and g >= ACT_PT):
                    return
                act.wait_ge(lt["PTp"], g + 1)
                act.wait_ge(lt["Op"], g - 1)
                act.wait_ge(lt["PT"], g)
                act.activation(pt[k % 2][:, :], ps[4 + k % 2][:, :], ACT.Copy).then_inc(lt["PT"], 1)

            def xq_evac(p, k):
                if k % 4:
                    return
                b = 2 * p + k // 4
                act.wait_ge(hv["xqp"], b + 1)
                act.activation(xq[b_par(k)][:, :], ps[1][:, 0:NQ], ACT.Copy).then_inc(hv["xq"], 1)

            def gt_evac(p, k):
                if k % 4:
                    return
                b = 2 * p + k // 4
                act.wait_ge(hv["gtp"], b + 1)
                act.activation(GT[b_par(k)][:, :, :], ps[1][:, P:3 * P].rearrange("p (c t) -> p c t", c=C),
                               ACT.Copy).then_inc(hv["gt"], 1)

            def t_hi(p, k):
                g, j = 8 * p + k, k % 4
                act.wait_ge(hv["tp"], g + 1)
                act.activation(U[b_par(k)][0][:, 2 * j:2 * j + 2, 0:NQ],
                               ps[0][:, 0:2 * NQ].rearrange("p (h t) -> p h t", h=2), ACT.Copy).then_inc(hv["thi"], 1)

            def exps_h(p, k):
                g = 8 * p + k
                act.wait_ge(hv["mx"], g + 1)
                if is_unit(g, 0, 1, 2, 3):
                    act.wait_ge(lt["PTp"], 8 * PAIRS - 3 + g)
                at_least(act, hv["PTp"], g - 3)
                for i in range(2):
                    act.activation(pr[k % 4][:, i * N:(i + 1) * N], ps[2 + k % 2][:, i * N:(i + 1) * N], ACT.Exp,
                                   bias=nmx[k % 4][:, i:i + 1],
                                   accum_out=sums[k % 4][:, i:i + 1]).then_inc(hv["p"], 1)

            def rt_evac(p, k):
                if k % 4 != 3:
                    return
                b = 2 * p + k // 4
                act.wait_ge(hv["outp"], b + 1)
                act.activation(rt[b_par(k)][:, :], ps[1][:, 0:D], ACT.Copy).then_inc(hv["rt"], 1)

            def pt_evac_h(p, k):
                g = 8 * p + k
                act.wait_ge(hv["PTp"], g + 1)
                if is_unit(g, 0):
                    act.wait_ge(lt["Op"], 8 * PAIRS)
                at_least(act, hv["Op"], g - 1)
                act.activation(pt[k % 2][:, :], ps[4 + k % 2][:, :], ACT.Copy).then_inc(hv["PT"], 1)

            run_phases(act, ([(2, qk_evac), (1, h_evac), (6, squares), (3, exps_a), (5, ln2), (0, ln1), (3, pt_evac_a),
                              (7, xt_hi)], w_evac),
                       ([(7, o_evac), (1, v_evac_l), (0, u_hi), (6, pt_evac_act), (3, exps), (0, cd_act)], None),
                       ([(0, xq_evac), (10, rt_evac), (5, pt_evac_h), (7, gt_evac), (2, exps_h), (0, t_hi)], None),
                       "aal al al al la la", "lh lh lh lh lh lh lh")

        @block.tensor
        def _(pe):
            def triple(out, weights, moving, start=True, stop=True):
                pe.matmul(out, weights[1], moving[0], start=start, stop=False)
                pe.matmul(out, weights[0], moving[1], start=False, stop=False)
                return pe.matmul(out, weights[0], moving[0], start=False, stop=stop)

            pe.wait_ge(g_tab, 1)
            pe.wait_ge(c_act, 1)
            pe.transpose(ps[4][:, 0:B], c_s[:, :], ident[0:B, 0:B]).then_inc(cT_ps, 1)
            pe.wait_ge(cT_sb, 1)
            pe.wait_ge(wmod_in, 16)
            for j in range(2):
                mm = pe.matmul(ps[7][:, j * B:(j + 1) * B], wmod_sb[:, j * D:(j + 1) * D], cT[:, :],
                               start=True, stop=True)
            mm.then_inc(col_ps, 1)
            pe.matmul(ps[5][0:B, :], cT[:, :], wmod_sb[:, 2 * D:6 * D], start=True, stop=True).then_inc(row_ps, 1)
            pe.wait_ge(w_at_in, 16)

            def w_piece(p, k):
                n = 2 * p + k
                if not isinstance(n, int) or n >= len(W_PIECES):
                    return
                if n == 0:
                    pe.wait_ge(col_sb, 2)
                    pe.wait_ge(wl_in, 32)
                else:
                    pe.wait_ge(*evacuated(n - 1))
                if n == 4:
                    pe.wait_ge(wh_in, 80)
                what, light = W_PIECES[n].split()[0], "light" in W_PIECES[n]
                for q in range(4):
                    o = ps[7][:, q * P:(q + 1) * P]
                    if what == "wv":
                        mm = pe.transpose(o, wv_hT[:, q, :], ident[:, :])
                    elif what in ("wq", "wk"):
                        src = wkv_raw[:, 0:HID] if what == "wk" else wq_raw[:, 0 if light else 1, :]
                        mm = pe.transpose(o, src[:, q * P:(q + 1) * P], ident[:, :])
                    else:
                        r0 = DH * (what == "odd")
                        if light:
                            mm = pe.matmul(o, wkT[r0:r0 + DH, q, :], wqT[r0:r0 + DH, 0, q, :], start=True, stop=True)
                        else:
                            mm = pe.matmul(o, wqT[r0:r0 + DH, 1, q, :], wk_hT[r0:r0 + DH, q, :], start=True, stop=True)
                mm.then_inc(w_ps, 1)

            def h_transpose(p, k):
                b = 2 * p + k
                pe.wait_ge(a["xl"], 2 * b + 2)
                at_least(pe, a["hT"], b)
                for i in range(C):
                    mm = pe.transpose(ps[0][:, i * P:(i + 1) * P], xl[k][:, i, :], ident[:, :])
                mm.then_inc(a["hp"], 1)

            def query_key(p, k):
                b = 2 * p + k
                pe.wait_ge(a["hT"], b + 1)
                at_least(pe, a["qkT"], 2 * b)
                pe.matmul(ps[2][:, 0:N], w_at[:, 0:D], hT[k][:, :], start=True, stop=True)
                pe.matmul(ps[2][:, N:2 * N], w_at[:, D:2 * D], hT[k][:, :], start=True, stop=True).then_inc(a["qkp"], 1)

            def value_a(p, k):
                b = 2 * p + k
                at_least(pe, a["v"], b)
                for i in range(C):
                    mm = pe.matmul(ps[3][:, i * P:(i + 1) * P], hT[k][:, i * P:(i + 1) * P], w_at[:, 2 * D:3 * D],
                                   start=True, stop=True)
                mm.then_inc(a["vp"], 1)

            def scores_a(p, k):
                b = 2 * p + k
                pe.wait_ge(a["qkT"], 2 * b + 2)
                at_least(pe, a["sm"], 2 * b)
                pe.matmul(ps[4][:, 0:P], qT[k][:, 0:P], kT[k][:, 0:P], start=True, stop=True)
                pe.matmul(ps[4][:, P:3 * P], qT[k][:, P:2 * P], kT[k][:, :], start=True, stop=True).then_inc(a["Sp"], 1)

            def p_transpose_a(p, k):
                b = 2 * p + k
                pe.wait_ge(a["p"], 2 * b + 2)
                at_least(pe, a["PT"], b)
                for i in range(3):
                    mm = pe.transpose(ps[5][:, i * P:(i + 1) * P], pa[k][:, i * P:(i + 1) * P], ident[:, :])
                mm.then_inc(a["PTp"], 1)

            def values_a(p, k):
                b = 2 * p + k
                pe.wait_ge(a["PT"], b + 1)
                pe.wait_ge(a["v"], b + 1)
                at_least(pe, a["ao"], 2 * b)
                pe.matmul(ps[6][:, 0:P], pta[k][:, 0:P], va[k][:, 0, :], start=True, stop=True)
                pe.matmul(ps[6][:, P:2 * P], pta[k][:, P:2 * P], va[k][:, 0, :], start=True, stop=False)
                pe.matmul(ps[6][:, P:2 * P], pta[k][:, 2 * P:3 * P], va[k][:, 1, :], start=False, stop=True)\
                    .then_inc(a["Op"], 1)

            def x_transpose(p, k):
                b = 2 * p + k
                pe.wait_ge(a["xh"], 2 * b + 2)
                at_least(pe, a["xlo"], b)
                for i in range(C):
                    mm = pe.transpose(ps[1][:, i * P:(i + 1) * P], xhs[k][:, i, :], ident[:, :])
                mm.then_inc(a["xp"], 1)

            def score_rows(p, k):
                pe.wait_ge(r["Sd"], 2)
                pe.wait_ge(a["ao"], 2 * B)
                for i in range(C):
                    mm = pe.transpose(ps[6][0:R, i * P:(i + 1) * P], S_dense[:, i, :], ident[:, :])
                mm.then_inc(r["Sp"], 1)

            def extra_a(p, k):
                w_piece(p, k)
                if is_unit(2 * p + k, ROWS_AT + 1):
                    score_rows(p, k)

            def project(p, k):
                b, j = 2 * p + k // 4, k % 4
                if is_unit(j, 0) and is_unit(b, 0, 1, 2):
                    pe.wait_ge(a["xlo"], b + 1 if b < 2 else B)
                if is_unit(b, 0) and j == 0:
                    pe.wait_ge(a["hT"], B)
                    pe.wait_ge(w_split, 3)
                if j == 1:
                    at_least(pe, lt["v"], 2 * b)
                else:
                    at_least(pe, lt["lo"], 4 * b + (0, None, 1, 3)[j])
                for i in range(2):
                    mm = triple(ps[7 * (j == 1)][:, i * N:(i + 1) * N], [u[:, 2 * j + i, :] for u in U_w],
                                (XT_hi[:, b, :], XT_lo[:, b, :]))
                mm.then_inc(lt["up"], 1)

            def project_v(p, k):
                b, w, par = 2 * p + k // 4, k % 4 - 2, b_par(k)
                if w < 0:
                    return
                if w == 0:
                    pe.wait_ge(lt["lo"], 4 * b + 2)
                else:
                    pe.wait_ge(lt["v"], 2 * b + 1)
                pe.wait_ge(lt[f"xt{par}"], 32 * (p + 1))
                triple(ps[7][:, :], [t[:, w * P:(w + 1) * P] for t in xt[par]],
                       [v[:, :] for v in V_w]).then_inc(lt["vp"], 1)

            def scores(p, k):
                g, b, j, par = 8 * p + k, 2 * p + k // 4, k % 4, b_par(k)
                w, half = j // 2, j % 2
                pe.wait_ge(lt["lo"], 4 * b + (2 if j == 0 else 4))
                if is_unit(g, 0):
                    pe.wait_ge(a["qkT"], 2 * B)
                if is_unit(g, 1):
                    pe.wait_ge(a["v"], B)
                at_least(pe, lt["p"], 4 * (g - 1))
                triple(ps[2 + k % 2][:, :].rearrange("p (h t) -> p h t", h=4),
                       [t[:, w * P:(w + 1) * P] for t in xt[par]],
                       [u[:, 4 * half:4 * half + 4, w * P:(w + 1) * P] for u in U[par]]).then_inc(lt["Sp"], 1)

            def p_transpose(p, k):
                g = 8 * p + k
                pe.wait_ge(lt["pn"], g + 1)
                if is_unit(g, 0):
                    pe.wait_ge(a["sm"], 2 * B)
                if is_unit(g, 1):
                    pe.wait_ge(a["PT"], B)
                at_least(pe, lt["PT"], g - 1)
                for i in range(4):
                    mm = pe.transpose(ps[4 + k % 2][:, i * P:(i + 1) * P], pr[k % 4][:, i * P:(i + 1) * P], ident[:, :])
                mm.then_inc(lt["PTp"], 1)

            def values(p, k):
                g, b, j, par = 8 * p + k, 2 * p + k // 4, k % 4, b_par(k)
                w, half = j // 2, j % 2
                pe.wait_ge(lt["PT"], g + 1)
                pe.wait_ge(lt["v"], 2 * b + w + 1)
                if is_unit(g, 0):
                    pe.wait_ge(r["rows"], 1)
                at_least(pe, lt["oT"], g)
                for q in range(2):
                    for i in range(2):
                        h = 4 * half + 2 * q + i
                        mm = pe.matmul(ps[6][i * DH:(i + 1) * DH, q * P:(q + 1) * P],
                                       V[par][:, w, h * DH:(h + 1) * DH],
                                       pt[k % 2][:, (2 * q + i) * P:(2 * q + i + 1) * P], start=True, stop=True)
                mm.then_inc(lt["Op"], 1)

            def out_light(p, k):
                if k % 2 == 0:
                    return
                g, b, w = 8 * p + k, 2 * p + k // 4, k % 4 // 2
                pe.wait_ge(lt["oT"], g + 1)
                if is_unit(g, 1):
                    pe.wait_ge(a["xlo"], B)
                    pe.wait_ge(wo_in, 32)
                at_least(pe, lt["fin"], 2 * b + w)
                if isinstance(g, int) and g + OUT_LAG >= H_AT:
                    pe.wait_ge(hv["xq"], (g + OUT_LAG - H_AT) // 4 + 1)
                for q in range(4):
                    mm = pe.matmul(ps[1][:, 0:D], oT[w][:, q, :], wo_l_sb[:, q, :], start=(q == 0), stop=(q == 3))
                mm.then_inc(lt["outp"], 1)

            def selection(p, k):
                u = 8 * p + k
                if is_unit(u, SELECTION):
                    pe.wait_ge(r["w"], 2)
                    pe.wait_ge(lt["lo"], 4 * B)
                    for n in range(2):
                        for i in range(C):
                            mm = pe.transpose(ps[0][:, (n * C + i) * R:(n * C + i + 1) * R],
                                              wsel[:, n, i * P:(i + 1) * P], ident[0:R, 0:R])
                    mm.then_inc(r["selp"], 1)
                if is_unit(u, SELECTION + 1):
                    pe.wait_ge(r["selT"], 1)
                    pe.matmul(ps[0][:, 0:B], tri[:, :], selT[:, 1, 0, 0:B], start=True, stop=True)
                    pe.matmul(ps[0][:, B:2 * B], tri[:, :], selT[:, 1, 1, 0:B], start=True, stop=False)
                    pe.matmul(ps[0][:, B:2 * B], ones[:, :], selT[:, 1, 0, 0:B], start=False, stop=True).then_inc(r["cum"], 1)

            def gather(p, k):
                if k % 4:
                    return
                b, par = 2 * p + k // 4, b_par(k)
                pe.wait_ge(hv["G"], 2 * b + 2)
                pe.wait_ge(hv[f"xt{par}"], 48 * (p + 1))
                if is_unit(b, 0, 1, 2):
                    pe.wait_ge(lt["fin"], min(2 * B, (H_AT + 4 * b - OUT_LAG) // 2))
                at_least(pe, hv["gt"], b - 1)
                for i in range(C):
                    mm = pe.matmul(ps[1][:, 0:NQ], xh[par][:, i, :], G[par][:, i, :], start=(i == 0), stop=(i == C - 1))
                mm.then_inc(hv["xqp"], 1)

            def g_transpose(p, k):
                if k % 4:
                    return
                b, par = 2 * p + k // 4, b_par(k)
                if is_unit(b, 0):
                    pe.wait_ge(lt["fin"], 2 * B)
                at_least(pe, hv["fin"], 2 * (b - 1))
                for i in range(C):
                    mm = pe.transpose(ps[1][:, P + i * P:P + (i + 1) * P], G[par][:, i, :], ident[:, :])
                mm.then_inc(hv["gtp"], 1)

            def project_h(p, k):
                g, b, j, par = 8 * p + k, 2 * p + k // 4, k % 4, b_par(k)
                pe.wait_ge(hv["xq"], b + 1)
                if is_unit(g, 0):
                    pe.wait_ge(r["pp"], 1)
                at_least(pe, hv["tlo"], g)
                for i in range(2):
                    mm = pe.matmul(ps[0][:, i * NQ:(i + 1) * NQ], T_w[:, 2 * j + i, :], xq[par][:, :],
                                   start=True, stop=True)
                mm.then_inc(hv["tp"], 1)

            def project_vh(p, k):
                b, w, par = 2 * p + k // 4, k % 4 // 2, b_par(k)
                if k % 2 == 0:
                    return
                if is_unit(b, 0) and w == 0:
                    pe.wait_ge(lt["v"], 2 * B)
                at_least(pe, hv["v"], 2 * b + w)
                triple(ps[7][:, :], [t[:, w * P:(w + 1) * P] for t in xt[par]],
                       [v[:, :] for v in VH_w]).then_inc(hv["vp"], 1)

            def scores_h(p, k):
                g, b, j, par = 8 * p + k, 2 * p + k // 4, k % 4, b_par(k)
                pe.wait_ge(hv["tlo"], g + 1)
                if is_unit(g, 0):
                    pe.wait_ge(lt["p"], 32 * PAIRS)
                at_least(pe, hv["p"], 2 * (g - 1))
                for i in range(2):
                    mm = triple(ps[2 + k % 2][:, i * N:(i + 1) * N], [u[:, 2 * j + i, 0:NQ] for u in U[par]],
                                (XT_hi[:, b, :], XT_lo[:, b, :]))
                mm.then_inc(hv["Sp"], 1)

            def p_transpose_h(p, k):
                g = 8 * p + k
                pe.wait_ge(hv["pn"], g + 1)
                if is_unit(g, 0):
                    pe.wait_ge(lt["PT"], 8 * PAIRS)
                at_least(pe, hv["PT"], g - 1)
                for i in range(4):
                    mm = pe.transpose(ps[4 + k % 2][:, i * P:(i + 1) * P], pr[k % 4][:, i * P:(i + 1) * P], ident[:, :])
                mm.then_inc(hv["PTp"], 1)

            def values_h(p, k):
                g, b, j, par = 8 * p + k, 2 * p + k // 4, k % 4, b_par(k)
                pe.wait_ge(hv["PT"], g + 1)
                pe.wait_ge(hv["v"], 2 * b + 2)
                if is_unit(g, 0):
                    pe.wait_ge(lt["oT"], 8 * PAIRS)
                at_least(pe, hv["oT"], g)
                for w in range(C):
                    for i in range(2):
                        h = 2 * j + i
                        mm = pe.matmul(ps[6][i * DH:(i + 1) * DH, 0:NQ], V[par][:, w, h * DH:(h + 1) * DH],
                                       pt[k % 2][:, (2 * i + w) * P:(2 * i + w + 1) * P],
                                       start=(w == 0), stop=(w == C - 1))
                mm.then_inc(hv["Op"], 1)

            def out_heavy(p, k):
                if k % 4 != 3:
                    return
                g, b, par = 8 * p + k, 2 * p + k // 4, b_par(k)
                pe.wait_ge(hv["oT"], g + 1)
                pe.wait_ge(hv["xq"], min(b + 4, B) if isinstance(b, int) else b + 4)
                if isinstance(b, int) and b + 4 > B:
                    pe.wait_ge(hv["gt"], min(b + 2, B))
                    pe.wait_ge(hv["fin"], 2 * b)
                for q in range(4):
                    mm = pe.matmul(ps[1][:, 0:D], oT[par][:, q, :], wo_h_sb[:, q, :], start=(q == 0), stop=(q == 3))
                mm.then_inc(hv["outp"], 1)

            def scatter(p, k):
                if k % 4 != 3:
                    return
                b, par = 2 * p + k // 4, b_par(k)
                pe.wait_ge(hv["rt"], b + 1)
                for i in range(C):
                    mm = pe.matmul(ps[1][:, P + i * P:P + (i + 1) * P], GT[par][:, i, :], rt[par][:, :],
                                   start=True, stop=True)
                mm.then_inc(hv["scp"], 1)

            run_phases(pe, ([(0, h_transpose), (2, value_a), (3, values_a), (1, scores_a), (0, query_key),
                             (2, p_transpose_a), (6, x_transpose)], extra_a),
                       ([(3, scores), (0, project), (OUT_LAG, out_light), (5, p_transpose), (0, project_v), (6, values)],
                        selection),
                       ([(6, values_h), (0, gather), (0, project_vh), (7, g_transpose), (4, p_transpose_h),
                         (0, project_h), (9, out_heavy), (10, scatter), (1, scores_h)], None),
                       "al al al al la la la", "lh lh lh lh lh lh lh")

        @block.vector
        def _(dve):
            def mean_var(st, t, mean, ve, three, six, seven, base=0):
                (me, ce), (mo, co) = (st[..., 1], st[..., 2]), (st[..., 4], st[..., 5])
                dve.tensor_tensor(t[0], me, mo, ALU.add).then_inc(three, 1)
                dve.tensor_tensor(t[1], me, mo, ALU.subtract).then_inc(three, 1)
                dve.tensor_tensor(t[2], ce, co, ALU.add).then_inc(three, 1)
                dve.wait_ge(three, 3 * base + 3)
                dve.tensor_scalar(mean, t[0], 0.5, None, ALU.mult).then_inc(six, 1)
                dve.scalar_tensor_tensor(t[3], t[1], 0.25, t[1], ALU.mult, ALU.mult).then_inc(six, 1)
                dve.tensor_scalar(t[4], t[2], 1.0 / D, LN_EPS, ALU.mult, ALU.add).then_inc(six, 1)
                dve.wait_ge(six, 3 * base + 3)
                dve.tensor_tensor(ve, t[3], t[4], ALU.add).then_inc(seven, 1)

            def stats1(i):
                dve.wait_ge(x_in[i], 16)
                for b in range(4 * i, 4 * i + 4):
                    for q in range(C):
                        dve.bn_stats(st1[:, b, q, :], X[:, b, q, :]).then_inc(st1_done, 1)

            def mean_var1(n, lo, hi):
                dve.wait_ge(st1_done, C * hi)
                mean_var(st1[:, lo:hi, :, :].rearrange("p b c s -> p (b c) s"), [t1[:, i, C * lo:C * hi] for i in range(5)],
                         mean1[:, C * lo:C * hi], ve1[:, C * lo:C * hi], mv1_sums, mv1_parts, ve1_done, n)

            def neg_mean_rstd(n, lo, hi):
                dve.wait_ge(rs1_done, n + 1)
                dve.scalar_tensor_tensor(nm1[:, C * lo:C * hi], mean1[:, C * lo:C * hi], -1.0, rs1[:, C * lo:C * hi],
                                         ALU.mult, ALU.mult).then_inc(nm1_done, 1)

            dve.wait_ge(c_exp, 1)
            dve.tensor_scalar(c_d[:, :], c_e[:, :], 1.0, None, ALU.add).then_inc(c_den, 1)
            dve.wait_ge(c_den, 1)
            dve.reciprocal(c_r[:, :], c_d[:, :]).then_inc(c_den, 1)
            dve.wait_ge(c_den, 2)
            dve.wait_ge(c_in, 16)
            dve.tensor_tensor(c_s[:, :], c_sb[:, :], c_r[:, :], ALU.mult).then_inc(c_act, 1)
            stats1(0)
            dve.wait_ge(cT_ps, 1)
            dve.tensor_copy(cT[:, :], ps[4][:, 0:B]).then_inc(cT_sb, 1)
            mean_var1(0, 0, 4)
            stats1(1)
            neg_mean_rstd(0, 0, 4)
            dve.wait_ge(col_ps, 1)
            dve.tensor_copy(modT[:, 0, :], ps[7][:, 0:B]).then_inc(col_sb, 1)
            dve.tensor_scalar(modT[:, 1, :], ps[7][:, B:2 * B], 1.0, None, ALU.add).then_inc(col_sb, 1)
            dve.wait_ge(row_ps, 1)
            dve.tensor_copy(mod_raw[:, :, :], ps[5][0:B, :].rearrange("b (j d) -> b j d", j=4)).then_inc(row_sb, 1)
            dve.wait_ge(row_sb, 1)
            gates = mod_raw[:, 0:4:3, :]
            dve.tensor_scalar(gate_s[:, :, :], gates, 0.0, 2.0, ALU.is_ge, ALU.mult).then_inc(gate_done, 1)
            dve.scalar_tensor_tensor(gate_a[:, :, :], gates, -1.0, gates, ALU.mult, ALU.max).then_inc(gate_done, 1)
            dve.tensor_copy(mod_fix[:, 2, :], mod_raw[:, 1, :]).then_inc(fix_done, 1)
            dve.tensor_scalar(mod_fix[:, 1, :], mod_raw[:, 2, :], 1.0, None, ALU.add).then_inc(fix_done, 1)
            dve.wait_ge(gate_done, 2)
            dve.tensor_scalar(gate_m[:, :, :], gate_a[:, :, :], 0.25, None, ALU.max).then_inc(gate_done, 1)
            dve.wait_ge(gate_done, 3)
            dve.scalar_tensor_tensor(mod_fix[:, 0:4:3, :], gate_s[:, :, :], -1.0, gate_m[:, :, :], ALU.add, ALU.mult)\
                .then_inc(fix_done, 1)
            stats1(2)
            dve.wait_ge(col_in, 32)
            dve.tensor_scalar(bq_sc[:, :], b_col[:, 0:1], ATTN_SCALE, None, ALU.mult).then_inc(w_small, 1)
            stats1(3)
            mean_var1(1, 4, B)
            dve.wait_ge(gam_in, 32)
            dve.tensor_scalar(gam_sc[:, :], gam_col[:, :], HEAD_SCALE, None, ALU.mult).then_inc(w_small, 1)
            dve.wait_ge(wl_in, 32)
            dve.tensor_scalar(v_big[:, 0, :], wkv_raw[:, HID:2 * HID], gam_col[:, 0:1], None, ALU.mult).then_inc(v_scaled, 1)
            dve.wait_ge(v_scaled, 1)
            dve.tensor_copy(V_w[0][:, :], v_big[:, 0, :]).then_inc(w_hi, 1)
            dve.wait_ge(w_hi, 1)
            dve.tensor_tensor(V_w[1][:, :], v_big[:, 0, :], V_w[0][:, :].bitcast(F32), ALU.subtract).then_inc(w_split, 1)
            dve.memset(cd_t[:, :], 0.0).then_inc(r["t"], 1)
            dve.memset(cd_m[:, :], 0.0).then_inc(r["m"], 1)
            dve.wait_ge(bc_in, 16 * 5)
            dve.wait_ge(g_tab, 5)

            def w_prods(p, k):
                n = 2 * p + k - 1
                if not isinstance(n, int) or not 0 <= n <= len(W_PIECES):
                    return
                if n == 4:
                    dve.wait_ge(w_prod, 2)
                    dve.tensor_copy(U_w[0][:, :, :], big[:, :, :]).then_inc(w_hi, 1)
                    dve.wait_ge(w_hi, 2)
                    dve.tensor_tensor(U_w[1][:, :, :], big[:, :, :], U_w[0][:, :, :].bitcast(F32), ALU.subtract)\
                        .then_inc(w_split, 1)
                elif n == 8:
                    dve.wait_ge(w_prod, 5)
                    dve.tensor_copy(VH_w[0][:, :], v_big[:, 1, :]).then_inc(w_hi, 1)
                    dve.wait_ge(w_hi, 3)
                    dve.tensor_tensor(VH_w[1][:, :], v_big[:, 1, :], VH_w[0][:, :].bitcast(F32), ALU.subtract)\
                        .then_inc(w_split, 1)
                elif n not in TRANSPOSED:
                    dve.wait_ge(w_ps, n + 1)
                    if n == 7:
                        dve.tensor_scalar(v_big[:, 1, :], ps[7][:, :], gam_col[:, 1:2], None, ALU.mult).then_inc(w_prod, 1)
                    else:
                        dst, j = (big, 0) if n < 4 else (T_w, 1)
                        i = int("odd" in W_PIECES[n])
                        dve.scalar_tensor_tensor(dst[:, i:HEADS:2, :], ps[7][:, :].rearrange("p (h d) -> p h d", h=4),
                                                 gam_sc[:, j:j + 1], gam_bc[:, j:j + 1, :].broadcast_to([P, 4, D]),
                                                 ALU.mult, ALU.mult).then_inc(w_prod, 1)

            def v_evac(p, k):
                b = 2 * p + k
                dve.wait_ge(a["vp"], b + 1)
                at_least(dve, a["Op"], b - 1)
                dve.tensor_tensor(va[k][:, :, :], ps[3][:, 0:N].rearrange("p (c d) -> p c d", c=C),
                                  bv_bc[:, None, :].broadcast_to([P, C, D]), ALU.add).then_inc(a["v"], 1)

            def scores_ready(p, k):
                dve.wait_ge(a["Sp"], 2 * p + k + 1)

            def stats_ready(p, k):
                dve.wait_ge(a["st"], 2 * (2 * p + k) + 2)

            def recip_a(p, k):
                b = 2 * p + k
                dve.wait_ge(a["p"], 2 * b + 2)
                dve.reciprocal(rinva[k][:, :], suma[k][:, :]).then_inc(a["ri"], 1)

            def mask_max(p, k):
                for i, (s, e) in enumerate(((0, P), (P, 3 * P))):
                    dve.tensor_tensor_reduce(sm[k][:, s:e], ps[4][:, s:e], mask[:, s:e], 1.0, -3.0e38, ALU.add, ALU.max,
                                             mxa[k][:, i:i + 1]).then_inc(a["sm"], 1)

            def neg_max_a(p, k):
                b = 2 * p + k
                dve.wait_ge(a["sm"], 2 * b + 2)
                at_least(dve, a["p"], 2 * (b - 1))
                dve.tensor_scalar(nmxa[k][:, :], mxa[k][:, :], -1.0, None, ALU.mult).then_inc(a["nmx"], 1)

            def attn_out(p, k):
                b = 2 * p + k
                dve.wait_ge(a["ri"], b + 1)
                dve.wait_ge(a["Op"], b + 1)
                if is_unit(b, 0, MOD_FIRST):
                    dve.wait_ge(mod_in[b // MOD_FIRST], 16)
                at_least(dve, a["x1"], b - 1)
                for i in range(C):
                    dve.scalar_tensor_tensor(ao[k][:, i, :], ps[6][:, i * P:(i + 1) * P], rinva[k][:, i:i + 1],
                                             mod_bc[:, b, 0, :], ALU.mult, ALU.mult).then_inc(a["ao"], 1)

            def ln2_stats(p, k):
                b = 2 * p + k
                dve.wait_ge(a["x1"], b + 1)
                for i in range(C):
                    dve.bn_stats(st2[k][:, i, :], X[:, b, i, :]).then_inc(a["st"], 1)

            def aggregate(p, k):
                for i in range(C):
                    dve.bn_aggr(mv2[k][:, i, :], st2[k][:, i, :]).then_inc(a["mv"], 1)

            def var_eps(p, k):
                b = 2 * p + k
                dve.wait_ge(a["mv"], 2 * b + 2)
                at_least(dve, a["rs"], b - 1)
                dve.tensor_scalar(ve2[k][:, :], mv2[k][:, :, 1], LN_EPS, None, ALU.add).then_inc(a["ve"], 1)

            def neg_mean_rstd2(p, k):
                b = 2 * p + k
                dve.wait_ge(a["rs"], b + 1)
                at_least(dve, a["hn"], 2 * (b - 1))
                dve.scalar_tensor_tensor(nm2[k][:, :], mv2[k][:, :, 0], -1.0, rs2[k][:, :], ALU.mult, ALU.mult)\
                    .then_inc(a["nm"], 1)

            def route(p, k):
                b = 2 * p + k
                dve.wait_ge(a["h2"], b + 1)
                for i in range(C):
                    for t in range(2):
                        dve.tensor_tensor_reduce(rprod[:, k, 2 * i + t, :], h2[k][:, i, :], tok_bc[:, t, :], 1.0, 0.0,
                                                 ALU.mult, ALU.add, s4[k][:, 2 * i + t:2 * i + t + 1])\
                            .then_inc(a["s4"], 1)

            def keep_scores(p, k):
                b = 2 * p + k
                dve.wait_ge(a["ss"], 2 * b + 2)
                at_least(dve, a["rn"], b - 1)
                dve.tensor_scalar(ssc[k][:, :], ss[k][:, :], 1e-24, None, ALU.max).then_inc(a["ssc"], 1)
                dve.wait_ge(a["s4"], 4 * b + 4)
                dve.tensor_copy(S_all[:, b, :, :], s4[k][:, :].rearrange("p (c t) -> p c t", c=C)).then_inc(a["S"], 1)

            def xhat(p, k):
                b = 2 * p + k
                dve.wait_ge(a["rn"], b + 1)
                at_least(dve, a["xp"], b - 1)
                at_least(dve, a[f"xhd{k}"], 16 * p)
                for i in range(C):
                    dve.tensor_scalar(xhs[k][:, i, :], h2[k][:, i, :], rn[k][:, i:i + 1], float(D) ** 0.5,
                                      ALU.mult, ALU.mult).then_inc(a["xh"], 1)

            def xt_lo(p, k):
                b = 2 * p + k
                dve.wait_ge(a["xhi"], b + 1)
                dve.tensor_tensor(XT_lo[:, b, :], ps[1][:, 0:N], XT_hi[:, b, :].bitcast(F32), ALU.subtract)\
                    .then_inc(a["xlo"], 1)

            def score_rows(n):
                if n == 0:
                    dve.wait_ge(a["S"], B)
                    for t in range(2):
                        dve.tensor_copy(S_dense[:, :, t * B:(t + 1) * B], S_all[:, :, :, t].rearrange("p b c -> p c b"))\
                            .then_inc(r["Sd"], 1)
                else:
                    dve.wait_ge(r["Sp"], 1)
                    dve.tensor_copy(s_rows[:, :], ps[6][0:R, 0:N]).then_inc(r["rows"], 1)
                    dve.wait_ge(r["rows"], 1)
                    dve.tensor_reduce(smax[:, :], s_rows[:, :], AX.X, ALU.max).then_inc(r["smax"], 1)

            def extra_a(p, k):
                if is_unit(2 * p + k, 2):
                    neg_mean_rstd(1, 4, B)
                w_prods(p, k)
                if is_unit(2 * p + k, ROWS_AT, ROWS_AT + 1):
                    score_rows(2 * p + k - ROWS_AT)

            def cd_next(n):
                if is_unit(n, 1):
                    dve.wait_ge(r["smax"], 1)
                dve.wait_ge(r["ln"], n)
                dve.tensor_scalar(cd_na[:, :], cd_ln[:, :], cd_m[:, :], log_k[:, :], ALU.add, ALU.subtract)\
                    .then_inc(r["na"], 1)
                dve.wait_ge(r["na"], n)
                dve.tensor_tensor(cd_m[:, :], smax[:, :], cd_na[:, :], ALU.min).then_inc(r["m"], 1)
                dve.wait_ge(r["m"], n + 1)
                dve.tensor_scalar(cd_t[:, :], s_rows[:, :], cd_na[:, :], cd_m[:, :], ALU.min, ALU.subtract)\
                    .then_inc(r["t"], 1)

            def u_lo(p, k):
                b, j, par = 2 * p + k // 4, k % 4, b_par(k)
                dve.wait_ge(lt["hi"], 4 * b + j + 1)
                dve.tensor_tensor(U[par][1][:, 2 * j:2 * j + 2, :], ps[7 * (j == 1)][:, :].rearrange("p (h t) -> p h t", h=2),
                                  U[par][0][:, 2 * j:2 * j + 2, :].bitcast(F32), ALU.subtract).then_inc(lt["lo"], 1)

            def neg_max(p, k):
                g = 8 * p + k
                dve.wait_ge(lt["Sp"], g + 1)
                dve.tensor_reduce(nmx[k % 4][:, :], ps[2 + k % 2][:, :].rearrange("p (h t) -> p h t", h=4), AX.X,
                                  ALU.max, negate=True).then_inc(lt["mx"], 1)

            def recip(p, k):
                g = 8 * p + k
                dve.wait_ge(lt["p"], 4 * g + 4)
                dve.reciprocal(rinv[k % 4][:, :], sums[k % 4][:, :]).then_inc(lt["ri"], 1)

            def pt_evac(p, k):
                if isinstance(p, int) and 8 * p + k >= ACT_PT:
                    return
                g = 8 * p + k
                dve.wait_ge(lt["PTp"], g + 1)
                at_least(dve, lt["Op"], g - 1)
                dve.tensor_copy(pt[k % 2][:, :], ps[4 + k % 2][:, :]).then_inc(lt["PT"], 1)

            def finish_light(p, k):
                if k % 2 == 0:
                    return
                b, w = 2 * p + k // 4, k % 4 // 2
                dve.wait_ge(lt["outp"], 2 * b + w + 1)
                at_least(dve, lt["x"], 2 * b + w - 1)
                dve.tensor_tensor(tmp[w][:, 0, :], ps[1][:, 0:D], mod_bc[:, b, 3, :], ALU.mult).then_inc(lt["fin"], 1)

            def top_round(n):
                src = score if n == 0 else left[(n + 1) % 2]
                if n:
                    dve.wait_ge(r["left"], n)
                dve.max(top8[n % 2][:, :], src[:, :]).then_inc(r["top"], 1)
                dve.wait_ge(r["top"], n + 1)
                dve.match_replace(left[n % 2][:, :], top8[n % 2][:, :], src[:, :], -1.0).then_inc(r["left"], 1)

            def top_rounds(u):
                share = SELECTION - TOP_FIRST
                return range(-(-(u - TOP_FIRST) * ROUNDS // share), -(-(u - TOP_FIRST + 1) * ROUNDS // share))

            def top_between(p, k):
                u = 8 * p + k
                if isinstance(p, int) and u > TOP_FIRST:
                    top_round(top_rounds(u)[0])

            def cd_dve(p, k):
                u = 8 * p + k
                if not isinstance(p, int) or CD_FIRST < u < CD_FIRST + CD_ITERS:
                    cd_next(u - CD_FIRST)
                elif u == CD_FIRST + CD_ITERS:
                    dve.wait_ge(r["ln"], CD_ITERS)
                    dve.tensor_scalar(cd_na[:, :], cd_ln[:, :], cd_m[:, :], log_k[:, :], ALU.add, ALU.subtract)\
                        .then_inc(r["na"], 1)
                    dve.wait_ge(r["na"], CD_ITERS)
                    dve.tensor_scalar(cd_t[:, :], s_rows[:, :], cd_na[:, :], 0.0, ALU.subtract, ALU.min).then_inc(r["tf"], 1)
                elif TOP_FIRST <= u < SELECTION:
                    if u == TOP_FIRST:
                        dve.wait_ge(r["sc"], 1)
                    if u == TOP_FIRST + 1:
                        dve.tensor_scalar(w1m[:, :], score[:, :], -1.0, 1.0, ALU.mult, ALU.add).then_inc(r["w1"], 1)
                    for n in top_rounds(u)[1 if u > TOP_FIRST else 0:]:
                        top_round(n)
                    if u == TOP_FIRST + 1:
                        dve.wait_ge(r["w1"], 1)
                        dve.tensor_tensor(wsel[:, 0, :], score[:, :], w1m[:, :], ALU.add).then_inc(r["w"], 1)
                    if u == SELECTION - 1:
                        dve.wait_ge(r["left"], ROUNDS)
                        dve.tensor_scalar(wsel[:, 1, :], left[(ROUNDS - 1) % 2][:, :], -1.0, None, ALU.is_equal)\
                            .then_inc(r["w"], 1)
                elif u == SELECTION:
                    dve.wait_ge(r["selp"], 1)
                    dve.tensor_copy(selT[:, :, :, :].rearrange("p n c r -> p (n c r)"), ps[0][:, 0:2 * C * R])\
                        .then_inc(r["selT"], 1)
                elif u == SELECTION + 1:
                    dve.wait_ge(r["cum"], 1)
                    dve.wait_ge(r["selT"], 1)
                    dve.tensor_tensor(pos_p[:, :, :], ps[0][:, 0:C * B].rearrange("p (c b) -> p c b", c=C),
                                      selT[:, 1, :, 0:B], ALU.mult).then_inc(r["pp"], 1)
                    dve.wait_ge(r["pp"], 1)
                    dve.tensor_scalar(pos[:, :, :], pos_p[:, :, :], -1.0, None, ALU.add).then_inc(r["pos"], 1)

            def one_hot(p, k):
                if k % 4:
                    return
                b, par = 2 * p + k // 4, b_par(k)
                if is_unit(b, 0):
                    dve.wait_ge(r["pos"], 1)
                at_least(dve, hv["gtp"], b - 1)
                for i in range(C):
                    dve.tensor_scalar(G[par][:, i, :], iota[:, :], pos[:, i, bass.ds(b, 1)], None, ALU.is_equal)\
                        .then_inc(hv["G"], 1)

            def t_lo(p, k):
                g, b, j, par = 8 * p + k, 2 * p + k // 4, k % 4, b_par(k)
                dve.wait_ge(hv["thi"], g + 1)
                dve.tensor_tensor(U[par][1][:, 2 * j:2 * j + 2, 0:NQ],
                                  ps[0][:, 0:2 * NQ].rearrange("p (h t) -> p h t", h=2),
                                  U[par][0][:, 2 * j:2 * j + 2, 0:NQ].bitcast(F32), ALU.subtract).then_inc(hv["tlo"], 1)

            def v_evac_h(p, k):
                b, w, par = 2 * p + k // 4, k % 4 // 2, b_par(k)
                if k % 2 == 0:
                    return
                dve.wait_ge(hv["vp"], 2 * b + w + 1)
                if is_unit(b, 0, 1):
                    dve.wait_ge(lt["Op"], 4 * (B - 1 + b))
                at_least(dve, hv["Op"], 4 * (b - 1))
                dve.tensor_scalar(V[par][:, w, :], ps[7][:, :], selT[:, 0, w, bass.ds(B + b, 1)], None, ALU.mult)\
                    .then_inc(hv["v"], 1)

            def neg_max_h(p, k):
                g = 8 * p + k
                dve.wait_ge(hv["Sp"], g + 1)
                dve.tensor_reduce(nmx[k % 4][:, 0:2], ps[2 + k % 2][:, :].rearrange("p (h t) -> p h t", h=2), AX.X,
                                  ALU.max, negate=True).then_inc(hv["mx"], 1)

            def recip_h(p, k):
                g = 8 * p + k
                dve.wait_ge(hv["p"], 2 * g + 2)
                dve.reciprocal(rinv[k % 4][:, 0:2], sums[k % 4][:, 0:2]).then_inc(hv["ri"], 1)

            def o_evac_h(p, k):
                g, b, j, par = 8 * p + k, 2 * p + k // 4, k % 4, b_par(k)
                dve.wait_ge(hv["Op"], g + 1)
                if is_unit(g, 0):
                    dve.wait_ge(lt["outp"], 2 * B)
                at_least(dve, hv["outp"], b - 1)
                dve.tensor_copy(oT[par][:, j, :], ps[6][:, 0:NQ]).then_inc(hv["oT"], 1)

            def finish_heavy(p, k):
                if k % 4 != 3:
                    return
                b, par = 2 * p + k // 4, b_par(k)
                dve.wait_ge(hv["scp"], b + 1)
                if is_unit(b, 0):
                    dve.wait_ge(lt["x"], 2 * B)
                at_least(dve, hv["ob"], b - 1)
                for i in range(C):
                    dve.scalar_tensor_tensor(tmp[par][:, i, :], ps[1][:, P + i * P:P + (i + 1) * P],
                                             selT[:, 0, i, bass.ds(b, 1)], mod_bc[:, b, 3, :], ALU.mult, ALU.mult)\
                        .then_inc(hv["fin"], 1)

            run_phases(dve, ([(2, scores_ready), (4, stats_ready), (3, recip_a), (2, mask_max), (4, aggregate), (4, var_eps),
                              (2, neg_max_a), (5, route), (3, attn_out), (4, neg_mean_rstd2), (5, keep_scores), (6, xhat),
                              (7, xt_lo), (2, v_evac), (3, ln2_stats)], extra_a),
                       ([(5, recip), (9, finish_light), (1, u_lo), (0, top_between), (6, pt_evac), (3, neg_max)], cd_dve),
                       ([(7, o_evac_h), (12, finish_heavy), (1, v_evac_h), (0, one_hot), (1, t_lo), (2, neg_max_h),
                         (3, recip_h)], None),
                       "al al al al la la la", "lh lh lh lh lh lh lh")


_INS = ["L0_attn_x", "L0_attn_W", "L0_attn_b", "L0_ffn_gamma_light", "L0_ffn_wq_light", "L0_ffn_wkv_light",
        "L0_ffn_wo_light", "L0_ffn_q_routing_token", "L0_ffn_kv_routing_token", "L0_ffn_gamma_heavy",
        "L0_ffn_wq_heavy", "L0_ffn_wkv_heavy", "L0_ffn_wo_heavy", "L0_c", "L0_wmod"]


def kernel(**inputs):
    import numpy as _np
    import concourse.bacc as _bacc
    from concourse import mybir as _mybir
    from concourse.bass_utils import run_bass_kernel_spmd as _run

    nc = _bacc.Bacc("TRN2", target_bir_lowering=False, num_devices=1)
    arrays, args = {}, []
    for name in _INS:
        arr = _np.ascontiguousarray(inputs[name])
        arrays[f"in_{name}"] = arr
        args.append(nc.dram_tensor(f"in_{name}", arr.shape, _mybir.dt.from_np(arr.dtype), kind="ExternalInput").ap())
    out = nc.dram_tensor("out", (B, N, D), F32, kind="ExternalOutput").ap()
    adaln_routed_attention(nc, *args, out)
    r = _run(nc, [arrays], core_ids=[0])
    return r.results[0]["out"]
```
